# Optimizing a Trainium2 kernel written in Bass

```python
import numpy as np
import jax
import jax.numpy as jnp

def _softmax(x, axis=-1):
    return jax.nn.softmax(x, axis=axis)

def _gelu(x):
    return jax.nn.gelu(x, approximate=True)

def _silu(x):
    return jax.nn.silu(x)

def _sigmoid(x):
    return jax.nn.sigmoid(x)

def _layernorm(x, axis=-1, eps=1e-05):
    m = jnp.mean(x, axis=axis, keepdims=True)
    v = jnp.var(x, axis=axis, keepdims=True)
    return (x - m) / jnp.sqrt(v + eps)

def _scatter_add(tgt, idx, src, axis=0):
    return tgt.at[idx].add(src)

def _segment_sum(src, seg, n):
    return jax.ops.segment_sum(src, seg, n)
kernel_name = 'mk_gnn_resnorm_d4_gnn_r64_f253d2'

def setup_inputs(seed: int=0):
    np.random.seed(seed)
    _w = jnp.asarray

    def _rec_inputs():
        import jax
        import jax.numpy as jnp
        _gk = jax.random.key(seed)
        x = -0.0005121 + 1.001 * jax.random.normal(jax.random.fold_in(_gk, 1), (100000, 32), jnp.float32)
        src = jax.random.randint(jax.random.fold_in(_gk, 2), (25000,), 0, 100000, jnp.int32)
        dst = jax.random.randint(jax.random.fold_in(_gk, 3), (25000,), 0, 100000, jnp.int32)
        _o = jnp.argsort(dst, stable=True)
        src = src[_o]
        dst = dst[_o]
        edge_attr_3 = 0.000844983 + 0.999762 * jax.random.normal(jax.random.fold_in(_gk, 12), (25000, 3), jnp.float32)
        edge_weight = jax.random.uniform(jax.random.fold_in(_gk, 14), (25000,), jnp.float32, 0.0, 1)
        return (x, src, dst, edge_attr_3, edge_weight)
    x, src, dst, edge_attr_3, edge_weight = _rec_inputs()

    def _L0_gnn_setup():
        import jax, jax.numpy as jnp
        import numpy as np
        ALPHA = 0.1
        K = 10
        key = jax.random.key(seed)
        k1, k2, k3 = jax.random.split(key, 3)
        N, E, D = (100000, 25000, 32)
        feat = jax.random.normal(k1, (N, D), dtype=jnp.float32)
        src = jax.random.randint(k2, (E,), 0, N)
        dst = jax.random.randint(k3, (E,), 0, N)
        return {'feat': feat, 'src': src, 'dst': dst}
    _L0_gnn_all = _L0_gnn_setup()
    _L0_gnn_in = {k: v for k, v in _L0_gnn_all.items() if k in ()}
    del _L0_gnn_all

    def _L1_gnn_setup():
        import jax, jax.numpy as jnp
        import numpy as np
        N_NODES = 100000
        N_EDGES = 25000
        DIM1 = 32
        LEAKY_SLOPE = 0.01
        key = jax.random.key(seed)
        k1, k2, k3, k4 = jax.random.split(key, 4)
        h = jax.random.normal(k1, (N_NODES, DIM1), dtype=jnp.float32)
        attn_w = jax.random.normal(k2, (2 * DIM1,), dtype=jnp.float32) * (1.0 / np.sqrt(2 * DIM1))
        src = jax.random.randint(k3, (N_EDGES,), 0, N_NODES, dtype=jnp.int32)
        dst = jax.random.randint(k4, (N_EDGES,), 0, N_NODES, dtype=jnp.int32)
        return {'h': h, 'attn_w': attn_w, 'src': src, 'dst': dst}
    _L1_gnn_all = _L1_gnn_setup()
    _L1_gnn_in = {k: v for k, v in _L1_gnn_all.items() if k in ('attn_w',)}
    del _L1_gnn_all

    def _L2_gnn_setup():
        import jax, jax.numpy as jnp
        import numpy as np
        from math import factorial, pi, sqrt
        MUL = 8
        RS = [(MUL, 0), (MUL, 1)]
        N_NODES = 20000
        N_EDGES = 10000
        FEAT_DIM = sum((m * (2 * l + 1) for m, l in RS))
        R_DIM = sum((mo * mi * (2 * min(lo, li) + 1) for mo, lo in RS for mi, li in RS))
        HIDDEN = 64

        def _cg(j1, j2, j3, m1, m2, m3):
            if m1 + m2 != m3:
                return 0.0
            f = factorial
            pre = sqrt((2 * j3 + 1) * f(j3 + j1 - j2) * f(j3 - j1 + j2) * f(j1 + j2 - j3) / f(j1 + j2 + j3 + 1))
            pre *= sqrt(f(j3 + m3) * f(j3 - m3) * f(j1 - m1) * f(j1 + m1) * f(j2 - m2) * f(j2 + m2))
            kmin = max(0, j2 - j3 - m1, j1 - j3 + m2)
            kmax = min(j1 + j2 - j3, j1 - m1, j2 + m2)
            s = 0.0
            for k in range(kmin, kmax + 1):
                s += (-1) ** k / (f(k) * f(j1 + j2 - j3 - k) * f(j1 - m1 - k) * f(j2 + m2 - k) * f(j3 - j2 + m1 + k) * f(j3 - j1 - m2 + k))
            return pre * s

        def _w3j_complex(l1, l2, l3):
            w = np.zeros((2 * l1 + 1, 2 * l2 + 1, 2 * l3 + 1))
            for m1 in range(-l1, l1 + 1):
                for m2 in range(-l2, l2 + 1):
                    m3 = -(m1 + m2)
                    if abs(m3) <= l3:
                        w[m1 + l1, m2 + l2, m3 + l3] = (-1) ** (l1 - l2 - m3) / sqrt(2 * l3 + 1) * _cg(l1, l2, l3, m1, m2, -m3)
            return w

        def _A(l):
            A = np.zeros((2 * l + 1, 2 * l + 1), dtype=complex)
            A[l, l] = 1.0
            for m in range(1, l + 1):
                A[l + m, l + m] = (-1) ** m / sqrt(2)
                A[l + m, l - m] = 1.0 / sqrt(2)
                A[l - m, l - m] = 1j / sqrt(2)
                A[l - m, l + m] = -1j * (-1) ** m / sqrt(2)
            return A

        def real_w3j(l1, l2, l3):
            wc = _w3j_complex(l1, l2, l3).astype(complex)
            wr = np.einsum('abc,ma,nb,oc->mno', wc, _A(l1).conj(), _A(l2).conj(), _A(l3).conj())
            i = int(np.argmax(np.abs(wr)))
            ph = wr.flat[i] / abs(wr.flat[i])
            wr = wr / ph
            assert np.abs(wr.imag).max() < 1e-10
            return np.real(wr).astype(np.float32)
        _W3J = {}
        for _mo, _lo in RS:
            for _mi, _li in RS:
                for _lf in range(abs(_lo - _li), _lo + _li + 1):
                    if (_lo, _lf, _li) not in _W3J:
                        _W3J[_lo, _lf, _li] = jnp.asarray(real_w3j(_lo, _lf, _li))
        _NORM = []
        for _mo, _lo in RS:
            _num = sum((mi * (2 * min(_lo, li) + 1) for mi, li in RS))
            _NORM.append(sqrt(4.0 * pi) * sqrt(2.0 * _lo + 1.0) / sqrt(_num))
        _F_OFFS = [0] + list(np.cumsum([mi * (2 * li + 1) for mi, li in RS]))

        def spherical_harmonics(rel_vec):
            r = rel_vec / jnp.linalg.norm(rel_vec, axis=-1, keepdims=True)
            x, y, z = (r[:, 0], r[:, 1], r[:, 2])
            y0 = jnp.full_like(x, 0.5 / sqrt(pi))[:, None]
            c1 = sqrt(3.0 / (4.0 * pi))
            y1 = c1 * jnp.stack([y, z, x], axis=-1)
            c2a = 0.5 * sqrt(15.0 / pi)
            c2b = 0.25 * sqrt(5.0 / pi)
            c2c = 0.25 * sqrt(15.0 / pi)
            y2 = jnp.stack([c2a * x * y, c2a * y * z, c2b * (3.0 * z * z - 1.0), c2a * x * z, c2c * (x * x - y * y)], axis=-1)
            return jnp.concatenate([y0, y1, y2], axis=-1)
        key = jax.random.key(seed)
        ks = jax.random.split(key, 6)
        features = jax.random.normal(ks[0], (N_NODES, FEAT_DIM), dtype=jnp.float32)
        abs_distances = jax.random.uniform(ks[1], (N_EDGES,), dtype=jnp.float32, minval=0.1, maxval=1.0)
        rel_vec = jax.random.normal(ks[2], (N_EDGES, 3), dtype=jnp.float32)
        edge_index = jax.random.randint(ks[3], (2, N_EDGES), 0, N_NODES, dtype=jnp.int32)
        w1 = jax.random.normal(ks[4], (1, HIDDEN), dtype=jnp.float32)
        b1 = jnp.zeros((HIDDEN,), jnp.float32)
        w2 = jax.random.normal(ks[5], (HIDDEN, R_DIM), dtype=jnp.float32) / sqrt(HIDDEN)
        b2 = jnp.zeros((R_DIM,), jnp.float32)
        return {'features': features, 'abs_distances': abs_distances, 'rel_vec': rel_vec, 'edge_index': edge_index, 'w1': w1, 'b1': b1, 'w2': w2, 'b2': b2}
    _L2_gnn_all = _L2_gnn_setup()
    _L2_gnn_in = {k: v for k, v in _L2_gnn_all.items() if k in ('w1', 'b1', 'w2', 'b2')}
    del _L2_gnn_all

    def _L3_gnn_setup():
        import jax, jax.numpy as jnp
        import numpy as np
        N = 100000
        E = 25000
        IN, HID, OUT = (32, 64, 32)

        def gcn_conv(x, src, dst, W, b, n):
            h = x @ W
            ones = jnp.ones_like(dst, dtype=h.dtype)
            deg = jax.ops.segment_sum(ones, dst, num_segments=n)
            dinv = jax.lax.rsqrt(jnp.maximum(deg, 1.0))
            norm = dinv[src] * dinv[dst]
            agg = jax.ops.segment_sum(norm[:, None] * h[src], dst, num_segments=n)
            return agg + b
        key = jax.random.key(seed)
        k0, k1, k2, k3 = jax.random.split(key, 4)
        x = jax.random.normal(k0, (N, IN), dtype=jnp.float32)
        edge_index = jax.random.randint(k1, (2, E), 0, N, dtype=jnp.int32)
        W1 = jax.random.normal(k2, (IN, HID), dtype=jnp.float32) * (1.0 / np.sqrt(IN))
        b1 = jnp.zeros((HID,), dtype=jnp.float32)
        W2 = jax.random.normal(k3, (HID, OUT), dtype=jnp.float32) * (1.0 / np.sqrt(HID))
        b2 = jnp.zeros((OUT,), dtype=jnp.float32)
        return {'x': x, 'edge_index': edge_index, 'W1': W1, 'b1': b1, 'W2': W2, 'b2': b2}
    _L3_gnn_all = _L3_gnn_setup()
    _L3_gnn_in = {k: v for k, v in _L3_gnn_all.items() if k in ('W1', 'b1', 'W2', 'b2')}
    del _L3_gnn_all
    return {'x': x, 'src': src, 'dst': dst, 'edge_attr_3': edge_attr_3, 'edge_weight': edge_weight, 'L1_gnn_attn_w': _L1_gnn_in['attn_w'], 'L2_gnn_w1': _L2_gnn_in['w1'], 'L2_gnn_b1': _L2_gnn_in['b1'], 'L2_gnn_w2': _L2_gnn_in['w2'], 'L2_gnn_b2': _L2_gnn_in['b2'], 'L3_gnn_W1': _L3_gnn_in['W1'], 'L3_gnn_b1': _L3_gnn_in['b1'], 'L3_gnn_W2': _L3_gnn_in['W2'], 'L3_gnn_b2': _L3_gnn_in['b2']}

def reference(x, src, dst, edge_attr_3, edge_weight, L1_gnn_attn_w, L2_gnn_w1, L2_gnn_b1, L2_gnn_w2, L2_gnn_b2, L3_gnn_W1, L3_gnn_b1, L3_gnn_W2, L3_gnn_b2):
    import jax
    import jax.numpy as jnp

    def _L0_gnn_ref(feat, src, dst):
        import jax, jax.numpy as jnp
        import numpy as np
        ALPHA = 0.1
        K = 10
        N = feat.shape[0]
        deg = jax.ops.segment_sum(jnp.ones_like(dst, dtype=feat.dtype), dst, num_segments=N)
        norm = jnp.where(deg > 0, deg ** (-0.5), 0.0)[:, None]
        feat_0 = feat

        def step(h, _):
            h = h * norm
            h = jax.ops.segment_sum(h[src], dst, num_segments=N)
            h = h * norm
            h = (1.0 - ALPHA) * h + ALPHA * feat_0
            return (h, None)
        h, _ = jax.lax.scan(step, feat, None, length=K)
        return h

    def _L1_gnn_ref(h, attn_w, src, dst):
        import jax, jax.numpy as jnp
        import numpy as np
        N_NODES = 100000
        N_EDGES = 25000
        DIM1 = 32
        LEAKY_SLOPE = 0.01
        N, d = h.shape
        s_src = h @ attn_w[:d]
        s_dst = h @ attn_w[d:]
        e = s_src[src] + s_dst[dst]
        e = jnp.where(e >= 0, e, LEAKY_SLOPE * e)
        m = jax.ops.segment_max(e, dst, num_segments=N)
        ex = jnp.exp(e - m[dst])
        denom = jax.ops.segment_sum(ex, dst, num_segments=N)
        alpha = ex / denom[dst]
        out = jax.ops.segment_sum(h[src] * alpha[:, None], dst, num_segments=N)
        return out

    def _L2_gnn_ref(features, abs_distances, rel_vec, edge_index, w1, b1, w2, b2):
        import jax, jax.numpy as jnp
        import numpy as np
        from math import factorial, pi, sqrt
        MUL = 8
        RS = [(MUL, 0), (MUL, 1)]
        N_NODES = 20000
        N_EDGES = 10000
        FEAT_DIM = sum((m * (2 * l + 1) for m, l in RS))
        R_DIM = sum((mo * mi * (2 * min(lo, li) + 1) for mo, lo in RS for mi, li in RS))
        HIDDEN = 64

        def _cg(j1, j2, j3, m1, m2, m3):
            if m1 + m2 != m3:
                return 0.0
            f = factorial
            pre = sqrt((2 * j3 + 1) * f(j3 + j1 - j2) * f(j3 - j1 + j2) * f(j1 + j2 - j3) / f(j1 + j2 + j3 + 1))
            pre *= sqrt(f(j3 + m3) * f(j3 - m3) * f(j1 - m1) * f(j1 + m1) * f(j2 - m2) * f(j2 + m2))
            kmin = max(0, j2 - j3 - m1, j1 - j3 + m2)
            kmax = min(j1 + j2 - j3, j1 - m1, j2 + m2)
            s = 0.0
            for k in range(kmin, kmax + 1):
                s += (-1) ** k / (f(k) * f(j1 + j2 - j3 - k) * f(j1 - m1 - k) * f(j2 + m2 - k) * f(j3 - j2 + m1 + k) * f(j3 - j1 - m2 + k))
            return pre * s

        def _w3j_complex(l1, l2, l3):
            w = np.zeros((2 * l1 + 1, 2 * l2 + 1, 2 * l3 + 1))
            for m1 in range(-l1, l1 + 1):
                for m2 in range(-l2, l2 + 1):
                    m3 = -(m1 + m2)
                    if abs(m3) <= l3:
                        w[m1 + l1, m2 + l2, m3 + l3] = (-1) ** (l1 - l2 - m3) / sqrt(2 * l3 + 1) * _cg(l1, l2, l3, m1, m2, -m3)
            return w

        def _A(l):
            A = np.zeros((2 * l + 1, 2 * l + 1), dtype=complex)
            A[l, l] = 1.0
            for m in range(1, l + 1):
                A[l + m, l + m] = (-1) ** m / sqrt(2)
                A[l + m, l - m] = 1.0 / sqrt(2)
                A[l - m, l - m] = 1j / sqrt(2)
                A[l - m, l + m] = -1j * (-1) ** m / sqrt(2)
            return A

        def real_w3j(l1, l2, l3):
            wc = _w3j_complex(l1, l2, l3).astype(complex)
            wr = np.einsum('abc,ma,nb,oc->mno', wc, _A(l1).conj(), _A(l2).conj(), _A(l3).conj())
            i = int(np.argmax(np.abs(wr)))
            ph = wr.flat[i] / abs(wr.flat[i])
            wr = wr / ph
            assert np.abs(wr.imag).max() < 1e-10
            return np.real(wr).astype(np.float32)
        _W3J = {}
        for _mo, _lo in RS:
            for _mi, _li in RS:
                for _lf in range(abs(_lo - _li), _lo + _li + 1):
                    if (_lo, _lf, _li) not in _W3J:
                        _W3J[_lo, _lf, _li] = jnp.asarray(real_w3j(_lo, _lf, _li))
        _NORM = []
        for _mo, _lo in RS:
            _num = sum((mi * (2 * min(_lo, li) + 1) for mi, li in RS))
            _NORM.append(sqrt(4.0 * pi) * sqrt(2.0 * _lo + 1.0) / sqrt(_num))
        _F_OFFS = [0] + list(np.cumsum([mi * (2 * li + 1) for mi, li in RS]))

        def spherical_harmonics(rel_vec):
            r = rel_vec / jnp.linalg.norm(rel_vec, axis=-1, keepdims=True)
            x, y, z = (r[:, 0], r[:, 1], r[:, 2])
            y0 = jnp.full_like(x, 0.5 / sqrt(pi))[:, None]
            c1 = sqrt(3.0 / (4.0 * pi))
            y1 = c1 * jnp.stack([y, z, x], axis=-1)
            c2a = 0.5 * sqrt(15.0 / pi)
            c2b = 0.25 * sqrt(5.0 / pi)
            c2c = 0.25 * sqrt(15.0 / pi)
            y2 = jnp.stack([c2a * x * y, c2a * y * z, c2b * (3.0 * z * z - 1.0), c2a * x * z, c2c * (x * x - y * y)], axis=-1)
            return jnp.concatenate([y0, y1, y2], axis=-1)
        src, dst = (edge_index[0], edge_index[1])
        R = jax.nn.relu(abs_distances[:, None] @ w1 + b1) @ w2 + b2
        Y = spherical_harmonics(rel_vec)
        Fj = features[src]
        E = Fj.shape[0]
        msg_blocks = []
        r_off = 0
        for i, (mo, lo) in enumerate(RS):
            acc = jnp.zeros((E, mo, 2 * lo + 1), dtype=features.dtype)
            for j, (mi, li) in enumerate(RS):
                n_lf = 2 * min(lo, li) + 1
                sz = mo * mi * n_lf
                Rb = R[:, r_off:r_off + sz].reshape(E, mo, mi, n_lf)
                r_off += sz
                Fb = Fj[:, _F_OFFS[j]:_F_OFFS[j + 1]].reshape(E, mi, 2 * li + 1)
                for k, lf in enumerate(range(abs(lo - li), lo + li + 1)):
                    C = _W3J[lo, lf, li]
                    Yf = Y[:, lf * lf:(lf + 1) * (lf + 1)]
                    acc = acc + _NORM[i] * jnp.einsum('euv,ef,evi,ofi->euo', Rb[..., k], Yf, Fb, C)
            msg_blocks.append(acc.reshape(E, -1))
        msg = jnp.concatenate(msg_blocks, axis=-1)
        out = jnp.zeros((features.shape[0], msg.shape[1]), dtype=features.dtype)
        out = out.at[dst].add(msg)
        return out

    def _L3_gnn_ref(x, edge_index, W1, b1, W2, b2):
        import jax, jax.numpy as jnp
        import numpy as np
        N = 100000
        E = 25000
        IN, HID, OUT = (32, 64, 32)

        def gcn_conv(x, src, dst, W, b, n):
            h = x @ W
            ones = jnp.ones_like(dst, dtype=h.dtype)
            deg = jax.ops.segment_sum(ones, dst, num_segments=n)
            dinv = jax.lax.rsqrt(jnp.maximum(deg, 1.0))
            norm = dinv[src] * dinv[dst]
            agg = jax.ops.segment_sum(norm[:, None] * h[src], dst, num_segments=n)
            return agg + b
        n = x.shape[0]
        loop = jnp.arange(n, dtype=edge_index.dtype)
        src = jnp.concatenate([edge_index[0], loop])
        dst = jnp.concatenate([edge_index[1], loop])
        h = jax.nn.relu(gcn_conv(x, src, dst, W1, b1, n))
        out = gcn_conv(h, src, dst, W2, b2, n)
        return out
    edge_index = jnp.stack([src, dst])
    x = _layernorm(x + _L0_gnn_ref(x, src, dst), axis=-1)
    x = _layernorm(x + _L1_gnn_ref(x, L1_gnn_attn_w, src, dst), axis=-1)
    x = _layernorm(x + _L2_gnn_ref(x, edge_weight, edge_attr_3, edge_index, L2_gnn_w1, L2_gnn_b1, L2_gnn_w2, L2_gnn_b2), axis=-1)
    x = _layernorm(x + _L3_gnn_ref(x, edge_index, L3_gnn_W1, L3_gnn_b1, L3_gnn_W2, L3_gnn_b2), axis=-1)
    return x

_drawn_inputs = setup_inputs


def setup_inputs(seed=0):
    import zlib

    import numpy as np

    out = dict(_drawn_inputs(seed))
    spreads = {'L2_gnn_b1': (0.0, 0.337),
     'L2_gnn_b2': (0.0, 0.1),
     'L3_gnn_b1': (0.0, 0.1),
     'L3_gnn_b2': (0.0, 0.1)}
    factors = {}
    for name, (base, spread) in spreads.items():
        noise = np.random.default_rng([zlib.crc32(name.encode()), seed]).standard_normal(out[name].shape)
        drawn = base * np.exp(spread * noise) if base else spread * noise
        out[name] = jnp.asarray(drawn.astype(out[name].dtype))
    for name, factor in factors.items():
        out[name] = (out[name] * factor).astype(out[name].dtype)
    return out
```

```python
from contextlib import ExitStack
from math import factorial, pi, sqrt

import numpy as np

import concourse.bass as bass
from concourse import mybir

F32 = mybir.dt.float32
BF16 = mybir.dt.bfloat16
I32 = mybir.dt.int32
U32 = mybir.dt.uint32
ALU = mybir.AluOpType
ACT = mybir.ActivationFunctionType
AX = mybir.AxisListType

P = 128
D = 32
HID = 64
U = 14
EPS = 1e-5
BIG = 1e30
APPNP_STEPS = 10
RW = D + 2
ROWS = 512
NQ = P // D
C7 = 7
MULT = 8


def sizes(n_nodes, n_edges):
    t = -(-n_edges // (P * 2 * U)) * 2 * U
    pair = 2 * ROWS * NQ
    return t, P * t, -(-n_nodes // pair) * pair


def _cg(j1, j2, j3, m1, m2, m3):
    if m1 + m2 != m3:
        return 0.0
    f = factorial
    pre = sqrt((2 * j3 + 1) * f(j3 + j1 - j2) * f(j3 - j1 + j2) * f(j1 + j2 - j3) / f(j1 + j2 + j3 + 1))
    pre *= sqrt(f(j3 + m3) * f(j3 - m3) * f(j1 - m1) * f(j1 + m1) * f(j2 - m2) * f(j2 + m2))
    s = 0.0
    for k in range(max(0, j2 - j3 - m1, j1 - j3 + m2), min(j1 + j2 - j3, j1 - m1, j2 + m2) + 1):
        s += (-1) ** k / (f(k) * f(j1 + j2 - j3 - k) * f(j1 - m1 - k) * f(j2 + m2 - k)
                          * f(j3 - j2 + m1 + k) * f(j3 - j1 - m2 + k))
    return pre * s


def _real_basis(l):
    a = np.zeros((2 * l + 1, 2 * l + 1), dtype=complex)
    a[l, l] = 1.0
    for m in range(1, l + 1):
        a[l + m, l + m] = (-1) ** m / sqrt(2)
        a[l + m, l - m] = 1.0 / sqrt(2)
        a[l - m, l - m] = 1j / sqrt(2)
        a[l - m, l + m] = -1j * (-1) ** m / sqrt(2)
    return a


def wigner_3j(l1, l2, l3):
    w = np.zeros((2 * l1 + 1, 2 * l2 + 1, 2 * l3 + 1), dtype=complex)
    for m1 in range(-l1, l1 + 1):
        for m2 in range(-l2, l2 + 1):
            if abs(m1 + m2) <= l3:
                w[m1 + l1, m2 + l2, l3 - m1 - m2] = ((-1) ** (l1 - l2 + m1 + m2) / sqrt(2 * l3 + 1)
                                                    * _cg(l1, l2, l3, m1, m2, m1 + m2))
    r = np.einsum("abc,ma,nb,oc->mno", w, _real_basis(l1).conj(), _real_basis(l2).conj(), _real_basis(l3).conj())
    top = r.flat[int(np.argmax(np.abs(r)))]
    return np.real(r / (top / abs(top)))


def gnn_kernel(nc, x, src, dst, dst_next, dst_first, rel, wt_cols, attn_w, w1, b1, w2, b2,
               gcn_w1, gcn_b1, gcn_w2, gcn_b2, ident, center, average, upper, out, n_edges):
    E = src.shape[0]
    T = E // P
    NR = out.shape[0] - E
    PAIRS = NR // (2 * ROWS * NQ)
    GROUPS = T // U
    NK = NR // P // 8
    R_DIM = w2.shape[1]

    norm = [sqrt(4 * pi) * sqrt(2 * lo + 1) / sqrt(sum(MULT * (2 * min(lo, li) + 1) for li in (0, 1)))
            for lo in (0, 1)]
    y0 = 0.5 / sqrt(pi)
    c1 = sqrt(3.0 / (4.0 * pi))
    c2a, c2b, c2c = 0.5 * sqrt(15.0 / pi), 0.25 * sqrt(5.0 / pi), 0.25 * sqrt(15.0 / pi)

    rec = nc.dram_tensor("node_records", (NR + E, RW), F32).ap()
    rec_pairs = rec.rearrange("n (a b) -> (n a) b", b=2)
    tables = [nc.dram_tensor(f"edge_table_{i}", (E, D), F32).ap() for i in range(5)]

    with ExitStack() as ctx:
        def sb(name, shape, dt=F32):
            return ctx.enter_context(nc.sbuf_tensor(name, shape, dt))

        def sem(name):
            return ctx.enter_context(nc.semaphore(name))

        ps = ctx.enter_context(nc.psum_tensor("ps", [P, 8, 512], F32))
        carry = ps[:, 7, :]

        xd = sb("xd", [P, T, D])
        xs = sb("xs", [P, T, D])
        bufA = sb("bufA", [P, T * D])
        bufB = sb("bufB", [P, T * D])
        bufN = sb("bufN", [P, T * D])
        bufG = sb("bufG", [P, T * RW])
        contf = sb("contf", [P, D, T], BF16)
        A_jd = bufA[:].rearrange("p (j d) -> p j d", d=D)
        A_dj = bufA[:].rearrange("p (d j) -> p d j", d=D)
        B_dj = bufB[:].rearrange("p (d j) -> p d j", d=D)
        N_jd = bufN[:].rearrange("p (j d) -> p j d", d=D)
        N_dj = bufN[:].rearrange("p (d j) -> p d j", d=D)
        G_jd = bufG[:, 0:T * D].rearrange("p (j d) -> p j d", d=D)
        G_dj = bufG[:, 0:T * D].rearrange("p (d j) -> p d j", d=D)
        G_rec = bufG[:].rearrange("p (j r) -> p j r", r=RW)

        ring_idx = sb("ring_idx", [P, 2, U], I32)
        ring_rows = sb("ring_rows", [P, 2, U * RW])

        src_i = sb("src_i", [P, T], I32)
        dst_i = sb("dst_i", [P, T], I32)
        next_i = sb("next_i", [P, T], I32)
        slot_i = sb("slot_i", [P, T], I32)
        node_i = sb("node_i", [P, T], I32)
        pair_i = sb("pair_i", [P, T], I32)
        src_slot_i = sb("src_slot_i", [P, T], I32)
        dstf = sb("dstf", [P, T])
        cont = sb("cont", [P, T])
        contn = sb("contn", [P, T])
        last = sb("last", [P, T])
        infirst = sb("infirst", [P, T])
        deg = sb("deg", [P, T])
        slotdeg = sb("slotdeg", [P, T, 2])
        act = sb("act", [P, T])
        scale_s = sb("scale_s", [P, T])
        norm_d = sb("norm_d", [P, T])
        dinv_s = sb("dinv_s", [P, T])
        dinv_d = sb("dinv_d", [P, T])
        relv = sb("relv", [P, T, 3])
        ta = sb("ta", [P, T])
        tb = sb("tb", [P, T])
        tc = sb("tc", [P, T])
        td = sb("td", [P, T])
        lnv = sb("lnv", [P, T])
        both = sb("both", [P, 2, T])
        first2 = sb("first2", [P, 2])
        init2 = sb("init2", [P, 2])
        colmax = sb("colmax", [P, 1])
        diag = sb("diag", [P, P])
        epsc = sb("epsc", [P, 1])
        zeroc = sb("zeroc", [P, 1])

        id_sb = sb("id_sb", [P, P])
        cen_sb = sb("cen_sb", [P, P])
        avg_sb = sb("avg_sb", [P, P])
        up_sb = sb("up_sb", [P, P])
        ones = sb("ones", [P, T])
        dfirst = sb("dfirst", [P, P], I32)
        link_f = sb("link_f", [P, P])
        link_b = sb("link_b", [P, P])
        nolink = sb("nolink", [P, P])
        attn_sb = sb("attn_sb", [P, 2, D])
        w1_sb = sb("w1_sb", [HID, 1])
        w2_sb = sb("w2_sb", [HID + 1, R_DIM])
        b1_sb = sb("b1_sb", [HID, 1])
        gw1_sb = sb("gw1_sb", [P, NQ * HID])
        gw2_sb = sb("gw2_sb", [P, 2, P])
        gb1_sb = sb("gb1_sb", [P, 1])
        gb2_col = sb("gb2_col", [P, 1])
        gb2_row = sb("gb2_row", [P, D])
        wrow = [bufN[0:HID, i * C7 * P:(i + 1) * C7 * P] for i in range(2)]
        hid = [bufN[0:HID + 1, (2 + i) * C7 * P:(3 + i) * C7 * P] for i in range(2)]

        def dense_buf(k):
            base = bufB if k < 8 else bufN
            return base[:, (k % 8) * ROWS:(k % 8 + 1) * ROWS]

        dx, dy, dq, dr, h0, h1, do = ([dense_buf(2 * k + u) for u in range(2)] for k in range(7))
        rec_sb = [b[:, 0:NK * RW].rearrange("p (n r) -> p n r", r=RW)
                  for b in (bufA[:], bufG[:])]

        loaded = sem("loaded")
        attr_loaded = sem("attr_loaded")
        consts_ready = sem("consts_ready")
        rec_in = [sem(f"rec_in{i}") for i in range(2)]
        rec_out = [sem(f"rec_out{i}") for i in range(2)]
        staged = [sem(f"staged{i}") for i in range(2)]
        landed = [sem(f"landed{i}") for i in range(2)]
        copied = [sem(f"copied{i}") for i in range(2)]
        out_staged = [sem(f"out_staged{i}") for i in range(2)]
        scattered = [sem(f"scattered{i}") for i in range(2)]
        pool_tick = sem("pool_tick")
        iota_done = sem("iota_done")
        slots_ready = sem("slots_ready")
        src_slots_ready = sem("src_slots_ready")
        table_ready = sem("table_ready")
        table_stored = sem("table_stored")
        state_ready = sem("state_ready")
        vdone = sem("vdone")
        tail_ready = sem("tail_ready")
        carry_ready = sem("carry_ready")
        centered = sem("centered")
        squared = sem("squared")
        var_ready = sem("var_ready")
        rstd_ready = sem("rstd_ready")
        act_in = sem("act_in")
        act_out = sem("act_out")
        adone = sem("adone")
        sp_tick = sem("sp_tick")
        dve_tick = sem("dve_tick")
        d_in = [sem(f"d_in{u}") for u in range(2)]
        d_pe = [sem(f"d_pe{u}") for u in range(2)]
        d_act = [sem(f"d_act{u}") for u in range(2)]
        d_dve = [sem(f"d_dve{u}") for u in range(2)]
        d_out = [sem(f"d_out{u}") for u in range(2)]
        m_t = sem("m_t")
        m_in = sem("m_in")
        m_x = sem("m_x")
        m_h = sem("m_h")
        m_a = sem("m_a")
        m_b = sem("m_b")
        m_o = sem("m_o")
        m_y = sem("m_y")
        conv_open = sem("conv_open")
        wrow_in = [sem(f"wrow_in{i}") for i in range(2)]
        hid_ready = sem("hid_ready")
        hid_free = sem("hid_free")
        r_ready = sem("r_ready")
        r_used = sem("r_used")
        out_done = sem("out_done")

        LOADS = 21
        PE_D, ACT_D, DVE_D = 12, 14, 7

        block = ctx.enter_context(nc.Block())

        @block.sync
        def _(sp):
            e_view = lambda a: a.rearrange("(p j) -> p j", p=P)
            pairs = [(src_i[:], e_view(src)), (dst_i[:], e_view(dst)), (next_i[:], e_view(dst_next)),
                     (dfirst[:], dst_first.partition_broadcast(P)),
                     (up_sb[:], upper), (id_sb[:], ident), (cen_sb[:], center), (avg_sb[:], average),
                     (relv[:], rel.rearrange("(p j) c -> p j c", p=P)),
                     (attn_sb[:].rearrange("p a d -> p (a d)"), attn_w.partition_broadcast(P)),
                     (w1_sb[:], w1.rearrange("a h -> h a")),
                     (w2_sb[0:HID, :], w2), (w2_sb[HID:HID + 1, :], b2.unsqueeze(0)),
                     (b1_sb[:], b1.unsqueeze(1)),
                     (gb2_row[:], gcn_b2.partition_broadcast(P))]
            for i in range(2):
                pairs.append((gb1_sb[HID * i:HID * (i + 1), :], gcn_b1.unsqueeze(1)))
            for i in range(NQ):
                pairs.append((gb2_col[D * i:D * (i + 1), :], gcn_b2.unsqueeze(1)))
            for a, b in pairs:
                sp.dma_start(a, b).then_inc(loaded, 16)
            sp.wait_ge(consts_ready, 1)
            for q in range(NQ):
                sp.dma_start(gw1_sb[D * q:D * (q + 1), HID * q:HID * (q + 1)], gcn_w1).then_inc(attr_loaded, 16)
                a, r = q // 2, q % 2
                sp.dma_start(gw2_sb[HID * r:HID * (r + 1), a, D * q:D * (q + 1)], gcn_w2).then_inc(attr_loaded, 16)

            def gather(first, idx, dest, width):
                def stage(c, h):
                    sp.dma_start(ring_idx[:, h, :], idx[:, bass.ds(c, U)]).then_inc(staged[h], 16)

                def take(g, h):
                    sp.wait_ge(landed[h], 16 * U * (first + g + 1))
                    sp.dma_start(dest[:, bass.ds((2 * g + h) * U * width, U * width)],
                                 ring_rows[:, h, 0:U * width]).then_inc(copied[h], 16)
                    sp.wait_ge(copied[h], 16 * (first + g + 1))
                    sp.sem_inc(sp_tick, 1)

                for h in range(2):
                    stage(h * U, h)
                with sp.Fori(0, GROUPS // 2 - 1) as g:
                    for h in range(2):
                        take(g, h)
                        stage((2 * g + 2 + h) * U, h)
                for h in range(2):
                    take(GROUPS // 2 - 1, h)

            def scatter(first, idx, rows, width):
                def stage(c, h):
                    sp.dma_start(ring_idx[:, h, :], idx[:, bass.ds(c, U)]).then_inc(out_staged[h], 16)
                    sp.dma_start(ring_rows[:, h, 0:U * width],
                                 rows[:, bass.ds(c * width, U * width)]).then_inc(out_staged[h], 16)

                for h in range(2):
                    stage(h * U, h)
                with sp.Fori(0, GROUPS // 2 - 1) as g:
                    for h in range(2):
                        sp.wait_ge(scattered[h], 16 * U * (first + g + 1))
                        sp.sem_inc(sp_tick, 1)
                        stage((2 * g + 2 + h) * U, h)
                for h in range(2):
                    sp.wait_ge(scattered[h], 16 * U * (first + GROUPS // 2))

            H = GROUPS // 2
            sp.wait_ge(loaded, 16 * LOADS)
            gather(0, dst_i, xd[:].rearrange("p j d -> p (j d)"), D)
            sp.wait_ge(slots_ready, 1)
            for i in range(2):
                sp.wait_ge(rec_out[i], 16 * 4)
            scatter(0, pair_i, slotdeg[:].rearrange("p j c -> p (j c)"), 2)
            gather(H, src_i, bufG, RW)
            with sp.Fori(0, APPNP_STEPS - 1) as it:
                sp.wait_ge(table_ready, it + 1)
                sp.dma_start(tables[0].rearrange("(p j) d -> p (j d)", p=P), bufA[:]).then_inc(table_stored, 16)
                sp.wait_ge(table_stored, 16 * (it + 1))
                sp.wait_ge(src_slots_ready, 1)
                gather(2 * H + it * H, src_slot_i, bufG, D)
            for k in range(4):
                n = APPNP_STEPS - 1 + k
                sp.wait_ge(table_ready, n + 2)
                state = bufN[:] if k == 3 else xd[:].rearrange("p j d -> p (j d)")
                sp.dma_start(tables[1 + k].rearrange("(p j) d -> p (j d)", p=P), state).then_inc(table_stored, 16)
                sp.wait_ge(table_stored, 16 * (n + 1))
                gather((2 + n) * H, src_slot_i, bufG, D)
            sp.wait_ge(state_ready, 1)
            for u in range(2):
                sp.wait_ge(d_out[u], 16 * PAIRS)
            scatter(H, node_i, xd[:].rearrange("p j d -> p (j d)"), D)

        @block.gpsimd
        def _(pool):
            nc.gpsimd.iota(slot_i[:], pattern=[[1, T]], base=0, channel_multiplier=T).then_inc(iota_done, 1)
            H = GROUPS // 2

            def gather(first, table, width):
                with pool.Fori(0, H) as g:
                    for h in range(2):
                        pool.wait_ge(staged[h], 16 * (first + g + 1))
                        pool.sem_inc(pool_tick, 1)
                        for c in range(U):
                            pool.indirect_dma_start(
                                ring_rows[:, h, c * width:(c + 1) * width], None, table,
                                bass.IndirectOffsetOnAxis(ap=ring_idx[:, h, c:c + 1], axis=0),
                            ).then_inc(landed[h], 16)

            def scatter(first, table, width):
                with pool.Fori(0, H) as g:
                    for h in range(2):
                        pool.wait_ge(out_staged[h], 32 * (first + g + 1))
                        pool.sem_inc(pool_tick, 1)
                        for c in range(U):
                            pool.indirect_dma_start(
                                table, bass.IndirectOffsetOnAxis(ap=ring_idx[:, h, c:c + 1], axis=0),
                                ring_rows[:, h, c * width:(c + 1) * width], None,
                            ).then_inc(scattered[h], 16)

            gather(0, x[0:NR, :], D)
            scatter(0, rec_pairs, 2)
            gather(H, rec[0:NR, :], RW)
            with pool.Fori(0, APPNP_STEPS - 1) as it:
                gather(2 * H + it * H, tables[0], D)
            for k in range(4):
                gather((1 + APPNP_STEPS + k) * H, tables[1 + k], D)
            scatter(H, out, D)
            for h in range(2):
                pool.wait_ge(scattered[h], 16 * U * 2 * H)

        @block.tensor
        def _(pe):
            mm = nc.tensor.matmul
            pe.wait_ge(loaded, 16 * LOADS)
            pe.wait_ge(tail_ready, 1)
            nc.tensor.transpose(carry[:, 0:P], link_f[:], id_sb[:]).then_inc(carry_ready, 1)
            pe.wait_ge(tail_ready, 2)
            mm(carry[:, 0:1], link_f[:], deg[:, T - 1:T], start=True, stop=True).then_inc(carry_ready, 1)
            n = [2]

            pe.wait_ge(attr_loaded, 16 * 2 * NQ)
            with pe.Fori(0, PAIRS) as i:
                def step(u, ready, done):
                    pe.wait_ge(ready[u], i * {id(d_act): ACT_D, id(d_dve): DVE_D}[id(ready)] + done)

                for u in range(2):
                    pe.wait_ge(d_in[u], 16 * (i + 1))
                    xc = dx[u].rearrange("p (b c) -> p b c", b=4)
                    for b in range(4):
                        ins = nc.tensor.transpose(ps[:, u, b * P:(b + 1) * P], xc[:, b, :], id_sb[:])
                    ins.then_inc(d_pe[u], 1)
                for l in range(4):
                    for u in range(2):
                        step(u, *((d_act, 1) if l == 0 else (d_dve, l if l < 3 else 5)))
                        mm(ps[:, 2 + u, :], cen_sb[:], dy[u], start=True, stop=True).then_inc(d_pe[u], 1)
                    for u in range(2):
                        step(u, d_act, (2 if l < 3 else 3) + 3 * l)
                        mm(ps[:, u, :], avg_sb[:], dq[u], start=True, stop=True).then_inc(d_pe[u], 1)
                    if l == 2:
                        for u in range(2):
                            step(u, d_dve, 3)
                            mm(ps[:, u, :], gw1_sb[:, 0:P], dy[u], start=True, stop=True)
                            mm(ps[:, 2 + u, :], gw1_sb[:, P:2 * P], dy[u], start=True, stop=True).then_inc(d_pe[u], 1)
                        for u in range(2):
                            step(u, d_act, 11)
                            step(u, d_dve, 4)
                            mm(ps[:, u, :], gw2_sb[:, 0, :], h0[u], start=True, stop=False)
                            mm(ps[:, u, :], gw2_sb[:, 1, :], h1[u], start=False, stop=True).then_inc(d_pe[u], 1)
                for u in range(2):
                    step(u, d_dve, 6)
                    yc = dy[u].rearrange("p (b c) -> p b c", b=4)
                    for b in range(4):
                        ins = nc.tensor.transpose(ps[:, 2 + u, b * P:(b + 1) * P], yc[:, b, :], id_sb[:])
                    ins.then_inc(d_pe[u], 1)

            def hand_on(width, lhs=link_f, tail=None):
                pe.wait_ge(tail_ready, n[0] + 1)
                mm(carry[:, 0:width], lhs[:], tail, start=True, stop=True).then_inc(carry_ready, 1)
                n[0] += 1

            tails = B_dj[:, :, T - 1]
            hand_on(D, tail=tails)
            with pe.Fori(0, APPNP_STEPS - 1) as it:
                pe.wait_ge(tail_ready, n[0] + 1 + it)
                mm(carry[:, 0:D], link_f[:], tails, start=True, stop=True).then_inc(carry_ready, 1)
            n[0] += APPNP_STEPS - 1
            pe.wait_ge(tail_ready, n[0] + 1)
            mm(carry[:, 0:P], ones[:, 0:P], diag[:], start=True, stop=True).then_inc(carry_ready, 1)
            n[0] += 1
            hand_on(2, link_b, first2[:])
            hand_on(1, tail=ta[:, T - 1:T])
            hand_on(D, tail=tails)

            with pe.Fori(0, T // C7 // 2) as i:
                for s in range(2):
                    k = 2 * i + s
                    pe.wait_ge(hid_ready, k + 1)
                    for c in range(C7):
                        before = c - 5 + C7 if c >= 5 else c + 5 if c < 2 else c
                        pe.wait_ge(r_used, k * C7 + before + 1)
                        mm(ps[:, c % 5, 0:R_DIM], hid[s][:, c * P:(c + 1) * P], w2_sb[:],
                           start=True, stop=True).then_inc(r_ready, 1)
                    pe.wait_ge(r_ready, (k + 1) * C7)
                    pe.sem_inc(hid_free, 1)
            hand_on(D, tail=tails)
            hand_on(D, tail=tails)

            for m in range(2):
                with pe.Fori(0, T // 28) as i:
                    k = i + m * (T // 28)
                    pe.wait_ge(m_in, k + 1)
                    pe.wait_ge(m_x, k + 1)
                    for c in range(7):
                        ins = nc.tensor.transpose(ps[:, 0:2, :].rearrange("p a b -> p (a b)")[:, c * P:(c + 1) * P],
                                                  bufB[:, (21 + c) * P:(22 + c) * P], id_sb[:])
                    ins.then_inc(m_t, 1)
                    pe.wait_ge(m_a, k * 2 + 1)
                    xt = bufB[:, 0:7 * P]
                    for s in range(2):
                        for half in range(2):
                            o = half * 448
                            ins = mm(ps[:, 2 + 2 * s + half, 0:448], gw1_sb[:, s * P:(s + 1) * P],
                                     xt[:, o:o + 448], start=True, stop=True)
                    ins.then_inc(m_h, 1)
                    pe.wait_ge(m_a, k * 2 + 2)
                    pe.wait_ge(m_b, k + 1)
                    for c in range(7):
                        for s in range(2):
                            hs = bufB[:, (1 + s) * 7 * P + c * P:(1 + s) * 7 * P + (c + 1) * P]
                            ins = mm(ps[:, c // 4, (c % 4) * P + s * HID:(c % 4) * P + (s + 1) * HID], hs,
                                     gw2_sb[:, s, s * HID:(s + 1) * HID], start=True, stop=True)
                    ins.then_inc(m_o, 1)
            hand_on(D, tail=tails)

        @block.scalar
        def _(act_e):
            A = nc.scalar.activation
            nc.scalar.preload_act_table_set("natural_log_exp_and_others")
            x_rec = x[0:NR, :].rearrange("(k p n) d -> k p n d", k=8, p=P)
            rec_rows = rec[0:NR, :].rearrange("(k p n) r -> k p (n r)", k=8, p=P)
            act_e.wait_ge(consts_ready, 1)
            for k in range(8):
                s = k % 2
                if k >= 2:
                    act_e.wait_ge(rec_out[s], 16 * (k // 2))
                act_e.dma_start(rec_sb[s][:, :, 0:D], x_rec[k]).then_inc(rec_in[s], 16)
                if k >= 1:
                    act_e.wait_ge(rec_in[1 - s], 16 * ((k - 1) // 2 + 1))
                    act_e.dma_start(rec_rows[k - 1], rec_sb[1 - s][:].rearrange("p n r -> p (n r)")).then_inc(rec_out[1 - s], 16)
            act_e.wait_ge(rec_in[1], 16 * 4)
            act_e.dma_start(rec_rows[7], rec_sb[1][:].rearrange("p n r -> p (n r)")).then_inc(rec_out[1], 16)

            x_rows = x.rearrange("(k r q) d -> k r (q d)", r=ROWS, q=NQ)
            o_rows = out[0:NR, :].rearrange("(k r q) d -> k r (q d)", r=ROWS, q=NQ)
            x_c = x_rows.rearrange("k (p b) c -> k p (b c)", p=P)
            o_c = o_rows.rearrange("k (p b) c -> k p (b c)", p=P)
            for u in range(2):
                act_e.dma_start(dx[u], x_c[u]).then_inc(d_in[u], 16)
            act_e.wait_ge(loaded, 16 * LOADS)
            with act_e.Fori(0, PAIRS) as i:
                def norm_steps(base_pe, base_act):
                    for u in range(2):
                        act_e.wait_ge(d_pe[u], i * PE_D + base_pe)
                        A(dq[u], ps[:, 2 + u, :], ACT.Square).then_inc(d_act[u], 1)
                    for u in range(2):
                        act_e.wait_ge(d_pe[u], i * PE_D + base_pe + 1)
                        A(dr[u], ps[:, u, :], ACT.Ln, bias=epsc[:, 0:1]).then_inc(d_act[u], 1)
                    for u in range(2):
                        act_e.wait_ge(d_act[u], i * ACT_D + base_act + 2)
                        A(dr[u], dr[u], ACT.Exp, bias=zeroc[:, 0:1], scale=-0.5).then_inc(d_act[u], 1)

                for u in range(2):
                    act_e.wait_ge(d_pe[u], i * PE_D + 1)
                    A(dy[u], ps[:, u, :], ACT.Copy, scale=1.1).then_inc(d_act[u], 1)
                    act_e.dma_start(dx[u], x_c[bass.ds(2 * i + 2 + u, 1)].rearrange("a p c -> (a p) c")).then_inc(d_in[u], 16)
                norm_steps(2, 1)
                norm_steps(4, 4)
                norm_steps(6, 7)
                for u in range(2):
                    act_e.wait_ge(d_pe[u], i * PE_D + 8)
                    A(h0[u], ps[:, u, :], ACT.Relu, bias=gb1_sb[:, 0:1]).then_inc(d_act[u], 1)
                norm_steps(10, 11)
                for u in range(2):
                    act_e.wait_ge(d_dve[u], i * DVE_D + 7)
                    act_e.dma_start(o_c[bass.ds(2 * i + u, 1)].rearrange("a p c -> (a p) c"), do[u]).then_inc(d_out[u], 16)

            for u in range(2):
                act_e.wait_ge(d_in[u], 16 * (PAIRS + 1))

            k_in = [0]

            def ln_exp(t):
                A(t, t, ACT.Ln, bias=zeroc[:, 0:1]).then_inc(adone, 1)
                k_in[0] += 1
                act_e.wait_ge(adone, k_in[0])
                return A(t, t, ACT.Exp, bias=zeroc[:, 0:1], scale=-0.5)

            norms = [0]

            def layer_norm(y, tmp):
                n = norms[0] + 1
                norms[0] = n
                act_e.wait_ge(centered, n)
                A(tmp, y, ACT.Square).then_inc(squared, 1)
                act_e.wait_ge(var_ready, n)
                A(lnv[:], lnv[:], ACT.Ln, bias=epsc[:, 0:1], scale=1.0 / D).then_inc(adone, 1)
                k_in[0] += 1
                act_e.wait_ge(adone, k_in[0])
                A(lnv[:], lnv[:], ACT.Exp, bias=zeroc[:, 0:1], scale=-0.5).then_inc(rstd_ready, 1)

            act_e.wait_ge(act_in, 1)
            for t in (norm_d, dinv_d, scale_s, dinv_s):
                ins = ln_exp(t[:])
            ins.then_inc(act_out, 1)
            flat = lambda t: t.rearrange("p j d -> p (j d)")
            layer_norm(flat(xd[:]), bufA[:])
            layer_norm(flat(xs[:]), bufA[:])
            act_e.wait_ge(act_in, 2)
            A(tb[:], tb[:], ACT.Exp, bias=zeroc[:, 0:1]).then_inc(act_out, 1)
            layer_norm(flat(xd[:]), bufA[:])
            wt_rows = wt_cols.rearrange("(k c) p -> k (c p)", c=C7)
            act_e.wait_ge(act_in, 3)
            ln_exp(ta[:]).then_inc(act_out, 1)
            layer_norm(flat(xs[:]), bufA[:])
            act_e.wait_ge(conv_open, 1)
            for s in range(2):
                act_e.dma_start(wrow[s], wt_rows[s].partition_broadcast(HID)).then_inc(wrow_in[s], 16)
            with act_e.Fori(0, T // C7 // 2) as i:
                for s in range(2):
                    act_e.wait_ge(wrow_in[s], 16 * (i + 1))
                    act_e.wait_ge(hid_free, 2 * i + s + 1)
                    A(hid[s][0:HID, :], wrow[s], ACT.Relu, bias=b1_sb[:, 0:1], scale=w1_sb[:, 0:1]).then_inc(hid_ready, 1)
                    act_e.wait_ge(hid_ready, 2 * i + s + 1)
                    act_e.dma_start(wrow[s], wt_rows[bass.ds(2 * i + s + 2, 1)].rearrange("a c -> (a c)")
                                    .partition_broadcast(HID)).then_inc(wrow_in[s], 16)
            for s in range(2):
                act_e.wait_ge(wrow_in[s], 16 * (T // C7 // 2 + 1))
            layer_norm(flat(xd[:]), bufA[:])
            layer_norm(flat(xs[:]), bufA[:])
            for m, inp in enumerate((bufA[:], flat(xs[:]))):
                if m == 0:
                    act_e.wait_ge(m_x, 1)
                with act_e.Fori(0, T // 28) as i:
                    k = i + m * (T // 28)
                    A(bufB[:, 21 * P:28 * P], inp[:, bass.ds(i * 7 * P, 7 * P)], ACT.Copy).then_inc(m_in, 1)
                    act_e.wait_ge(m_t, k + 1)
                    A(bufB[:, 0:7 * P], ps[:, 0:2, :].rearrange("p a b -> p (a b)")[:, 0:7 * P], ACT.Copy).then_inc(m_a, 1)
                    act_e.wait_ge(m_h, k + 1)
                    A(bufB[:, 7 * P:14 * P].rearrange("p (a b) -> p a b", a=2), ps[:, 2:4, 0:448], ACT.Relu,
                      bias=gb1_sb[:, 0:1]).then_inc(m_a, 1)
            layer_norm(flat(xd[:]), bufA[:])

        @block.vector
        def _(dve):
            V = nc.vector
            done = [0]

            def link(ins):
                done[0] += 1
                ins.then_inc(vdone, 1)
                dve.wait_ge(vdone, done[0])

            def bj(col):
                return col.unsqueeze(2).to_broadcast([P, T, D])

            def bd(col):
                return col.unsqueeze(1).to_broadcast([P, D, T])

            turned = lambda t: t.rearrange("p j d -> p d j")
            flat = lambda t: t.rearrange("p j d -> p (j d)")

            V.memset(gw1_sb[:], 0.0).then_inc(vdone, 1)
            V.memset(gw2_sb[:], 0.0).then_inc(vdone, 1)
            V.memset(ones[:], 1.0).then_inc(vdone, 1)
            V.memset(epsc[:], EPS).then_inc(vdone, 1)
            V.memset(zeroc[:], 0.0).then_inc(vdone, 1)
            V.memset(cont[:, 0:1], 0.0).then_inc(vdone, 1)
            V.memset(rec_sb[0][:, :, D:RW], 0.0).then_inc(vdone, 1)
            V.memset(rec_sb[1][:, :, D:RW], 0.0).then_inc(vdone, 1)
            done[0] = 8
            dve.wait_ge(vdone, 8)
            dve.sem_inc(consts_ready, 1)

            dve.wait_ge(loaded, 16 * LOADS)
            link(V.tensor_copy(dstf[:], dst_i[:]))
            link(V.tensor_copy(ta[:], next_i[:]))
            link(V.tensor_tensor(cont[:, 1:T], dstf[:, 1:T], dstf[:, 0:T - 1], ALU.is_equal))
            link(V.tensor_tensor(contn[:], dstf[:], ta[:], ALU.is_equal))
            link(V.tensor_scalar(last[:], contn[:], -1.0, 1.0, ALU.mult, ALU.add))
            link(V.tensor_scalar(infirst[:], dstf[:], dstf[:, 0:1], None, ALU.is_equal))
            link(V.tensor_copy(diag[:], dfirst[:]))
            V.scalar_tensor_tensor(out=link_f[:], in0=diag[:], scalar=dstf[:, T - 1:T], in1=up_sb[:],
                                   op0=ALU.is_equal, op1=ALU.mult).then_inc(tail_ready, 1)
            dve.wait_ge(carry_ready, 1)
            link(V.tensor_copy(link_b[:], carry[:, 0:P]))
            link(V.tensor_scalar(nolink[:], link_b[:], -1.0, BIG, ALU.add, ALU.mult))
            V.tensor_tensor_scan(deg[:], cont[:], ones[:], 0.0, ALU.mult, ALU.add).then_inc(tail_ready, 1)
            dve.wait_ge(carry_ready, 2)
            link(V.scalar_tensor_tensor(out=deg[:], in0=infirst[:], scalar=carry[:, 0:1], in1=deg[:],
                                        op0=ALU.mult, op1=ALU.add))
            dve.wait_ge(iota_done, 1)
            link(V.tensor_copy(slotdeg[:, :, 0], slot_i[:]))
            link(V.tensor_copy(slotdeg[:, :, 1], deg[:]))
            link(V.tensor_scalar(ta[:], slotdeg[:, :, 0], float(NR), None, ALU.add))
            link(V.tensor_tensor(tb[:], dstf[:], ta[:], ALU.subtract))
            link(V.tensor_tensor(tb[:], tb[:], last[:], ALU.mult))
            link(V.tensor_tensor(tb[:], tb[:], ta[:], ALU.add))
            link(V.tensor_copy(node_i[:], tb[:]))
            link(V.tensor_scalar(tb[:], tb[:], float(RW // 2), float(D // 2), ALU.mult, ALU.add))
            V.tensor_copy(pair_i[:], tb[:]).then_inc(slots_ready, 1)
            link(V.tensor_copy(contf[:], bd(cont[:])))

            def dense_round(i, first):
                def scaled(k, base_act):
                    for u in range(2):
                        dve.wait_ge(d_act[u], i * ACT_D + base_act)
                        V.tensor_tensor(dy[u], ps[:, 2 + u, :], dr[u], ALU.mult).then_inc(d_dve[u], 1)

                scaled(1, 4)
                scaled(2, 7)
                scaled(3, 10)
                for u in range(2):
                    dve.wait_ge(d_pe[u], i * PE_D + 8)
                    V.tensor_scalar(h1[u], ps[:, 2 + u, :], gb1_sb[:, 0:1], 0.0, ALU.add, ALU.max).then_inc(d_dve[u], 1)
                for u in range(2):
                    dve.wait_ge(d_pe[u], i * PE_D + 9)
                    V.scalar_tensor_tensor(out=dy[u], in0=ps[:, u, :], scalar=gb2_col[:, 0:1], in1=dy[u],
                                           op0=ALU.add, op1=ALU.add).then_inc(d_dve[u], 1)
                scaled(6, 14)
                for u in range(2):
                    dve.wait_ge(d_pe[u], i * PE_D + 12)
                    if not first:
                        dve.wait_ge(d_out[u], 16 * i)
                    V.tensor_copy(do[u], ps[:, 2 + u, :]).then_inc(d_dve[u], 1)

            dense_round(0, True)
            with dve.Fori(1, PAIRS) as i:
                dense_round(i, False)

            n_carry = [2]

            def segment_sums():
                V.tensor_tensor_scan(bufB[:], contf[:].rearrange("p d j -> p (d j)"), bufA[:], 0.0,
                                     ALU.mult, ALU.add).then_inc(tail_ready, 1)
                n_carry[0] += 1
                dve.wait_ge(carry_ready, n_carry[0])
                link(V.tensor_tensor(G_dj, bd(infirst[:]), carry[:, 0:D].unsqueeze(2).to_broadcast([P, D, T]), ALU.mult))
                link(V.tensor_tensor(A_jd.rearrange("p j d -> p d j"), B_dj, G_dj, ALU.add))

            norms = [0]

            def layer_norm(y, tmp, signal=None):
                norms[0] += 1
                n = norms[0]
                link(V.tensor_reduce(lnv[:], y, AX.X, ALU.add))
                link(V.tensor_scalar(lnv[:], lnv[:], 1.0 / D, None, ALU.mult))
                V.tensor_tensor(y, y, bj(lnv[:]), ALU.subtract).then_inc(centered, 1)
                dve.wait_ge(squared, n)
                V.tensor_reduce(lnv[:], tmp, AX.X, ALU.add).then_inc(var_ready, 1)
                dve.wait_ge(rstd_ready, n)
                link(V.tensor_tensor(y, y, bj(lnv[:]), ALU.mult))
                if signal is not None:
                    dve.sem_inc(signal, 1)

            def gathered(n):
                for h in range(2):
                    dve.wait_ge(copied[h], 16 * (GROUPS // 2) * (n + 1))

            def from_table():
                mask = act[:].bitcast(U32).unsqueeze(2).to_broadcast([P, T, D])
                link(V.copy_predicated(xs[:], mask, G_jd))

            gathered(1)
            link(V.tensor_scalar(act[:], G_rec[:, :, D + 1], 0.0, None, ALU.is_gt))
            link(V.tensor_tensor(ta[:], G_rec[:, :, D], slotdeg[:, :, 0], ALU.subtract))
            link(V.tensor_tensor(ta[:], ta[:], act[:], ALU.mult))
            link(V.tensor_tensor(ta[:], ta[:], slotdeg[:, :, 0], ALU.add))
            V.tensor_copy(src_slot_i[:], ta[:]).then_inc(src_slots_ready, 1)
            link(V.tensor_copy(norm_d[:], deg[:]))
            link(V.tensor_scalar(dinv_d[:], deg[:], 1.0, None, ALU.add))
            link(V.tensor_scalar(scale_s[:], G_rec[:, :, D + 1], 1.0, None, ALU.max))
            link(V.tensor_scalar(dinv_s[:], G_rec[:, :, D + 1], 1.0, None, ALU.add))
            dve.sem_inc(act_in, 1)
            link(V.tensor_copy(xs[:], G_rec[:, :, 0:D]))
            dve.wait_ge(act_out, 1)

            link(V.tensor_tensor(tb[:], scale_s[:], act[:], ALU.mult))
            for u in range(2):
                dve.wait_ge(d_out[u], 16 * PAIRS)
            link(V.tensor_tensor(N_dj, turned(xs[:]), bd(tb[:]), ALU.mult))
            link(V.tensor_tensor(scale_s[:], tb[:], tb[:], ALU.mult))
            link(V.tensor_scalar(scale_s[:], scale_s[:], 0.9, None, ALU.mult))
            link(V.tensor_copy(bufA[:], bufN[:]))
            segment_sums()
            dve.sem_inc(table_ready, 1)
            base, per, carries, H = done[0], 4, n_carry[0], GROUPS // 2
            with dve.Fori(0, APPNP_STEPS - 1) as it:
                def mark(k):
                    dve.wait_ge(vdone, base + it * per + k)

                for h in range(2):
                    dve.wait_ge(copied[h], 16 * H * 3 + it * 16 * H)
                V.tensor_tensor(A_dj, turned(G_jd), bd(scale_s[:]), ALU.mult).then_inc(vdone, 1)
                mark(1)
                V.scalar_tensor_tensor(out=bufA[:], in0=bufN[:], scalar=0.1, in1=bufA[:],
                                       op0=ALU.mult, op1=ALU.add).then_inc(vdone, 1)
                mark(2)
                V.tensor_tensor_scan(bufB[:], contf[:].rearrange("p d j -> p (d j)"), bufA[:], 0.0,
                                     ALU.mult, ALU.add).then_inc(tail_ready, 1)
                dve.wait_ge(carry_ready, carries + 1 + it)
                V.tensor_tensor(G_dj, bd(infirst[:]), carry[:, 0:D].unsqueeze(2).to_broadcast([P, D, T]),
                                ALU.mult).then_inc(vdone, 1)
                mark(3)
                V.tensor_tensor(A_jd.rearrange("p j d -> p d j"), B_dj, G_dj, ALU.add).then_inc(vdone, 1)
                mark(4)
                dve.sem_inc(table_ready, 1)
            done[0] += per * (APPNP_STEPS - 1)
            n_carry[0] += APPNP_STEPS - 1
            link(V.tensor_scalar(ta[:], norm_d[:], 0.9, None, ALU.mult))
            link(V.tensor_tensor(A_jd, A_jd, bj(ta[:]), ALU.mult))
            link(V.scalar_tensor_tensor(out=flat(xd[:]), in0=flat(xd[:]), scalar=1.1, in1=bufA[:],
                                        op0=ALU.mult, op1=ALU.add))
            layer_norm(xd[:], A_jd, table_ready)

            def leaf(t):
                link(V.tensor_scalar(flat(t), flat(t), 1.1, None, ALU.mult))

            def carried():
                n_carry[0] += 1
                dve.wait_ge(carry_ready, n_carry[0])

            leaf(xs[:])
            layer_norm(xs[:], A_jd)
            link(V.tensor_tensor(A_jd, xd[:], attn_sb[:, 1, :].unsqueeze(1).to_broadcast([P, T, D]), ALU.mult))
            link(V.tensor_reduce(td[:], A_jd, AX.X, ALU.add))
            gathered(APPNP_STEPS + 1)
            from_table()
            link(V.tensor_tensor(A_jd, xs[:], attn_sb[:, 0, :].unsqueeze(1).to_broadcast([P, T, D]), ALU.mult))
            link(V.tensor_reduce(tb[:], A_jd, AX.X, ALU.add))
            link(V.tensor_scalar(ta[:], cont[:], -1.0, BIG, ALU.add, ALU.mult))
            link(V.tensor_tensor_scan(tc[:], ta[:], tb[:], -BIG, ALU.add, ALU.max))
            V.tensor_scalar(diag[:], id_sb[:], tc[:, T - 1:T], None, ALU.mult).then_inc(tail_ready, 1)
            carried()
            link(V.tensor_tensor(diag[:], link_b[:], carry[:, 0:P], ALU.mult))
            link(V.tensor_tensor(diag[:], diag[:], nolink[:], ALU.add))
            link(V.tensor_reduce(colmax[:], diag[:], AX.X, ALU.max))
            link(V.tensor_scalar(ta[:], infirst[:], -1.0, BIG, ALU.add, ALU.mult))
            link(V.scalar_tensor_tensor(out=tc[:], in0=ta[:], scalar=colmax[:, 0:1], in1=tc[:],
                                        op0=ALU.add, op1=ALU.max))
            for r, t in enumerate((tc, td)):
                link(V.tensor_tensor(both[:, r, :], t[:], last[:], ALU.mult))
            for r in range(2):
                link(V.tensor_tensor(ta[:], both[:, r, :], infirst[:], ALU.mult))
                link(V.tensor_reduce(first2[:, r:r + 1], ta[:], AX.X, ALU.add))
            dve.sem_inc(tail_ready, 1)
            carried()
            link(V.tensor_copy(init2[:], carry[:, 0:2]))
            for r, t in enumerate((tc, td)):
                link(V.tensor_tensor_scan(t[:, ::-1], contn[:, ::-1], both[:, r, ::-1], init2[:, r:r + 1],
                                          ALU.mult, ALU.add))
            for t in (tb, tc):
                link(V.tensor_tensor(t[:], t[:], td[:], ALU.add))
                link(V.scalar_tensor_tensor(out=t[:], in0=t[:], scalar=0.01, in1=t[:], op0=ALU.mult, op1=ALU.max))
            V.tensor_tensor(tb[:], tb[:], tc[:], ALU.subtract).then_inc(act_in, 1)
            dve.wait_ge(act_out, 2)
            V.tensor_tensor_scan(ta[:], cont[:], tb[:], 0.0, ALU.mult, ALU.add).then_inc(tail_ready, 1)
            carried()
            link(V.scalar_tensor_tensor(out=ta[:], in0=infirst[:], scalar=carry[:, 0:1], in1=ta[:],
                                        op0=ALU.mult, op1=ALU.add))
            link(V.tensor_scalar(ta[:], ta[:], 1.0 / BIG, None, ALU.max))
            link(V.reciprocal(ta[:], ta[:]))
            link(V.tensor_tensor(A_dj, turned(xs[:]), bd(tb[:]), ALU.mult))
            segment_sums()
            link(V.tensor_tensor(A_jd, A_jd, bj(ta[:]), ALU.mult))
            link(V.tensor_tensor(xd[:], xd[:], A_jd, ALU.add))
            layer_norm(xd[:], A_jd, table_ready)

            w000, w011, w110, w101 = (wigner_3j(*l).flat[0] for l in ((0, 0, 0), (0, 1, 1), (1, 1, 0), (1, 0, 1)))
            sph = bufB[:, 3 * MULT * T:(3 * MULT + 8) * T].rearrange("p (j s) -> p j s", s=8)
            rx, ry, rz = (relv[:, :, i] for i in range(3))
            link(V.tensor_tensor(ta[:], rx, rx, ALU.mult))
            link(V.tensor_tensor(tb[:], ry, ry, ALU.mult))
            link(V.tensor_tensor(ta[:], ta[:], tb[:], ALU.add))
            link(V.tensor_tensor(tb[:], rz, rz, ALU.mult))
            V.tensor_tensor(ta[:], ta[:], tb[:], ALU.add).then_inc(act_in, 1)
            dve.wait_ge(act_out, 3)
            link(V.tensor_tensor(relv[:], relv[:], ta[:].unsqueeze(2).to_broadcast([P, T, 3]), ALU.mult))
            for s, r in enumerate((ry, rz, rx)):
                link(V.tensor_scalar(sph[:, :, s], r, c1, None, ALU.mult))
            for s, a, b in ((3, rx, ry), (4, ry, rz), (6, rx, rz)):
                link(V.scalar_tensor_tensor(out=sph[:, :, s], in0=a, scalar=c2a, in1=b, op0=ALU.mult, op1=ALU.mult))
            link(V.tensor_tensor(tb[:], rz, rz, ALU.mult))
            link(V.tensor_scalar(sph[:, :, 5], tb[:], 3 * c2b, -c2b, ALU.mult, ALU.add))
            link(V.scalar_tensor_tensor(out=tb[:], in0=rx, scalar=c2c, in1=rx, op0=ALU.mult, op1=ALU.mult))
            link(V.scalar_tensor_tensor(out=tc[:], in0=ry, scalar=c2c, in1=ry, op0=ALU.mult, op1=ALU.mult))
            link(V.tensor_tensor(sph[:, :, 7], tb[:], tc[:], ALU.subtract))
            for t in hid:
                link(V.memset(t[HID:HID + 1, :], 1.0))
            dve.sem_inc(hid_free, 2)
            dve.sem_inc(conv_open, 1)
            layer_norm(xs[:], A_jd)
            gathered(APPNP_STEPS + 2)
            from_table()
            vec = bufB[:, 0:3 * MULT * T].rearrange("p (j b v) -> p j b v", b=3, v=MULT)
            xs0 = xs[:, :, 0:MULT]
            xs1 = xs[:, :, MULT:D].rearrange("p j (v i) -> p j v i", i=3)
            link(V.tensor_scalar(vec[:, :, 0, :], xs0, norm[0] * w000 * y0, None, ALU.mult))
            link(V.tensor_scalar(vec[:, :, 2, :], xs0, norm[1] * w110, None, ALU.mult))
            prod = bufA[:, 0:3 * MULT * T].rearrange("p (j v i) -> p j v i", v=MULT, i=3)
            link(V.tensor_tensor(prod, xs1, sph[:, :, 0:3].unsqueeze(2).to_broadcast([P, T, MULT, 3]), ALU.mult))
            link(V.tensor_reduce(vec[:, :, 1, :], prod, AX.X, ALU.add))
            link(V.tensor_scalar(vec[:, :, 1, :], vec[:, :, 1, :], norm[0] * w011, None, ALU.mult))
            n_mk = 2 * 9
            mats = bufG[:, 0:n_mk * T].rearrange("p (j k o i) -> p j k o i", k=2, o=3, i=3)
            for k in (1, 2):
                w = wigner_3j(1, k, 1)
                for o in range(3):
                    for i in range(3):
                        terms = [(norm[1] * w[o, f, i], sph[:, :, (0 if k == 1 else 3) + f])
                                 for f in range(2 * k + 1) if abs(w[o, f, i]) > 1e-9]
                        m = mats[:, :, k - 1, o, i]
                        if not terms:
                            link(V.memset(m, 0.0))
                        for n, (c, y) in enumerate(terms):
                            link(V.tensor_scalar(m, y, c, None, ALU.mult) if n == 0 else
                                 V.scalar_tensor_tensor(out=m, in0=y, scalar=c, in1=m, op0=ALU.mult, op1=ALU.add))
            def rooms(buf, at, *shapes):
                for shape in shapes:
                    size = int(np.prod(shape))
                    assert at + size <= buf.shape[1]
                    yield buf[:, at:at + size]
                    at += size

            gk, gt, prod1, prod0 = rooms(bufG, n_mk * T, (C7, 3, MULT, 3), (6, C7, MULT, 3),
                                         (2, MULT, 3, 3 * MULT), (2, 3, MULT, MULT))
            q1, q0, q2 = rooms(bufN, 4 * C7 * P, (C7, MULT, 3), (C7, 3, MULT), (C7, MULT, 3))
            gk = gk.rearrange("p (c o v k) -> p c o v k", o=3, v=MULT, k=3)
            gk_flat = gk.rearrange("p c o v k -> p c o (v k)")
            gt = gt.rearrange("p (s c v i) -> p s c v i", c=C7, v=MULT, i=3)
            prod1 = prod1.rearrange("p (a u o w) -> p a u o w", a=2, u=MULT, o=3)
            prod0 = prod0.rearrange("p (a b u v) -> p a b u v", a=2, b=3, u=MULT)
            q1, q2 = (t.rearrange("p (c u o) -> p c u o", u=MULT, o=3) for t in (q1, q2))
            q0 = q0.rearrange("p (c b u) -> p c b u", b=3, u=MULT)
            dve.sem_inc(r_used, C7)
            PER = 7 + 6 + 4 * C7 + 4
            base = done[0]
            with dve.Fori(0, T // C7 // 2) as i:
                if True:
                    for s in range(2):
                        r = 2 * i + s
                        col = r * C7
                        cnt = [0]

                        def note(ins):
                            cnt[0] += 1
                            ins.then_inc(vdone, 1)

                        def settle():
                            dve.wait_ge(vdone, base + r * PER + cnt[0])

                        x1 = xs[:, bass.ds(col, C7), MULT:D].rearrange("p j (v i) -> p j v i", i=3)
                        mk = mats[:, bass.ds(col, C7)]
                        note(V.tensor_scalar(gk[:, :, :, :, 0].rearrange("p c o v -> p c v o"), x1,
                                             norm[1] * w101 * y0, None, ALU.mult))
                        for k in range(2):
                            for o in range(3):
                                note(V.tensor_tensor(gt[:, 3 * k + o], x1, mk[:, :, k, o, :].unsqueeze(2).to_broadcast(
                                    [P, C7, MULT, 3]), ALU.mult))
                        settle()
                        for k in range(2):
                            for o in range(3):
                                note(V.tensor_reduce(gk[:, :, o, :, 1 + k], gt[:, 3 * k + o], AX.X, ALU.add))
                        settle()
                        for c in range(C7):
                            dve.wait_ge(r_ready, col + c + 1)
                            rr = ps[:, c % 5, :]
                            note(V.tensor_tensor(
                                prod1[:, c % 2],
                                rr[:, 3 * MULT * MULT:R_DIM].rearrange("p (u w) -> p u w", u=MULT).unsqueeze(2).to_broadcast(
                                    [P, MULT, 3, 3 * MULT]),
                                gk_flat[:, c].unsqueeze(1).to_broadcast([P, MULT, 3, 3 * MULT]), ALU.mult))
                            note(V.tensor_tensor(
                                prod0[:, c % 2], rr[:, 0:3 * MULT * MULT].rearrange("p (b u v) -> p b u v", b=3, u=MULT),
                                vec[:, bass.ds(col + c, 1), :, :].rearrange("p a b v -> p (a b) v").unsqueeze(2).to_broadcast(
                                    [P, 3, MULT, MULT]), ALU.mult))
                            settle()
                            dve.sem_inc(r_used, 1)
                            note(V.tensor_reduce(q1[:, c], prod1[:, c % 2], AX.X, ALU.add))
                            note(V.tensor_reduce(q0[:, c], prod0[:, c % 2], AX.X, ALU.add))
                        settle()
                        out_c = A_dj[:, :, bass.ds(col, C7)]
                        note(V.tensor_tensor(out_c[:, 0:MULT, :].rearrange("p u c -> p c u"), q0[:, :, 0, :], q0[:, :, 1, :], ALU.add))
                        note(V.tensor_tensor(q2, q0[:, :, 2, :].unsqueeze(3).to_broadcast([P, C7, MULT, 3]),
                                             sph[:, bass.ds(col, C7), 0:3].unsqueeze(2).to_broadcast([P, C7, MULT, 3]), ALU.mult))
                        settle()
                        note(V.tensor_tensor(out_c[:, MULT:D, :].rearrange("p w c -> p c w"),
                                             q1.rearrange("p c u o -> p c (u o)"), q2.rearrange("p c u o -> p c (u o)"), ALU.add))
                        note(V.tensor_copy(colmax[:], zeroc[:]))
                        settle()
                        assert cnt[0] == PER, cnt[0]
            done[0] += PER * (T // C7)
            segment_sums()
            link(V.tensor_tensor(xd[:], xd[:], A_jd, ALU.add))
            layer_norm(xd[:], A_jd, table_ready)

            layer_norm(xs[:], A_jd)
            gathered(APPNP_STEPS + 3)
            from_table()
            link(V.tensor_tensor(A_dj, turned(xs[:]), bd(dinv_s[:]), ALU.mult))
            segment_sums()
            link(V.tensor_tensor(G_jd, xd[:], bj(dinv_d[:]), ALU.mult))
            link(V.tensor_tensor(A_jd, A_jd, G_jd, ALU.add))
            link(V.tensor_tensor(A_jd, A_jd, bj(dinv_d[:]), ALU.mult))
            dve.sem_inc(m_x, 1)
            for m, dest in enumerate((bufN[:], flat(xs[:]))):
                with dve.Fori(0, T // 28) as i:
                    k = i + m * (T // 28)
                    dve.wait_ge(m_h, k + 1)
                    V.tensor_scalar(bufB[:, 14 * P:21 * P].rearrange("p (a b) -> p a b", a=2), ps[:, 4:6, 0:448],
                                    gb1_sb[:, 0:1], 0.0, ALU.add, ALU.max).then_inc(m_b, 1)
                    dve.wait_ge(m_o, k + 1)
                    dve.sem_inc(dve_tick, 1)
                    V.tensor_copy(dest[:, bass.ds(i * 28 * D, 28 * D)],
                                  ps[:, 0:2, :].rearrange("p a b -> p (a b)")[:, 0:28 * D]).then_inc(m_x, 1)
                if m == 0:
                    dve.wait_ge(m_x, 1 + T // 28)
                    dve.sem_inc(table_ready, 1)
            dve.wait_ge(m_x, 1 + 2 * (T // 28))
            gathered(APPNP_STEPS + 4)
            from_table()
            link(V.tensor_tensor(A_dj, turned(xs[:]), bd(dinv_s[:]), ALU.mult))
            segment_sums()
            link(V.tensor_tensor(N_jd, N_jd, bj(dinv_d[:]), ALU.mult))
            link(V.tensor_tensor(A_jd, A_jd, N_jd, ALU.add))
            link(V.tensor_tensor(A_jd, A_jd, bj(dinv_d[:]), ALU.mult))
            link(V.tensor_tensor(A_jd, A_jd, gb2_row[:].unsqueeze(1).to_broadcast([P, T, D]), ALU.add))
            link(V.tensor_tensor(xd[:], xd[:], A_jd, ALU.add))
            layer_norm(xd[:], A_jd, state_ready)


def kernel(x, src, dst, edge_attr_3, edge_weight, L1_gnn_attn_w, L2_gnn_w1, L2_gnn_b1, L2_gnn_w2, L2_gnn_b2,
           L3_gnn_W1, L3_gnn_b1, L3_gnn_W2, L3_gnn_b2):
    import concourse.bacc as bacc
    from concourse.bass_utils import run_bass_kernel_spmd

    x, src, dst, rel, weight = (np.asarray(a) for a in (x, src, dst, edge_attr_3, edge_weight))
    n, e = x.shape[0], src.shape[0]
    T, E, NR = sizes(n, e)
    assert n < NR

    def padded(a, rows, value):
        return np.concatenate([a, np.full((rows - a.shape[0],) + a.shape[1:], value, a.dtype)])

    ends = padded(padded(dst, E, n), E + 1, n + 1)
    side = np.arange(P) // D
    same = (side[:, None] == side[None, :]).astype(np.float32) / D
    eye = np.eye(P, dtype=np.float32)
    arrays = {
        "x": padded(x, NR + 2 * ROWS * NQ, 0), "src": padded(src, E, 0),
        "dst": ends[:E], "dst_next": ends[1:], "dst_first": ends[:E:T],
        "rel": padded(rel, E, 1), "wt_cols": padded(padded(weight, E, 0).reshape(P, T).T, T + 2 * C7, 0),
        "attn_w": L1_gnn_attn_w, "w1": L2_gnn_w1, "b1": L2_gnn_b1, "w2": L2_gnn_w2, "b2": L2_gnn_b2,
        "gcn_w1": L3_gnn_W1, "gcn_b1": L3_gnn_b1, "gcn_w2": L3_gnn_W2, "gcn_b2": L3_gnn_b2,
        "ident": eye, "center": eye - same, "average": same,
        "upper": np.triu(np.ones((P, P), np.float32), 1),
    }
    arrays = {f"in_{k}": np.ascontiguousarray(v) for k, v in arrays.items()}
    nc = bacc.Bacc("TRN2", target_bir_lowering=False, num_devices=1)
    args = [nc.dram_tensor(k, v.shape, mybir.dt.from_np(v.dtype), kind="ExternalInput").ap()
            for k, v in arrays.items()]
    out = nc.dram_tensor("out", (NR + E, D), F32, kind="ExternalOutput").ap()
    gnn_kernel(nc, *args, out, e)
    return run_bass_kernel_spmd(nc, [arrays], core_ids=[0]).results[0]["out"][:n]
```

```python
from contextlib import ExitStack
from math import factorial, pi, sqrt

import numpy as np

import concourse.bass as bass
from concourse import mybir

F32 = mybir.dt.float32
BF16 = mybir.dt.bfloat16
I32 = mybir.dt.int32
U32 = mybir.dt.uint32
ALU = mybir.AluOpType
ACT = mybir.ActivationFunctionType
AX = mybir.AxisListType

P = 128
D = 32
HID = 64
U = 14
EPS = 1e-5
BIG = 1e30
APPNP_STEPS = 10
RW = D + 2
ROWS = 512
NQ = P // D
C7 = 7
MULT = 8
K1 = 72
K2 = 24
SLOT_BITS = 15


def sizes(n_nodes, n_edges):
    t = -(-n_edges // (P * 2 * U)) * 2 * U
    pair = 2 * ROWS * NQ
    return t, P * t, -(-n_nodes // pair) * pair


def _cg(j1, j2, j3, m1, m2, m3):
    if m1 + m2 != m3:
        return 0.0
    f = factorial
    pre = sqrt((2 * j3 + 1) * f(j3 + j1 - j2) * f(j3 - j1 + j2) * f(j1 + j2 - j3) / f(j1 + j2 + j3 + 1))
    pre *= sqrt(f(j3 + m3) * f(j3 - m3) * f(j1 - m1) * f(j1 + m1) * f(j2 - m2) * f(j2 + m2))
    s = 0.0
    for k in range(max(0, j2 - j3 - m1, j1 - j3 + m2), min(j1 + j2 - j3, j1 - m1, j2 + m2) + 1):
        s += (-1) ** k / (f(k) * f(j1 + j2 - j3 - k) * f(j1 - m1 - k) * f(j2 + m2 - k)
                          * f(j3 - j2 + m1 + k) * f(j3 - j1 - m2 + k))
    return pre * s


def _real_basis(l):
    a = np.zeros((2 * l + 1, 2 * l + 1), dtype=complex)
    a[l, l] = 1.0
    for m in range(1, l + 1):
        a[l + m, l + m] = (-1) ** m / sqrt(2)
        a[l + m, l - m] = 1.0 / sqrt(2)
        a[l - m, l - m] = 1j / sqrt(2)
        a[l - m, l + m] = -1j * (-1) ** m / sqrt(2)
    return a


def wigner_3j(l1, l2, l3):
    w = np.zeros((2 * l1 + 1, 2 * l2 + 1, 2 * l3 + 1), dtype=complex)
    for m1 in range(-l1, l1 + 1):
        for m2 in range(-l2, l2 + 1):
            if abs(m1 + m2) <= l3:
                w[m1 + l1, m2 + l2, l3 - m1 - m2] = ((-1) ** (l1 - l2 + m1 + m2) / sqrt(2 * l3 + 1)
                                                    * _cg(l1, l2, l3, m1, m2, m1 + m2))
    r = np.einsum("abc,ma,nb,oc->mno", w, _real_basis(l1).conj(), _real_basis(l2).conj(), _real_basis(l3).conj())
    top = r.flat[int(np.argmax(np.abs(r)))]
    return np.real(r / (top / abs(top)))


def gnn_kernel(nc, x, src, dst, dst_next, dst_first, rel, wt_cols, attn_w, w1, b1, w2, b2,
               gcn_w1, gcn_b1, gcn_w2, gcn_b2, ident, center, average, upper, out, n_edges):
    E = src.shape[0]
    T = E // P
    NR = out.shape[0] - E
    PAIRS = NR // (2 * ROWS * NQ)
    GROUPS = T // U
    NK = NR // P // 8
    R_DIM = w2.shape[1]
    E2 = P * K2
    assert E < 1 << SLOT_BITS and T < 1 << (24 - SLOT_BITS)

    norm = [sqrt(4 * pi) * sqrt(2 * lo + 1) / sqrt(sum(MULT * (2 * min(lo, li) + 1) for li in (0, 1)))
            for lo in (0, 1)]
    y0 = 0.5 / sqrt(pi)
    c1 = sqrt(3.0 / (4.0 * pi))
    c2a, c2b, c2c = 0.5 * sqrt(15.0 / pi), 0.25 * sqrt(5.0 / pi), 0.25 * sqrt(15.0 / pi)

    rec = nc.dram_tensor("node_records", (NR + E, RW), F32).ap()
    rec_pairs = rec.rearrange("n (a b) -> (n a) b", b=2)
    feeders = nc.dram_tensor("feeders", (E, 1), F32).ap()
    edge_records = nc.dram_tensor("edge_records", (E, 4), F32).ap()
    short_slots = nc.dram_tensor("short_slots", (NR + E2, 1), F32).ap()
    short_table = nc.dram_tensor("short_table", (E2, D), F32).ap()
    messages = nc.dram_tensor("messages", (E + E2, D), F32).ap()
    tables = [nc.dram_tensor(f"edge_table_{i}", (E, D), F32).ap() for i in range(5)]

    with ExitStack() as ctx:
        def sb(name, shape, dt=F32):
            return ctx.enter_context(nc.sbuf_tensor(name, shape, dt))

        def sem(name):
            return ctx.enter_context(nc.semaphore(name))

        ps = ctx.enter_context(nc.psum_tensor("ps", [P, 8, 512], F32))
        carry = ps[:, 7, :]

        xd = sb("xd", [P, T, D])
        xs = sb("xs", [P, T, D])
        bufA = sb("bufA", [P, T * D])
        bufB = sb("bufB", [P, T * D])
        bufN = sb("bufN", [P, T * D])
        bufG = sb("bufG", [P, T * RW])
        contf = sb("contf", [P, D, T], BF16)
        A_jd = bufA[:].rearrange("p (j d) -> p j d", d=D)
        A_dj = bufA[:].rearrange("p (d j) -> p d j", d=D)
        B_dj = bufB[:].rearrange("p (d j) -> p d j", d=D)
        N_jd = bufN[:].rearrange("p (j d) -> p j d", d=D)
        N_dj = bufN[:].rearrange("p (d j) -> p d j", d=D)
        G_jd = bufG[:, 0:T * D].rearrange("p (j d) -> p j d", d=D)
        G_dj = bufG[:, 0:T * D].rearrange("p (d j) -> p d j", d=D)
        G_rec = bufG[:].rearrange("p (j r) -> p j r", r=RW)

        ring_idx = sb("ring_idx", [P, 2, U], I32)
        ring_rows = sb("ring_rows", [P, 2, U * RW])

        src_i = sb("src_i", [P, T], I32)
        dst_i = sb("dst_i", [P, T], I32)
        next_i = sb("next_i", [P, T], I32)
        slot_i = sb("slot_i", [P, T], I32)
        node_i = sb("node_i", [P, T], I32)
        pair_i = sb("pair_i", [P, T], I32)
        src_slot_i = sb("src_slot_i", [P, T], I32)
        dstf = sb("dstf", [P, T])
        cont = sb("cont", [P, T])
        contn = sb("contn", [P, T])
        last = sb("last", [P, T])
        infirst = sb("infirst", [P, T])
        deg = sb("deg", [P, T])
        slotdeg = sb("slotdeg", [P, T, 2])
        act = sb("act", [P, T])
        scale_s = sb("scale_s", [P, T])
        norm_d = sb("norm_d", [P, T])
        dinv_s = sb("dinv_s", [P, T])
        dinv_d = sb("dinv_d", [P, T])
        relv = sb("relv", [P, T, 3])
        ta = sb("ta", [P, T])
        tb = sb("tb", [P, T])
        per_edge4 = sb("per_edge4", [P, 4 * T])
        erec = per_edge4[:].rearrange("p (j r) -> p j r", r=4)
        both = per_edge4[:, 0:2 * T].rearrange("p (r j) -> p r j", r=2)
        tc = per_edge4[:, 2 * T:3 * T]
        td = per_edge4[:, 3 * T:4 * T]
        lnv = sb("lnv", [P, T])
        first2 = sb("first2", [P, 2])
        init2 = sb("init2", [P, 2])
        colmax = sb("colmax", [P, 1])
        diag = sb("diag", [P, P])
        epsc = sb("epsc", [P, 1])
        zeroc = sb("zeroc", [P, 1])

        cand_key = sb("cand_key", [P, K1])
        cand_i = sb("cand_i", [P, K1], I32)
        cand_slot_i = sb("cand_slot_i", [P, K1], I32)
        cand_col = sb("cand_col", [P, K1])
        cand_feeders = sb("cand_feeders", [P, K1])
        fits = sb("fits", [P, 2])
        path_i = sb("path_i", [1, 1], I32)
        (e_key, e_valid, e_own, e_dst, e_cont, e_infirst, e_last, e_slot, e_q, e_fact, e_t) = (
            sb(n, [P, K2]) for n in ("e_key", "e_valid", "e_own", "e_dst", "e_cont", "e_infirst", "e_last",
                                     "e_slot", "e_q", "e_fact", "e_t"))
        (e_own_i, e_src_i, e_srcslot_i, e_put_i, e_q_i, e_msg_i, e_slot_i) = (
            sb(n, [P, K2], I32) for n in ("e_own_i", "e_src_i", "e_srcslot_i", "e_put_i", "e_q_i", "e_msg_i",
                                          "e_slot_i"))
        e_rec = sb("e_rec", [P, K2, 4])
        e_mdst = sb("e_mdst", [P, 2])
        link_e = sb("link_e", [P, P])
        SW = K2 * D
        g2, r2, base2, msg2, scan2, sum2, cont2, tmp2 = (bufB[:, k * SW:(k + 1) * SW] for k in range(8))
        short_jd = lambda t: t.rearrange("p (j d) -> p j d", d=D)
        short_dj = lambda t: t.rearrange("p (d j) -> p d j", d=D)

        id_sb = sb("id_sb", [P, P])
        cen_sb = sb("cen_sb", [P, P])
        avg_sb = sb("avg_sb", [P, P])
        up_sb = sb("up_sb", [P, P])
        ones = sb("ones", [P, T])
        dfirst = sb("dfirst", [P, P], I32)
        link_f = sb("link_f", [P, P])
        link_b = sb("link_b", [P, P])
        nolink = sb("nolink", [P, P])
        attn_sb = sb("attn_sb", [P, 2, D])
        w1_sb = sb("w1_sb", [HID, 1])
        w2_sb = sb("w2_sb", [HID + 1, R_DIM])
        b1_sb = sb("b1_sb", [HID, 1])
        gw1_sb = sb("gw1_sb", [P, NQ * HID])
        gw2_sb = sb("gw2_sb", [P, 2, P])
        gb1_sb = sb("gb1_sb", [P, 1])
        gb2_col = sb("gb2_col", [P, 1])
        gb2_row = sb("gb2_row", [P, D])
        wrow = [bufN[0:HID, i * C7 * P:(i + 1) * C7 * P] for i in range(2)]
        hid = [bufN[0:HID + 1, (2 + i) * C7 * P:(3 + i) * C7 * P] for i in range(2)]

        def dense_buf(k):
            base = bufB if k < 8 else bufN
            return base[:, (k % 8) * ROWS:(k % 8 + 1) * ROWS]

        dx, dy, dq, dr, h0, h1, do = ([dense_buf(2 * k + u) for u in range(2)] for k in range(7))
        rec_sb = [b[:, 0:NK * RW].rearrange("p (n r) -> p n r", r=RW)
                  for b in (bufA[:], bufG[:])]

        loaded = sem("loaded")
        attr_loaded = sem("attr_loaded")
        consts_ready = sem("consts_ready")
        rec_in = [sem(f"rec_in{i}") for i in range(2)]
        rec_out = [sem(f"rec_out{i}") for i in range(2)]
        staged = [sem(f"staged{i}") for i in range(2)]
        landed = [sem(f"landed{i}") for i in range(2)]
        copied = [sem(f"copied{i}") for i in range(2)]
        out_staged = [sem(f"out_staged{i}") for i in range(2)]
        scattered = [sem(f"scattered{i}") for i in range(2)]
        pool_tick = sem("pool_tick")
        iota_done = sem("iota_done")
        slots_ready = sem("slots_ready")
        table_ready = sem("table_ready")
        table_stored = sem("table_stored")
        state_ready = sem("state_ready")
        vdone = sem("vdone")
        zeroed = sem("zeroed")
        zeros_ready = sem("zeros_ready")
        feeders_ready = sem("feeders_ready")
        feeders_stored = sem("feeders_stored")
        cand_ready = sem("cand_ready")
        cand_landed = sem("cand_landed")
        erec_ready = sem("erec_ready")
        erec_stored = sem("erec_stored")
        path_known = sem("path_known")
        s_own_ready, s_src_ready, s_put_ready, s_q_ready, s_msg_ready = (
            sem(n) for n in ("s_own_ready", "s_src_ready", "s_put_ready", "s_q_ready", "s_msg_ready"))
        s_rec_landed, s_r_landed, s_put, s_q_landed, s_landed, s_msg_put, s_msg_loaded = (
            sem(n) for n in ("s_rec_landed", "s_r_landed", "s_put", "s_q_landed", "s_landed", "s_msg_put",
                             "s_msg_loaded"))
        s_table_ready, s_stored, s_tail, s_carry, s_vdone = (
            sem(n) for n in ("s_table_ready", "s_stored", "s_tail", "s_carry", "s_vdone"))
        g_staged = [sem(f"g_staged{i}") for i in range(2)]
        g_landed = [sem(f"g_landed{i}") for i in range(2)]
        g_copied = [sem(f"g_copied{i}") for i in range(2)]
        g_table_ready, g_stored, g_tail, g_carry, g_vdone = (
            sem(n) for n in ("g_table_ready", "g_stored", "g_tail", "g_carry", "g_vdone"))
        tail_ready = sem("tail_ready")
        carry_ready = sem("carry_ready")
        centered = sem("centered")
        squared = sem("squared")
        var_ready = sem("var_ready")
        rstd_ready = sem("rstd_ready")
        act_in = sem("act_in")
        act_out = sem("act_out")
        adone = sem("adone")
        sp_tick = sem("sp_tick")
        dve_tick = sem("dve_tick")
        d_in = [sem(f"d_in{u}") for u in range(2)]
        d_pe = [sem(f"d_pe{u}") for u in range(2)]
        d_act = [sem(f"d_act{u}") for u in range(2)]
        d_dve = [sem(f"d_dve{u}") for u in range(2)]
        d_out = [sem(f"d_out{u}") for u in range(2)]
        m_t = sem("m_t")
        m_in = sem("m_in")
        m_x = sem("m_x")
        m_h = sem("m_h")
        m_a = sem("m_a")
        m_b = sem("m_b")
        m_o = sem("m_o")
        m_y = sem("m_y")
        conv_open = sem("conv_open")
        wrow_in = [sem(f"wrow_in{i}") for i in range(2)]
        hid_ready = sem("hid_ready")
        hid_free = sem("hid_free")
        r_ready = sem("r_ready")
        r_used = sem("r_used")
        out_done = sem("out_done")

        LOADS = 21
        PE_D, ACT_D, DVE_D = 12, 14, 7

        block = ctx.enter_context(nc.Block())

        @block.sync
        def _(sp):
            e_view = lambda a: a.rearrange("(p j) -> p j", p=P)
            pairs = [(src_i[:], e_view(src)), (dst_i[:], e_view(dst)), (next_i[:], e_view(dst_next)),
                     (dfirst[:], dst_first.partition_broadcast(P)),
                     (up_sb[:], upper), (id_sb[:], ident), (cen_sb[:], center), (avg_sb[:], average),
                     (relv[:], rel.rearrange("(p j) c -> p j c", p=P)),
                     (attn_sb[:].rearrange("p a d -> p (a d)"), attn_w.partition_broadcast(P)),
                     (w1_sb[:], w1.rearrange("a h -> h a")),
                     (w2_sb[0:HID, :], w2), (w2_sb[HID:HID + 1, :], b2.unsqueeze(0)),
                     (b1_sb[:], b1.unsqueeze(1)),
                     (gb2_row[:], gcn_b2.partition_broadcast(P))]
            for i in range(2):
                pairs.append((gb1_sb[HID * i:HID * (i + 1), :], gcn_b1.unsqueeze(1)))
            for i in range(NQ):
                pairs.append((gb2_col[D * i:D * (i + 1), :], gcn_b2.unsqueeze(1)))
            for a, b in pairs:
                sp.dma_start(a, b).then_inc(loaded, 16)
            sp.wait_ge(consts_ready, 1)
            for q in range(NQ):
                sp.dma_start(gw1_sb[D * q:D * (q + 1), HID * q:HID * (q + 1)], gcn_w1).then_inc(attr_loaded, 16)
                a, r = q // 2, q % 2
                sp.dma_start(gw2_sb[HID * r:HID * (r + 1), a, D * q:D * (q + 1)], gcn_w2).then_inc(attr_loaded, 16)

            def gather(first, idx, dest, width, staged=staged, landed=landed, copied=copied):
                def stage(c, h):
                    sp.dma_start(ring_idx[:, h, :], idx[:, bass.ds(c, U)]).then_inc(staged[h], 16)

                def take(g, h):
                    sp.wait_ge(landed[h], 16 * U * (first + g + 1))
                    sp.dma_start(dest[:, bass.ds((2 * g + h) * U * width, U * width)],
                                 ring_rows[:, h, 0:U * width]).then_inc(copied[h], 16)
                    sp.wait_ge(copied[h], 16 * (first + g + 1))
                    sp.sem_inc(sp_tick, 1)

                for h in range(2):
                    stage(h * U, h)
                with sp.Fori(0, GROUPS // 2 - 1) as g:
                    for h in range(2):
                        take(g, h)
                        stage((2 * g + 2 + h) * U, h)
                for h in range(2):
                    take(GROUPS // 2 - 1, h)

            def scatter(first, idx, rows, width):
                def stage(c, h):
                    sp.dma_start(ring_idx[:, h, :], idx[:, bass.ds(c, U)]).then_inc(out_staged[h], 16)
                    sp.dma_start(ring_rows[:, h, 0:U * width],
                                 rows[:, bass.ds(c * width, U * width)]).then_inc(out_staged[h], 16)

                for h in range(2):
                    stage(h * U, h)
                with sp.Fori(0, GROUPS // 2 - 1) as g:
                    for h in range(2):
                        sp.wait_ge(scattered[h], 16 * U * (first + g + 1))
                        sp.sem_inc(sp_tick, 1)
                        stage((2 * g + 2 + h) * U, h)
                for h in range(2):
                    sp.wait_ge(scattered[h], 16 * U * (first + GROUPS // 2))

            H = GROUPS // 2
            sp.wait_ge(loaded, 16 * LOADS)
            gather(0, dst_i, xd[:].rearrange("p j d -> p (j d)"), D)
            sp.wait_ge(zeros_ready, 1)
            zeros = xs[:].rearrange("p j d -> p (j d)")
            sp.dma_start(messages[0:E, :].rearrange("(p j) d -> p (j d)", p=P), zeros).then_inc(zeroed, 16)
            sp.dma_start(short_slots[0:NR, :].rearrange("(p n) a -> p (n a)", p=P), zeros[:, 0:NR // P]).then_inc(zeroed, 16)
            sp.wait_ge(slots_ready, 1)
            for i in range(2):
                sp.wait_ge(rec_out[i], 16 * 4)
            scatter(0, pair_i, slotdeg[:].rearrange("p j c -> p (j c)"), 2)
            gather(H, src_i, bufG, RW)
            sp.wait_ge(feeders_ready, 1)
            sp.dma_start(feeders.rearrange("(p j) a -> p (j a)", p=P), lnv[:]).then_inc(feeders_stored, 16)
            sp.wait_ge(erec_ready, 1)
            sp.dma_start(edge_records.rearrange("(p j) r -> p (j r)", p=P), per_edge4[:]).then_inc(erec_stored, 16)
            table_0 = tables[0].rearrange("(p j) d -> p (j d)", p=P)
            sp.wait_ge(table_ready, 1)
            sp.dma_start(table_0, bufA[:]).then_inc(table_stored, 16)
            sp.wait_ge(path_known, 1)
            path = sp.value_load(path_i[0:1, 0:1], min_val=0, max_val=T + 1)
            with sp.If(path < K2 + 1):
                with sp.Fori(0, APPNP_STEPS - 2) as it:
                    sp.wait_ge(s_table_ready, it + 1)
                    sp.dma_start(short_table.rearrange("(p j) d -> p (j d)", p=P), sum2).then_inc(s_stored, 16)
                sp.wait_ge(s_msg_put, 16 * K2)
                sp.dma_start(bufG[:, 0:T * D], messages[0:E, :].rearrange("(p j) d -> p (j d)", p=P)).then_inc(
                    s_msg_loaded, 16)
            with sp.Else():
                sp.wait_ge(table_stored, 16)
                with sp.Fori(0, APPNP_STEPS - 1) as it:
                    sp.wait_ge(g_table_ready, it + 1)
                    sp.dma_start(table_0, bufA[:]).then_inc(g_stored, 16)
                    sp.wait_ge(g_stored, 16 * (it + 1))
                    gather(it * H, src_slot_i, bufG, D, g_staged, g_landed, g_copied)
            for k in range(4):
                n = 1 + k
                sp.wait_ge(table_ready, n + 1)
                state = bufN[:] if k == 3 else xd[:].rearrange("p j d -> p (j d)")
                sp.dma_start(tables[1 + k].rearrange("(p j) d -> p (j d)", p=P), state).then_inc(table_stored, 16)
                sp.wait_ge(table_stored, 16 * (n + 1))
                gather((1 + n) * H, src_slot_i, bufG, D)
            sp.wait_ge(state_ready, 1)
            for u in range(2):
                sp.wait_ge(d_out[u], 16 * PAIRS)
            scatter(H, node_i, xd[:].rearrange("p j d -> p (j d)"), D)

        @block.gpsimd
        def _(pool):
            nc.gpsimd.iota(slot_i[:], pattern=[[1, T]], base=0, channel_multiplier=T).then_inc(iota_done, 1)
            nc.gpsimd.iota(e_slot_i[:], pattern=[[1, K2]], base=0, channel_multiplier=K2).then_inc(iota_done, 1)
            H = GROUPS // 2

            def gather(first, table, width, staged=staged, landed=landed):
                with pool.Fori(0, H) as g:
                    for h in range(2):
                        pool.wait_ge(staged[h], 16 * (first + g + 1))
                        pool.sem_inc(pool_tick, 1)
                        for c in range(U):
                            pool.indirect_dma_start(
                                ring_rows[:, h, c * width:(c + 1) * width], None, table,
                                bass.IndirectOffsetOnAxis(ap=ring_idx[:, h, c:c + 1], axis=0),
                            ).then_inc(landed[h], 16)

            def scatter(first, table, width):
                with pool.Fori(0, H) as g:
                    for h in range(2):
                        pool.wait_ge(out_staged[h], 32 * (first + g + 1))
                        pool.sem_inc(pool_tick, 1)
                        for c in range(U):
                            pool.indirect_dma_start(
                                table, bass.IndirectOffsetOnAxis(ap=ring_idx[:, h, c:c + 1], axis=0),
                                ring_rows[:, h, c * width:(c + 1) * width], None,
                            ).then_inc(scattered[h], 16)

            gather(0, x[0:NR, :], D)
            scatter(0, rec_pairs, 2)
            gather(H, rec[0:NR, :], RW)

            def fetch(dest, table, idx, cols, landed):
                for c in range(cols):
                    pool.indirect_dma_start(dest(c), None, table,
                                            bass.IndirectOffsetOnAxis(ap=idx[:, c:c + 1], axis=0)).then_inc(landed, 16)

            def put(table, rows, idx, done):
                for c in range(K2):
                    pool.indirect_dma_start(table, bass.IndirectOffsetOnAxis(ap=idx[:, c:c + 1], axis=0),
                                            rows(c), None).then_inc(done, 16)

            pool.wait_ge(cand_ready, 1)
            pool.wait_ge(feeders_stored, 16)
            fetch(lambda c: cand_feeders[:, c:c + 1], feeders, cand_slot_i, K1, cand_landed)
            pool.wait_ge(path_known, 1)
            path = pool.value_load(path_i[0:1, 0:1], min_val=0, max_val=T + 1)
            with pool.If(path < K2 + 1):
                pool.wait_ge(s_own_ready, 1)
                pool.wait_ge(erec_stored, 16)
                fetch(lambda c: e_rec[:, c, :], edge_records, e_own_i, K2, s_rec_landed)
                pool.wait_ge(s_src_ready, 1)
                pool.wait_ge(table_stored, 16)
                fetch(lambda c: r2[:, c * D:(c + 1) * D], tables[0], e_srcslot_i, K2, s_r_landed)
                pool.wait_ge(s_put_ready, 1)
                put(short_slots, lambda c: e_q[:, c:c + 1], e_put_i, s_put)
                pool.wait_ge(s_put, 16 * K2)
                fetch(lambda c: e_t[:, c:c + 1], short_slots[0:NR, :], e_src_i, K2, s_q_landed)
                pool.wait_ge(s_q_ready, 1)
                with pool.Fori(0, APPNP_STEPS - 2) as it:
                    pool.wait_ge(s_stored, 16 * (it + 1))
                    pool.sem_inc(pool_tick, 1)
                    fetch(lambda c: g2[:, c * D:(c + 1) * D], short_table, e_q_i, K2, s_landed)
                pool.wait_ge(s_msg_ready, 1)
                put(messages, lambda c: msg2[:, c * D:(c + 1) * D], e_msg_i, s_msg_put)
            with pool.Else():
                with pool.Fori(0, APPNP_STEPS - 1) as it:
                    gather(it * H, tables[0], D, g_staged, g_landed)
            for k in range(4):
                gather((2 + k) * H, tables[1 + k], D)
            scatter(H, out, D)
            for h in range(2):
                pool.wait_ge(scattered[h], 16 * U * 2 * H)

        @block.tensor
        def _(pe):
            mm = nc.tensor.matmul
            pe.wait_ge(loaded, 16 * LOADS)
            pe.wait_ge(tail_ready, 1)
            nc.tensor.transpose(carry[:, 0:P], link_f[:], id_sb[:]).then_inc(carry_ready, 1)
            pe.wait_ge(tail_ready, 2)
            mm(carry[:, 0:1], link_f[:], deg[:, T - 1:T], start=True, stop=True).then_inc(carry_ready, 1)
            n = [2]

            pe.wait_ge(attr_loaded, 16 * 2 * NQ)
            with pe.Fori(0, PAIRS) as i:
                def step(u, ready, done):
                    pe.wait_ge(ready[u], i * {id(d_act): ACT_D, id(d_dve): DVE_D}[id(ready)] + done)

                for u in range(2):
                    pe.wait_ge(d_in[u], 16 * (i + 1))
                    xc = dx[u].rearrange("p (b c) -> p b c", b=4)
                    for b in range(4):
                        ins = nc.tensor.transpose(ps[:, u, b * P:(b + 1) * P], xc[:, b, :], id_sb[:])
                    ins.then_inc(d_pe[u], 1)
                for l in range(4):
                    for u in range(2):
                        step(u, *((d_act, 1) if l == 0 else (d_dve, l if l < 3 else 5)))
                        mm(ps[:, 2 + u, :], cen_sb[:], dy[u], start=True, stop=True).then_inc(d_pe[u], 1)
                    for u in range(2):
                        step(u, d_act, (2 if l < 3 else 3) + 3 * l)
                        mm(ps[:, u, :], avg_sb[:], dq[u], start=True, stop=True).then_inc(d_pe[u], 1)
                    if l == 2:
                        for u in range(2):
                            step(u, d_dve, 3)
                            mm(ps[:, u, :], gw1_sb[:, 0:P], dy[u], start=True, stop=True)
                            mm(ps[:, 2 + u, :], gw1_sb[:, P:2 * P], dy[u], start=True, stop=True).then_inc(d_pe[u], 1)
                        for u in range(2):
                            step(u, d_act, 11)
                            step(u, d_dve, 4)
                            mm(ps[:, u, :], gw2_sb[:, 0, :], h0[u], start=True, stop=False)
                            mm(ps[:, u, :], gw2_sb[:, 1, :], h1[u], start=False, stop=True).then_inc(d_pe[u], 1)
                for u in range(2):
                    step(u, d_dve, 6)
                    yc = dy[u].rearrange("p (b c) -> p b c", b=4)
                    for b in range(4):
                        ins = nc.tensor.transpose(ps[:, 2 + u, b * P:(b + 1) * P], yc[:, b, :], id_sb[:])
                    ins.then_inc(d_pe[u], 1)

            def hand_on(width, lhs=link_f, tail=None):
                pe.wait_ge(tail_ready, n[0] + 1)
                mm(carry[:, 0:width], lhs[:], tail, start=True, stop=True).then_inc(carry_ready, 1)
                n[0] += 1

            tails = B_dj[:, :, T - 1]
            hand_on(1, tail=ta[:, T - 1:T])
            hand_on(D, tail=tails)
            pe.wait_ge(tail_ready, n[0] + 1)
            mm(carry[0:1, 0:P], fits[:, 0:1], id_sb[:], start=True, stop=True).then_inc(carry_ready, 1)
            n[0] += 1
            pe.wait_ge(path_known, 1)
            path = pe.value_load(path_i[0:1, 0:1], min_val=0, max_val=T + 1)
            with pe.If(path < K2 + 1):
                pe.wait_ge(s_tail, 1)
                mm(carry[:, 0:P], ones[:, 0:P], diag[:], start=True, stop=True).then_inc(s_carry, 1)
                with pe.Fori(0, APPNP_STEPS - 2) as it:
                    pe.wait_ge(s_tail, it + 2)
                    mm(carry[:, 0:D], link_e[:], short_dj(scan2)[:, :, K2 - 1], start=True, stop=True).then_inc(s_carry, 1)
                pe.wait_ge(s_tail, APPNP_STEPS)
                mm(carry[:, 0:D], link_f[:], tails, start=True, stop=True).then_inc(s_carry, 1)
            with pe.Else():
                with pe.Fori(0, APPNP_STEPS - 1) as it:
                    pe.wait_ge(g_tail, it + 1)
                    mm(carry[:, 0:D], link_f[:], tails, start=True, stop=True).then_inc(g_carry, 1)
            pe.wait_ge(tail_ready, n[0] + 1)
            mm(carry[:, 0:P], ones[:, 0:P], diag[:], start=True, stop=True).then_inc(carry_ready, 1)
            n[0] += 1
            hand_on(2, link_b, first2[:])
            hand_on(1, tail=ta[:, T - 1:T])
            hand_on(D, tail=tails)

            with pe.Fori(0, T // C7 // 2) as i:
                for s in range(2):
                    k = 2 * i + s
                    pe.wait_ge(hid_ready, k + 1)
                    for c in range(C7):
                        before = c - 5 + C7 if c >= 5 else c + 5 if c < 2 else c
                        pe.wait_ge(r_used, k * C7 + before + 1)
                        mm(ps[:, c % 5, 0:R_DIM], hid[s][:, c * P:(c + 1) * P], w2_sb[:],
                           start=True, stop=True).then_inc(r_ready, 1)
                    pe.wait_ge(r_ready, (k + 1) * C7)
                    pe.sem_inc(hid_free, 1)
            hand_on(D, tail=tails)
            hand_on(D, tail=tails)

            for m in range(2):
                with pe.Fori(0, T // 28) as i:
                    k = i + m * (T // 28)
                    pe.wait_ge(m_in, k + 1)
                    pe.wait_ge(m_x, k + 1)
                    for c in range(7):
                        ins = nc.tensor.transpose(ps[:, 0:2, :].rearrange("p a b -> p (a b)")[:, c * P:(c + 1) * P],
                                                  bufB[:, (21 + c) * P:(22 + c) * P], id_sb[:])
                    ins.then_inc(m_t, 1)
                    pe.wait_ge(m_a, k * 2 + 1)
                    xt = bufB[:, 0:7 * P]
                    for s in range(2):
                        for half in range(2):
                            o = half * 448
                            ins = mm(ps[:, 2 + 2 * s + half, 0:448], gw1_sb[:, s * P:(s + 1) * P],
                                     xt[:, o:o + 448], start=True, stop=True)
                    ins.then_inc(m_h, 1)
                    pe.wait_ge(m_a, k * 2 + 2)
                    pe.wait_ge(m_b, k + 1)
                    for c in range(7):
                        for s in range(2):
                            hs = bufB[:, (1 + s) * 7 * P + c * P:(1 + s) * 7 * P + (c + 1) * P]
                            ins = mm(ps[:, c // 4, (c % 4) * P + s * HID:(c % 4) * P + (s + 1) * HID], hs,
                                     gw2_sb[:, s, s * HID:(s + 1) * HID], start=True, stop=True)
                    ins.then_inc(m_o, 1)
            hand_on(D, tail=tails)

        @block.scalar
        def _(act_e):
            A = nc.scalar.activation
            nc.scalar.preload_act_table_set("natural_log_exp_and_others")
            x_rec = x[0:NR, :].rearrange("(k p n) d -> k p n d", k=8, p=P)
            rec_rows = rec[0:NR, :].rearrange("(k p n) r -> k p (n r)", k=8, p=P)
            act_e.wait_ge(consts_ready, 1)
            for k in range(8):
                s = k % 2
                if k >= 2:
                    act_e.wait_ge(rec_out[s], 16 * (k // 2))
                act_e.dma_start(rec_sb[s][:, :, 0:D], x_rec[k]).then_inc(rec_in[s], 16)
                if k >= 1:
                    act_e.wait_ge(rec_in[1 - s], 16 * ((k - 1) // 2 + 1))
                    act_e.dma_start(rec_rows[k - 1], rec_sb[1 - s][:].rearrange("p n r -> p (n r)")).then_inc(rec_out[1 - s], 16)
            act_e.wait_ge(rec_in[1], 16 * 4)
            act_e.dma_start(rec_rows[7], rec_sb[1][:].rearrange("p n r -> p (n r)")).then_inc(rec_out[1], 16)

            x_rows = x.rearrange("(k r q) d -> k r (q d)", r=ROWS, q=NQ)
            o_rows = out[0:NR, :].rearrange("(k r q) d -> k r (q d)", r=ROWS, q=NQ)
            x_c = x_rows.rearrange("k (p b) c -> k p (b c)", p=P)
            o_c = o_rows.rearrange("k (p b) c -> k p (b c)", p=P)
            for u in range(2):
                act_e.dma_start(dx[u], x_c[u]).then_inc(d_in[u], 16)
            act_e.wait_ge(loaded, 16 * LOADS)
            with act_e.Fori(0, PAIRS) as i:
                def norm_steps(base_pe, base_act):
                    for u in range(2):
                        act_e.wait_ge(d_pe[u], i * PE_D + base_pe)
                        A(dq[u], ps[:, 2 + u, :], ACT.Square).then_inc(d_act[u], 1)
                    for u in range(2):
                        act_e.wait_ge(d_pe[u], i * PE_D + base_pe + 1)
                        A(dr[u], ps[:, u, :], ACT.Ln, bias=epsc[:, 0:1]).then_inc(d_act[u], 1)
                    for u in range(2):
                        act_e.wait_ge(d_act[u], i * ACT_D + base_act + 2)
                        A(dr[u], dr[u], ACT.Exp, bias=zeroc[:, 0:1], scale=-0.5).then_inc(d_act[u], 1)

                for u in range(2):
                    act_e.wait_ge(d_pe[u], i * PE_D + 1)
                    A(dy[u], ps[:, u, :], ACT.Copy, scale=1.1).then_inc(d_act[u], 1)
                    act_e.dma_start(dx[u], x_c[bass.ds(2 * i + 2 + u, 1)].rearrange("a p c -> (a p) c")).then_inc(d_in[u], 16)
                norm_steps(2, 1)
                norm_steps(4, 4)
                norm_steps(6, 7)
                for u in range(2):
                    act_e.wait_ge(d_pe[u], i * PE_D + 8)
                    A(h0[u], ps[:, u, :], ACT.Relu, bias=gb1_sb[:, 0:1]).then_inc(d_act[u], 1)
                norm_steps(10, 11)
                for u in range(2):
                    act_e.wait_ge(d_dve[u], i * DVE_D + 7)
                    act_e.dma_start(o_c[bass.ds(2 * i + u, 1)].rearrange("a p c -> (a p) c"), do[u]).then_inc(d_out[u], 16)

            for u in range(2):
                act_e.wait_ge(d_in[u], 16 * (PAIRS + 1))

            k_in = [0]

            def ln_exp(t):
                A(t, t, ACT.Ln, bias=zeroc[:, 0:1]).then_inc(adone, 1)
                k_in[0] += 1
                act_e.wait_ge(adone, k_in[0])
                return A(t, t, ACT.Exp, bias=zeroc[:, 0:1], scale=-0.5)

            norms = [0]

            def layer_norm(y, tmp):
                n = norms[0] + 1
                norms[0] = n
                act_e.wait_ge(centered, n)
                A(tmp, y, ACT.Square).then_inc(squared, 1)
                act_e.wait_ge(var_ready, n)
                A(lnv[:], lnv[:], ACT.Ln, bias=epsc[:, 0:1], scale=1.0 / D).then_inc(adone, 1)
                k_in[0] += 1
                act_e.wait_ge(adone, k_in[0])
                A(lnv[:], lnv[:], ACT.Exp, bias=zeroc[:, 0:1], scale=-0.5).then_inc(rstd_ready, 1)

            act_e.wait_ge(act_in, 1)
            for t in (norm_d, dinv_d, scale_s, dinv_s):
                ins = ln_exp(t[:])
            ins.then_inc(act_out, 1)
            flat = lambda t: t.rearrange("p j d -> p (j d)")
            layer_norm(flat(xd[:]), bufA[:])
            layer_norm(flat(xs[:]), bufA[:])
            act_e.wait_ge(act_in, 2)
            A(tb[:], tb[:], ACT.Exp, bias=zeroc[:, 0:1]).then_inc(act_out, 1)
            layer_norm(flat(xd[:]), bufA[:])
            wt_rows = wt_cols.rearrange("(k c) p -> k (c p)", c=C7)
            act_e.wait_ge(act_in, 3)
            ln_exp(ta[:]).then_inc(act_out, 1)
            layer_norm(flat(xs[:]), bufA[:])
            act_e.wait_ge(conv_open, 1)
            for s in range(2):
                act_e.dma_start(wrow[s], wt_rows[s].partition_broadcast(HID)).then_inc(wrow_in[s], 16)
            with act_e.Fori(0, T // C7 // 2) as i:
                for s in range(2):
                    act_e.wait_ge(wrow_in[s], 16 * (i + 1))
                    act_e.wait_ge(hid_free, 2 * i + s + 1)
                    A(hid[s][0:HID, :], wrow[s], ACT.Relu, bias=b1_sb[:, 0:1], scale=w1_sb[:, 0:1]).then_inc(hid_ready, 1)
                    act_e.wait_ge(hid_ready, 2 * i + s + 1)
                    act_e.dma_start(wrow[s], wt_rows[bass.ds(2 * i + s + 2, 1)].rearrange("a c -> (a c)")
                                    .partition_broadcast(HID)).then_inc(wrow_in[s], 16)
            for s in range(2):
                act_e.wait_ge(wrow_in[s], 16 * (T // C7 // 2 + 1))
            layer_norm(flat(xd[:]), bufA[:])
            layer_norm(flat(xs[:]), bufA[:])
            for m, inp in enumerate((bufA[:], flat(xs[:]))):
                if m == 0:
                    act_e.wait_ge(m_x, 1)
                with act_e.Fori(0, T // 28) as i:
                    k = i + m * (T // 28)
                    A(bufB[:, 21 * P:28 * P], inp[:, bass.ds(i * 7 * P, 7 * P)], ACT.Copy).then_inc(m_in, 1)
                    act_e.wait_ge(m_t, k + 1)
                    A(bufB[:, 0:7 * P], ps[:, 0:2, :].rearrange("p a b -> p (a b)")[:, 0:7 * P], ACT.Copy).then_inc(m_a, 1)
                    act_e.wait_ge(m_h, k + 1)
                    A(bufB[:, 7 * P:14 * P].rearrange("p (a b) -> p a b", a=2), ps[:, 2:4, 0:448], ACT.Relu,
                      bias=gb1_sb[:, 0:1]).then_inc(m_a, 1)
            layer_norm(flat(xd[:]), bufA[:])

        @block.vector
        def _(dve):
            V = nc.vector
            done = [0]

            def link(ins):
                done[0] += 1
                ins.then_inc(vdone, 1)
                dve.wait_ge(vdone, done[0])

            def bj(col):
                return col.unsqueeze(2).to_broadcast([P, T, D])

            def bd(col):
                return col.unsqueeze(1).to_broadcast([P, D, T])

            turned = lambda t: t.rearrange("p j d -> p d j")
            flat = lambda t: t.rearrange("p j d -> p (j d)")

            V.memset(gw1_sb[:], 0.0).then_inc(vdone, 1)
            V.memset(gw2_sb[:], 0.0).then_inc(vdone, 1)
            V.memset(ones[:], 1.0).then_inc(vdone, 1)
            V.memset(epsc[:], EPS).then_inc(vdone, 1)
            V.memset(zeroc[:], 0.0).then_inc(vdone, 1)
            V.memset(cont[:, 0:1], 0.0).then_inc(vdone, 1)
            V.memset(rec_sb[0][:, :, D:RW], 0.0).then_inc(vdone, 1)
            V.memset(rec_sb[1][:, :, D:RW], 0.0).then_inc(vdone, 1)
            done[0] = 8
            dve.wait_ge(vdone, 8)
            dve.sem_inc(consts_ready, 1)

            V.memset(xs[:], 0.0).then_inc(zeros_ready, 1)

            dve.wait_ge(loaded, 16 * LOADS)
            link(V.tensor_copy(dstf[:], dst_i[:]))
            link(V.tensor_copy(ta[:], next_i[:]))
            link(V.tensor_tensor(cont[:, 1:T], dstf[:, 1:T], dstf[:, 0:T - 1], ALU.is_equal))
            link(V.tensor_tensor(contn[:], dstf[:], ta[:], ALU.is_equal))
            link(V.tensor_scalar(last[:], contn[:], -1.0, 1.0, ALU.mult, ALU.add))
            link(V.tensor_scalar(infirst[:], dstf[:], dstf[:, 0:1], None, ALU.is_equal))
            link(V.tensor_copy(diag[:], dfirst[:]))
            V.scalar_tensor_tensor(out=link_f[:], in0=diag[:], scalar=dstf[:, T - 1:T], in1=up_sb[:],
                                   op0=ALU.is_equal, op1=ALU.mult).then_inc(tail_ready, 1)
            dve.wait_ge(carry_ready, 1)
            link(V.tensor_copy(link_b[:], carry[:, 0:P]))
            link(V.tensor_scalar(nolink[:], link_b[:], -1.0, BIG, ALU.add, ALU.mult))
            V.tensor_tensor_scan(deg[:], cont[:], ones[:], 0.0, ALU.mult, ALU.add).then_inc(tail_ready, 1)
            dve.wait_ge(carry_ready, 2)
            link(V.scalar_tensor_tensor(out=deg[:], in0=infirst[:], scalar=carry[:, 0:1], in1=deg[:],
                                        op0=ALU.mult, op1=ALU.add))
            dve.wait_ge(iota_done, 2)
            link(V.tensor_copy(slotdeg[:, :, 0], slot_i[:]))
            link(V.tensor_copy(slotdeg[:, :, 1], deg[:]))
            link(V.tensor_scalar(ta[:], slotdeg[:, :, 0], float(NR), None, ALU.add))
            link(V.tensor_tensor(tb[:], dstf[:], ta[:], ALU.subtract))
            link(V.tensor_tensor(tb[:], tb[:], last[:], ALU.mult))
            link(V.tensor_tensor(tb[:], tb[:], ta[:], ALU.add))
            link(V.tensor_copy(node_i[:], tb[:]))
            link(V.tensor_scalar(tb[:], tb[:], float(RW // 2), float(D // 2), ALU.mult, ALU.add))
            V.tensor_copy(pair_i[:], tb[:]).then_inc(slots_ready, 1)
            link(V.tensor_copy(contf[:], bd(cont[:])))

            def dense_round(i, first):
                def scaled(k, base_act):
                    for u in range(2):
                        dve.wait_ge(d_act[u], i * ACT_D + base_act)
                        V.tensor_tensor(dy[u], ps[:, 2 + u, :], dr[u], ALU.mult).then_inc(d_dve[u], 1)

                scaled(1, 4)
                scaled(2, 7)
                scaled(3, 10)
                for u in range(2):
                    dve.wait_ge(d_pe[u], i * PE_D + 8)
                    V.tensor_scalar(h1[u], ps[:, 2 + u, :], gb1_sb[:, 0:1], 0.0, ALU.add, ALU.max).then_inc(d_dve[u], 1)
                for u in range(2):
                    dve.wait_ge(d_pe[u], i * PE_D + 9)
                    V.scalar_tensor_tensor(out=dy[u], in0=ps[:, u, :], scalar=gb2_col[:, 0:1], in1=dy[u],
                                           op0=ALU.add, op1=ALU.add).then_inc(d_dve[u], 1)
                scaled(6, 14)
                for u in range(2):
                    dve.wait_ge(d_pe[u], i * PE_D + 12)
                    if not first:
                        dve.wait_ge(d_out[u], 16 * i)
                    V.tensor_copy(do[u], ps[:, 2 + u, :]).then_inc(d_dve[u], 1)

            dense_round(0, True)
            with dve.Fori(1, PAIRS) as i:
                dense_round(i, False)

            n_carry = [2]

            def segment_sums():
                V.tensor_tensor_scan(bufB[:], contf[:].rearrange("p d j -> p (d j)"), bufA[:], 0.0,
                                     ALU.mult, ALU.add).then_inc(tail_ready, 1)
                n_carry[0] += 1
                dve.wait_ge(carry_ready, n_carry[0])
                link(V.tensor_tensor(G_dj, bd(infirst[:]), carry[:, 0:D].unsqueeze(2).to_broadcast([P, D, T]), ALU.mult))
                link(V.tensor_tensor(A_jd.rearrange("p j d -> p d j"), B_dj, G_dj, ALU.add))

            norms = [0]

            def layer_norm(y, tmp, signal=None):
                norms[0] += 1
                n = norms[0]
                link(V.tensor_reduce(lnv[:], y, AX.X, ALU.add))
                link(V.tensor_scalar(lnv[:], lnv[:], 1.0 / D, None, ALU.mult))
                V.tensor_tensor(y, y, bj(lnv[:]), ALU.subtract).then_inc(centered, 1)
                dve.wait_ge(squared, n)
                V.tensor_reduce(lnv[:], tmp, AX.X, ALU.add).then_inc(var_ready, 1)
                dve.wait_ge(rstd_ready, n)
                link(V.tensor_tensor(y, y, bj(lnv[:]), ALU.mult))
                if signal is not None:
                    dve.sem_inc(signal, 1)

            def gathered(n):
                for h in range(2):
                    dve.wait_ge(copied[h], 16 * (GROUPS // 2) * (n + 1))

            def from_table():
                mask = act[:].bitcast(U32).unsqueeze(2).to_broadcast([P, T, D])
                link(V.copy_predicated(xs[:], mask, G_jd))

            gathered(1)
            link(V.tensor_scalar(act[:], G_rec[:, :, D + 1], 0.0, None, ALU.is_gt))
            link(V.tensor_tensor(ta[:], G_rec[:, :, D], slotdeg[:, :, 0], ALU.subtract))
            link(V.tensor_tensor(ta[:], ta[:], act[:], ALU.mult))
            link(V.tensor_tensor(ta[:], ta[:], slotdeg[:, :, 0], ALU.add))
            link(V.tensor_copy(src_slot_i[:], ta[:]))
            link(V.tensor_copy(norm_d[:], deg[:]))
            link(V.tensor_scalar(dinv_d[:], deg[:], 1.0, None, ALU.add))
            link(V.tensor_scalar(scale_s[:], G_rec[:, :, D + 1], 1.0, None, ALU.max))
            link(V.tensor_scalar(dinv_s[:], G_rec[:, :, D + 1], 1.0, None, ALU.add))
            dve.sem_inc(act_in, 1)

            row0 = slotdeg[:, 0:1, 0]
            link(V.tensor_scalar(tb[:], slotdeg[:, :, 0], row0, -1.0, ALU.subtract, ALU.mult))
            link(V.tensor_scalar(tb[:], tb[:], float(T), float(1 << SLOT_BITS), ALU.add, ALU.mult))
            link(V.tensor_tensor(tb[:], tb[:], ta[:], ALU.add))
            link(V.tensor_tensor(tb[:], tb[:], act[:], ALU.mult))
            V.tensor_tensor_scan(ta[:], cont[:], act[:], 0.0, ALU.mult, ALU.add).then_inc(tail_ready, 1)
            dve.wait_ge(carry_ready, 3)
            link(V.scalar_tensor_tensor(out=lnv[:], in0=infirst[:], scalar=carry[:, 0:1], in1=ta[:],
                                        op0=ALU.mult, op1=ALU.add))
            dve.sem_inc(feeders_ready, 1)

            def greatest(dest, keys, count):
                for k in range(0, count, 8):
                    link(V.max(dest[:, k:k + 8], keys))
                    if k + 8 < count:
                        link(V.match_replace(keys, dest[:, k:k + 8], keys, 0.0))

            greatest(cand_key, tb[:], K1)
            link(V.tensor_copy(cand_i[:], cand_key[:]))
            V.tensor_scalar(cand_slot_i[:], cand_i[:], (1 << SLOT_BITS) - 1, None, ALU.bitwise_and).then_inc(cand_ready, 1)
            link(V.tensor_scalar(cand_i[:], cand_i[:], SLOT_BITS, None, ALU.logical_shift_right))
            link(V.tensor_copy(cand_col[:], cand_i[:]))
            link(V.tensor_reduce(fits[:, 0:1], act[:], AX.X, ALU.add))
            link(V.tensor_scalar(fits[:, 0:1], fits[:, 0:1], float(K1 - K2), None, ALU.subtract))
            dve.wait_ge(zeroed, 32)
            link(V.tensor_copy(xs[:], G_rec[:, :, 0:D]))
            dve.wait_ge(act_out, 1)
            link(V.tensor_tensor(tb[:], scale_s[:], act[:], ALU.mult))
            link(V.tensor_tensor(scale_s[:], tb[:], tb[:], ALU.mult))
            link(V.tensor_scalar(scale_s[:], scale_s[:], 0.9, None, ALU.mult))
            link(V.tensor_copy(erec[:, :, 0], scale_s[:]))
            link(V.tensor_copy(erec[:, :, 1], dstf[:]))
            link(V.tensor_copy(erec[:, :, 2], src_i[:]))
            link(V.tensor_copy(erec[:, :, 3], src_slot_i[:]))
            dve.sem_inc(erec_ready, 1)

            for u in range(2):
                dve.wait_ge(d_out[u], 16 * PAIRS)
            link(V.tensor_tensor(N_dj, turned(xs[:]), bd(tb[:]), ALU.mult))
            link(V.tensor_copy(bufA[:], bufN[:]))
            n_carry[0] = 3
            segment_sums()
            dve.sem_inc(table_ready, 1)

            dve.wait_ge(cand_landed, 16 * K1)
            link(V.scalar_tensor_tensor(out=cand_col[:], in0=cand_feeders[:], scalar=0.0, in1=cand_col[:],
                                        op0=ALU.is_gt, op1=ALU.mult))
            link(V.tensor_scalar(cand_key[:], cand_col[:], 0.0, None, ALU.is_gt))
            link(V.tensor_reduce(fits[:, 1:2], cand_key[:], AX.X, ALU.add))
            V.tensor_tensor(fits[:, 0:1], fits[:, 0:1], fits[:, 1:2], ALU.max).then_inc(tail_ready, 1)
            dve.wait_ge(carry_ready, 5)
            n_carry[0] = 5
            link(V.tensor_reduce(colmax[0:1, :], carry[0:1, 0:P], AX.X, ALU.max))
            V.tensor_copy(path_i[:], colmax[0:1, :]).then_inc(path_known, 1)
            dve.wait_ge(path_known, 1)
            path = dve.value_load(path_i[0:1, 0:1], min_val=0, max_val=T + 1)

            with dve.If(path < K2 + 1):
                s_done = [0]

                def note(ins):
                    s_done[0] += 1
                    ins.then_inc(s_vdone, 1)
                    dve.wait_ge(s_vdone, s_done[0])

                def sd(col):
                    return col.unsqueeze(1).to_broadcast([P, D, K2])

                def sj(col):
                    return col.unsqueeze(2).to_broadcast([P, K2, D])

                for k in range(0, K2, 8):
                    note(V.max(e_key[:, k:k + 8], cand_col[:]))
                    if k + 8 < K2:
                        note(V.match_replace(cand_col[:], e_key[:, k:k + 8], cand_col[:], 0.0))
                note(V.tensor_scalar(e_valid[:], e_key[:], 0.0, None, ALU.is_gt))
                note(V.tensor_scalar(e_own[:], e_key[:], -1.0, float(T), ALU.mult, ALU.add))
                note(V.tensor_tensor(e_own[:], e_own[:], e_valid[:], ALU.mult))
                note(V.tensor_scalar(e_own[:], e_own[:], row0, None, ALU.add))
                V.tensor_copy(e_own_i[:], e_own[:]).then_inc(s_own_ready, 1)
                note(V.tensor_copy(e_slot[:], e_slot_i[:]))
                note(V.tensor_scalar(e_t[:], e_slot[:], float(E), None, ALU.add))
                note(V.tensor_tensor(e_own[:], e_own[:], e_t[:], ALU.subtract))
                note(V.tensor_tensor(e_own[:], e_own[:], e_valid[:], ALU.mult))
                note(V.tensor_tensor(e_own[:], e_own[:], e_t[:], ALU.add))
                note(V.tensor_copy(e_msg_i[:], e_own[:]))
                note(V.memset(e_cont[:, 0:1], 0.0))
                dve.wait_ge(s_rec_landed, 16 * K2)
                note(V.tensor_copy(e_src_i[:], e_rec[:, :, 2]))
                V.tensor_copy(e_srcslot_i[:], e_rec[:, :, 3]).then_inc(s_src_ready, 1)
                note(V.tensor_tensor(e_fact[:], e_rec[:, :, 0], e_valid[:], ALU.mult))
                note(V.scalar_tensor_tensor(out=e_dst[:], in0=e_rec[:, :, 1], scalar=1.0, in1=e_valid[:],
                                            op0=ALU.add, op1=ALU.mult))
                note(V.tensor_reduce(e_mdst[:, 0:1], e_dst[:], AX.X, ALU.max))
                note(V.tensor_scalar(e_mdst[:, 1:2], e_mdst[:, 0:1], 0.0, None, ALU.is_gt))
                note(V.tensor_scalar(e_t[:, 0:1], e_mdst[:, 1:2], 1.0, row0, ALU.subtract, ALU.mult))
                note(V.tensor_tensor(e_mdst[:, 0:1], e_mdst[:, 0:1], e_t[:, 0:1], ALU.add))
                note(V.tensor_scalar(e_t[:], e_valid[:], -1.0, 1.0, ALU.mult, ALU.add))
                note(V.scalar_tensor_tensor(out=e_dst[:], in0=e_t[:], scalar=e_mdst[:, 0:1], in1=e_dst[:],
                                            op0=ALU.mult, op1=ALU.add))
                note(V.tensor_scalar(e_dst[:], e_dst[:], 1.0, None, ALU.subtract))
                V.tensor_scalar(diag[:], id_sb[:], e_dst[:, 0:1], None, ALU.mult).then_inc(s_tail, 1)
                note(V.tensor_tensor(e_cont[:, 1:K2], e_dst[:, 1:K2], e_dst[:, 0:K2 - 1], ALU.is_equal))
                note(V.tensor_scalar(e_infirst[:], e_dst[:], e_dst[:, 0:1], None, ALU.is_equal))
                note(V.tensor_copy(short_dj(cont2), sd(e_cont[:])))
                dve.wait_ge(s_carry, 1)
                note(V.scalar_tensor_tensor(out=link_e[:], in0=carry[:, 0:P], scalar=e_dst[:, K2 - 1:K2], in1=up_sb[:],
                                            op0=ALU.is_equal, op1=ALU.mult))
                note(V.tensor_scalar(e_last[:, 0:K2 - 1], e_cont[:, 1:K2], -1.0, 1.0, ALU.mult, ALU.add))
                note(V.tensor_reduce(e_last[:, K2 - 1:K2], link_e[:], AX.X, ALU.max))
                note(V.tensor_scalar(e_last[:, K2 - 1:K2], e_last[:, K2 - 1:K2], -1.0, 1.0, ALU.mult, ALU.add))
                note(V.tensor_scalar(e_last[:], e_last[:], e_mdst[:, 1:2], None, ALU.mult))
                note(V.tensor_scalar(e_q[:], e_slot[:], 1.0, None, ALU.add))
                note(V.tensor_scalar(e_t[:], e_slot[:], float(NR), None, ALU.add))
                note(V.tensor_tensor(e_dst[:], e_dst[:], e_t[:], ALU.subtract))
                note(V.tensor_tensor(e_dst[:], e_dst[:], e_last[:], ALU.mult))
                note(V.tensor_tensor(e_dst[:], e_dst[:], e_t[:], ALU.add))
                note(V.tensor_copy(e_put_i[:], e_dst[:]))
                dve.sem_inc(s_put_ready, 1)

                def s_sums(mark, carry_count):
                    V.tensor_tensor_scan(scan2, cont2, msg2, 0.0, ALU.mult, ALU.add).then_inc(s_tail, 1)
                    dve.wait_ge(s_carry, carry_count)
                    mark(V.tensor_tensor(short_dj(tmp2), sd(e_infirst[:]),
                                         carry[:, 0:D].unsqueeze(2).to_broadcast([P, D, K2]), ALU.mult))
                    mark(V.tensor_tensor(short_jd(sum2).rearrange("p j d -> p d j"), short_dj(scan2),
                                         short_dj(tmp2), ALU.add))
                    dve.sem_inc(s_table_ready, 1)

                dve.wait_ge(s_r_landed, 16 * K2)
                note(V.tensor_tensor(short_dj(msg2), turned(short_jd(r2)), sd(e_fact[:]), ALU.mult))
                note(V.tensor_scalar(short_dj(base2), short_dj(msg2), 0.1, None, ALU.mult))
                s_sums(note, 2)
                dve.wait_ge(s_q_landed, 16 * K2)
                note(V.scalar_tensor_tensor(out=e_fact[:], in0=e_t[:], scalar=0.0, in1=e_fact[:],
                                            op0=ALU.is_gt, op1=ALU.mult))
                note(V.tensor_scalar(e_t[:], e_t[:], 1.0, 0.0, ALU.subtract, ALU.max))
                note(V.tensor_copy(e_q_i[:], e_t[:]))
                dve.sem_inc(s_q_ready, 1)
                s_base, s_per = s_done[0], 4
                with dve.Fori(0, APPNP_STEPS - 3) as it:
                    marks = [0]

                    def mark(ins):
                        marks[0] += 1
                        ins.then_inc(s_vdone, 1)
                        dve.wait_ge(s_vdone, s_base + it * s_per + marks[0])

                    dve.wait_ge(s_landed, it * 16 * K2 + 16 * K2)
                    mark(V.tensor_tensor(short_dj(msg2), turned(short_jd(g2)), sd(e_fact[:]), ALU.mult))
                    mark(V.tensor_tensor(msg2, msg2, base2, ALU.add))
                    s_sums(mark, it + 3)
                    assert marks[0] == s_per
                s_done[0] += s_per * (APPNP_STEPS - 3)
                dve.wait_ge(s_landed, 16 * K2 * (APPNP_STEPS - 2))
                note(V.tensor_tensor(short_jd(msg2), short_jd(g2), sj(e_fact[:]), ALU.mult))
                note(V.tensor_tensor(short_jd(msg2), short_jd(msg2), short_dj(base2).rearrange("p d j -> p j d"), ALU.add))
                dve.sem_inc(s_msg_ready, 1)
                dve.wait_ge(s_msg_loaded, 16)
                note(V.scalar_tensor_tensor(out=A_dj, in0=N_dj, scalar=0.1, in1=turned(G_jd),
                                            op0=ALU.mult, op1=ALU.add))
                V.tensor_tensor_scan(bufB[:], contf[:].rearrange("p d j -> p (d j)"), bufA[:], 0.0,
                                     ALU.mult, ALU.add).then_inc(s_tail, 1)
                dve.wait_ge(s_carry, APPNP_STEPS)
                note(V.tensor_tensor(G_dj, bd(infirst[:]), carry[:, 0:D].unsqueeze(2).to_broadcast([P, D, T]), ALU.mult))
                note(V.tensor_tensor(A_jd.rearrange("p j d -> p d j"), B_dj, G_dj, ALU.add))
            with dve.Else():
                g_per, H = 4, GROUPS // 2
                dve.sem_inc(g_table_ready, 1)
                with dve.Fori(0, APPNP_STEPS - 1) as it:
                    def mark(k):
                        dve.wait_ge(g_vdone, it * g_per + k)

                    for h in range(2):
                        dve.wait_ge(g_copied[h], it * 16 * H + 16 * H)
                    V.tensor_tensor(A_dj, turned(G_jd), bd(scale_s[:]), ALU.mult).then_inc(g_vdone, 1)
                    mark(1)
                    V.scalar_tensor_tensor(out=bufA[:], in0=bufN[:], scalar=0.1, in1=bufA[:],
                                           op0=ALU.mult, op1=ALU.add).then_inc(g_vdone, 1)
                    mark(2)
                    V.tensor_tensor_scan(bufB[:], contf[:].rearrange("p d j -> p (d j)"), bufA[:], 0.0,
                                         ALU.mult, ALU.add).then_inc(g_tail, 1)
                    dve.wait_ge(g_carry, it + 1)
                    V.tensor_tensor(G_dj, bd(infirst[:]), carry[:, 0:D].unsqueeze(2).to_broadcast([P, D, T]),
                                    ALU.mult).then_inc(g_vdone, 1)
                    mark(3)
                    V.tensor_tensor(A_jd.rearrange("p j d -> p d j"), B_dj, G_dj, ALU.add).then_inc(g_vdone, 1)
                    mark(4)
                    dve.sem_inc(g_table_ready, 1)
            link(V.tensor_scalar(ta[:], norm_d[:], 0.9, None, ALU.mult))
            link(V.tensor_tensor(A_jd, A_jd, bj(ta[:]), ALU.mult))
            link(V.scalar_tensor_tensor(out=flat(xd[:]), in0=flat(xd[:]), scalar=1.1, in1=bufA[:],
                                        op0=ALU.mult, op1=ALU.add))
            layer_norm(xd[:], A_jd, table_ready)

            def leaf(t):
                link(V.tensor_scalar(flat(t), flat(t), 1.1, None, ALU.mult))

            def carried():
                n_carry[0] += 1
                dve.wait_ge(carry_ready, n_carry[0])

            leaf(xs[:])
            layer_norm(xs[:], A_jd)
            link(V.tensor_tensor(A_jd, xd[:], attn_sb[:, 1, :].unsqueeze(1).to_broadcast([P, T, D]), ALU.mult))
            link(V.tensor_reduce(td[:], A_jd, AX.X, ALU.add))
            gathered(2)
            from_table()
            link(V.tensor_tensor(A_jd, xs[:], attn_sb[:, 0, :].unsqueeze(1).to_broadcast([P, T, D]), ALU.mult))
            link(V.tensor_reduce(tb[:], A_jd, AX.X, ALU.add))
            link(V.tensor_scalar(ta[:], cont[:], -1.0, BIG, ALU.add, ALU.mult))
            link(V.tensor_tensor_scan(tc[:], ta[:], tb[:], -BIG, ALU.add, ALU.max))
            V.tensor_scalar(diag[:], id_sb[:], tc[:, T - 1:T], None, ALU.mult).then_inc(tail_ready, 1)
            carried()
            link(V.tensor_tensor(diag[:], link_b[:], carry[:, 0:P], ALU.mult))
            link(V.tensor_tensor(diag[:], diag[:], nolink[:], ALU.add))
            link(V.tensor_reduce(colmax[:], diag[:], AX.X, ALU.max))
            link(V.tensor_scalar(ta[:], infirst[:], -1.0, BIG, ALU.add, ALU.mult))
            link(V.scalar_tensor_tensor(out=tc[:], in0=ta[:], scalar=colmax[:, 0:1], in1=tc[:],
                                        op0=ALU.add, op1=ALU.max))
            for r, t in enumerate((tc, td)):
                link(V.tensor_tensor(both[:, r, :], t[:], last[:], ALU.mult))
            for r in range(2):
                link(V.tensor_tensor(ta[:], both[:, r, :], infirst[:], ALU.mult))
                link(V.tensor_reduce(first2[:, r:r + 1], ta[:], AX.X, ALU.add))
            dve.sem_inc(tail_ready, 1)
            carried()
            link(V.tensor_copy(init2[:], carry[:, 0:2]))
            for r, t in enumerate((tc, td)):
                link(V.tensor_tensor_scan(t[:, ::-1], contn[:, ::-1], both[:, r, ::-1], init2[:, r:r + 1],
                                          ALU.mult, ALU.add))
            for t in (tb, tc):
                link(V.tensor_tensor(t[:], t[:], td[:], ALU.add))
                link(V.scalar_tensor_tensor(out=t[:], in0=t[:], scalar=0.01, in1=t[:], op0=ALU.mult, op1=ALU.max))
            V.tensor_tensor(tb[:], tb[:], tc[:], ALU.subtract).then_inc(act_in, 1)
            dve.wait_ge(act_out, 2)
            V.tensor_tensor_scan(ta[:], cont[:], tb[:], 0.0, ALU.mult, ALU.add).then_inc(tail_ready, 1)
            carried()
            link(V.scalar_tensor_tensor(out=ta[:], in0=infirst[:], scalar=carry[:, 0:1], in1=ta[:],
                                        op0=ALU.mult, op1=ALU.add))
            link(V.tensor_scalar(ta[:], ta[:], 1.0 / BIG, None, ALU.max))
            link(V.reciprocal(ta[:], ta[:]))
            link(V.tensor_tensor(A_dj, turned(xs[:]), bd(tb[:]), ALU.mult))
            segment_sums()
            link(V.tensor_tensor(A_jd, A_jd, bj(ta[:]), ALU.mult))
            link(V.tensor_tensor(xd[:], xd[:], A_jd, ALU.add))
            layer_norm(xd[:], A_jd, table_ready)

            w000, w011, w110, w101 = (wigner_3j(*l).flat[0] for l in ((0, 0, 0), (0, 1, 1), (1, 1, 0), (1, 0, 1)))
            sph = bufB[:, 3 * MULT * T:(3 * MULT + 8) * T].rearrange("p (j s) -> p j s", s=8)
            rx, ry, rz = (relv[:, :, i] for i in range(3))
            link(V.tensor_tensor(ta[:], rx, rx, ALU.mult))
            link(V.tensor_tensor(tb[:], ry, ry, ALU.mult))
            link(V.tensor_tensor(ta[:], ta[:], tb[:], ALU.add))
            link(V.tensor_tensor(tb[:], rz, rz, ALU.mult))
            V.tensor_tensor(ta[:], ta[:], tb[:], ALU.add).then_inc(act_in, 1)
            dve.wait_ge(act_out, 3)
            link(V.tensor_tensor(relv[:], relv[:], ta[:].unsqueeze(2).to_broadcast([P, T, 3]), ALU.mult))
            for s, r in enumerate((ry, rz, rx)):
                link(V.tensor_scalar(sph[:, :, s], r, c1, None, ALU.mult))
            for s, a, b in ((3, rx, ry), (4, ry, rz), (6, rx, rz)):
                link(V.scalar_tensor_tensor(out=sph[:, :, s], in0=a, scalar=c2a, in1=b, op0=ALU.mult, op1=ALU.mult))
            link(V.tensor_tensor(tb[:], rz, rz, ALU.mult))
            link(V.tensor_scalar(sph[:, :, 5], tb[:], 3 * c2b, -c2b, ALU.mult, ALU.add))
            link(V.scalar_tensor_tensor(out=tb[:], in0=rx, scalar=c2c, in1=rx, op0=ALU.mult, op1=ALU.mult))
            link(V.scalar_tensor_tensor(out=tc[:], in0=ry, scalar=c2c, in1=ry, op0=ALU.mult, op1=ALU.mult))
            link(V.tensor_tensor(sph[:, :, 7], tb[:], tc[:], ALU.subtract))
            for t in hid:
                link(V.memset(t[HID:HID + 1, :], 1.0))
            dve.sem_inc(hid_free, 2)
            dve.sem_inc(conv_open, 1)
            layer_norm(xs[:], A_jd)
            gathered(3)
            from_table()
            vec = bufB[:, 0:3 * MULT * T].rearrange("p (j b v) -> p j b v", b=3, v=MULT)
            xs0 = xs[:, :, 0:MULT]
            xs1 = xs[:, :, MULT:D].rearrange("p j (v i) -> p j v i", i=3)
            link(V.tensor_scalar(vec[:, :, 0, :], xs0, norm[0] * w000 * y0, None, ALU.mult))
            link(V.tensor_scalar(vec[:, :, 2, :], xs0, norm[1] * w110, None, ALU.mult))
            prod = bufA[:, 0:3 * MULT * T].rearrange("p (j v i) -> p j v i", v=MULT, i=3)
            link(V.tensor_tensor(prod, xs1, sph[:, :, 0:3].unsqueeze(2).to_broadcast([P, T, MULT, 3]), ALU.mult))
            link(V.tensor_reduce(vec[:, :, 1, :], prod, AX.X, ALU.add))
            link(V.tensor_scalar(vec[:, :, 1, :], vec[:, :, 1, :], norm[0] * w011, None, ALU.mult))
            n_mk = 2 * 9
            mats = bufG[:, 0:n_mk * T].rearrange("p (j k o i) -> p j k o i", k=2, o=3, i=3)
            for k in (1, 2):
                w = wigner_3j(1, k, 1)
                for o in range(3):
                    for i in range(3):
                        terms = [(norm[1] * w[o, f, i], sph[:, :, (0 if k == 1 else 3) + f])
                                 for f in range(2 * k + 1) if abs(w[o, f, i]) > 1e-9]
                        m = mats[:, :, k - 1, o, i]
                        if not terms:
                            link(V.memset(m, 0.0))
                        for n, (c, y) in enumerate(terms):
                            link(V.tensor_scalar(m, y, c, None, ALU.mult) if n == 0 else
                                 V.scalar_tensor_tensor(out=m, in0=y, scalar=c, in1=m, op0=ALU.mult, op1=ALU.add))
            def rooms(buf, at, *shapes):
                for shape in shapes:
                    size = int(np.prod(shape))
                    assert at + size <= buf.shape[1]
                    yield buf[:, at:at + size]
                    at += size

            gk, gt, prod1, prod0 = rooms(bufG, n_mk * T, (C7, 3, MULT, 3), (6, C7, MULT, 3),
                                         (2, MULT, 3, 3 * MULT), (2, 3, MULT, MULT))
            q1, q0, q2 = rooms(bufN, 4 * C7 * P, (C7, MULT, 3), (C7, 3, MULT), (C7, MULT, 3))
            gk = gk.rearrange("p (c o v k) -> p c o v k", o=3, v=MULT, k=3)
            gk_flat = gk.rearrange("p c o v k -> p c o (v k)")
            gt = gt.rearrange("p (s c v i) -> p s c v i", c=C7, v=MULT, i=3)
            prod1 = prod1.rearrange("p (a u o w) -> p a u o w", a=2, u=MULT, o=3)
            prod0 = prod0.rearrange("p (a b u v) -> p a b u v", a=2, b=3, u=MULT)
            q1, q2 = (t.rearrange("p (c u o) -> p c u o", u=MULT, o=3) for t in (q1, q2))
            q0 = q0.rearrange("p (c b u) -> p c b u", b=3, u=MULT)
            dve.sem_inc(r_used, C7)
            PER = 7 + 6 + 4 * C7 + 4
            base = done[0]
            with dve.Fori(0, T // C7 // 2) as i:
                if True:
                    for s in range(2):
                        r = 2 * i + s
                        col = r * C7
                        cnt = [0]

                        def note(ins):
                            cnt[0] += 1
                            ins.then_inc(vdone, 1)

                        def settle():
                            dve.wait_ge(vdone, base + r * PER + cnt[0])

                        x1 = xs[:, bass.ds(col, C7), MULT:D].rearrange("p j (v i) -> p j v i", i=3)
                        mk = mats[:, bass.ds(col, C7)]
                        note(V.tensor_scalar(gk[:, :, :, :, 0].rearrange("p c o v -> p c v o"), x1,
                                             norm[1] * w101 * y0, None, ALU.mult))
                        for k in range(2):
                            for o in range(3):
                                note(V.tensor_tensor(gt[:, 3 * k + o], x1, mk[:, :, k, o, :].unsqueeze(2).to_broadcast(
                                    [P, C7, MULT, 3]), ALU.mult))
                        settle()
                        for k in range(2):
                            for o in range(3):
                                note(V.tensor_reduce(gk[:, :, o, :, 1 + k], gt[:, 3 * k + o], AX.X, ALU.add))
                        settle()
                        for c in range(C7):
                            dve.wait_ge(r_ready, col + c + 1)
                            rr = ps[:, c % 5, :]
                            note(V.tensor_tensor(
                                prod1[:, c % 2],
                                rr[:, 3 * MULT * MULT:R_DIM].rearrange("p (u w) -> p u w", u=MULT).unsqueeze(2).to_broadcast(
                                    [P, MULT, 3, 3 * MULT]),
                                gk_flat[:, c].unsqueeze(1).to_broadcast([P, MULT, 3, 3 * MULT]), ALU.mult))
                            note(V.tensor_tensor(
                                prod0[:, c % 2], rr[:, 0:3 * MULT * MULT].rearrange("p (b u v) -> p b u v", b=3, u=MULT),
                                vec[:, bass.ds(col + c, 1), :, :].rearrange("p a b v -> p (a b) v").unsqueeze(2).to_broadcast(
                                    [P, 3, MULT, MULT]), ALU.mult))
                            settle()
                            dve.sem_inc(r_used, 1)
                            note(V.tensor_reduce(q1[:, c], prod1[:, c % 2], AX.X, ALU.add))
                            note(V.tensor_reduce(q0[:, c], prod0[:, c % 2], AX.X, ALU.add))
                        settle()
                        out_c = A_dj[:, :, bass.ds(col, C7)]
                        note(V.tensor_tensor(out_c[:, 0:MULT, :].rearrange("p u c -> p c u"), q0[:, :, 0, :], q0[:, :, 1, :], ALU.add))
                        note(V.tensor_tensor(q2, q0[:, :, 2, :].unsqueeze(3).to_broadcast([P, C7, MULT, 3]),
                                             sph[:, bass.ds(col, C7), 0:3].unsqueeze(2).to_broadcast([P, C7, MULT, 3]), ALU.mult))
                        settle()
                        note(V.tensor_tensor(out_c[:, MULT:D, :].rearrange("p w c -> p c w"),
                                             q1.rearrange("p c u o -> p c (u o)"), q2.rearrange("p c u o -> p c (u o)"), ALU.add))
                        note(V.tensor_copy(colmax[:], zeroc[:]))
                        settle()
                        assert cnt[0] == PER, cnt[0]
            done[0] += PER * (T // C7)
            segment_sums()
            link(V.tensor_tensor(xd[:], xd[:], A_jd, ALU.add))
            layer_norm(xd[:], A_jd, table_ready)

            layer_norm(xs[:], A_jd)
            gathered(4)
            from_table()
            link(V.tensor_tensor(A_dj, turned(xs[:]), bd(dinv_s[:]), ALU.mult))
            segment_sums()
            link(V.tensor_tensor(G_jd, xd[:], bj(dinv_d[:]), ALU.mult))
            link(V.tensor_tensor(A_jd, A_jd, G_jd, ALU.add))
            link(V.tensor_tensor(A_jd, A_jd, bj(dinv_d[:]), ALU.mult))
            dve.sem_inc(m_x, 1)
            for m, dest in enumerate((bufN[:], flat(xs[:]))):
                with dve.Fori(0, T // 28) as i:
                    k = i + m * (T // 28)
                    dve.wait_ge(m_h, k + 1)
                    V.tensor_scalar(bufB[:, 14 * P:21 * P].rearrange("p (a b) -> p a b", a=2), ps[:, 4:6, 0:448],
                                    gb1_sb[:, 0:1], 0.0, ALU.add, ALU.max).then_inc(m_b, 1)
                    dve.wait_ge(m_o, k + 1)
                    dve.sem_inc(dve_tick, 1)
                    V.tensor_copy(dest[:, bass.ds(i * 28 * D, 28 * D)],
                                  ps[:, 0:2, :].rearrange("p a b -> p (a b)")[:, 0:28 * D]).then_inc(m_x, 1)
                if m == 0:
                    dve.wait_ge(m_x, 1 + T // 28)
                    dve.sem_inc(table_ready, 1)
            dve.wait_ge(m_x, 1 + 2 * (T // 28))
            gathered(5)
            from_table()
            link(V.tensor_tensor(A_dj, turned(xs[:]), bd(dinv_s[:]), ALU.mult))
            segment_sums()
            link(V.tensor_tensor(N_jd, N_jd, bj(dinv_d[:]), ALU.mult))
            link(V.tensor_tensor(A_jd, A_jd, N_jd, ALU.add))
            link(V.tensor_tensor(A_jd, A_jd, bj(dinv_d[:]), ALU.mult))
            link(V.tensor_tensor(A_jd, A_jd, gb2_row[:].unsqueeze(1).to_broadcast([P, T, D]), ALU.add))
            link(V.tensor_tensor(xd[:], xd[:], A_jd, ALU.add))
            layer_norm(xd[:], A_jd, state_ready)


def kernel(x, src, dst, edge_attr_3, edge_weight, L1_gnn_attn_w, L2_gnn_w1, L2_gnn_b1, L2_gnn_w2, L2_gnn_b2,
           L3_gnn_W1, L3_gnn_b1, L3_gnn_W2, L3_gnn_b2):
    import concourse.bacc as bacc
    from concourse.bass_utils import run_bass_kernel_spmd

    x, src, dst, rel, weight = (np.asarray(a) for a in (x, src, dst, edge_attr_3, edge_weight))
    n, e = x.shape[0], src.shape[0]
    T, E, NR = sizes(n, e)
    assert n < NR

    def padded(a, rows, value):
        return np.concatenate([a, np.full((rows - a.shape[0],) + a.shape[1:], value, a.dtype)])

    ends = padded(padded(dst, E, n), E + 1, n + 1)
    side = np.arange(P) // D
    same = (side[:, None] == side[None, :]).astype(np.float32) / D
    eye = np.eye(P, dtype=np.float32)
    arrays = {
        "x": padded(x, NR + 2 * ROWS * NQ, 0), "src": padded(src, E, 0),
        "dst": ends[:E], "dst_next": ends[1:], "dst_first": ends[:E:T],
        "rel": padded(rel, E, 1), "wt_cols": padded(padded(weight, E, 0).reshape(P, T).T, T + 2 * C7, 0),
        "attn_w": L1_gnn_attn_w, "w1": L2_gnn_w1, "b1": L2_gnn_b1, "w2": L2_gnn_w2, "b2": L2_gnn_b2,
        "gcn_w1": L3_gnn_W1, "gcn_b1": L3_gnn_b1, "gcn_w2": L3_gnn_W2, "gcn_b2": L3_gnn_b2,
        "ident": eye, "center": eye - same, "average": same,
        "upper": np.triu(np.ones((P, P), np.float32), 1),
    }
    arrays = {f"in_{k}": np.ascontiguousarray(v) for k, v in arrays.items()}
    nc = bacc.Bacc("TRN2", target_bir_lowering=False, num_devices=1)
    args = [nc.dram_tensor(k, v.shape, mybir.dt.from_np(v.dtype), kind="ExternalInput").ap()
            for k, v in arrays.items()]
    out = nc.dram_tensor("out", (NR + E, D), F32, kind="ExternalOutput").ap()
    gnn_kernel(nc, *args, out, e)
    return run_bass_kernel_spmd(nc, [arrays], core_ids=[0]).results[0]["out"][:n]
```

```python
from contextlib import ExitStack
from math import factorial, pi, sqrt

import numpy as np

import concourse.bass as bass
from concourse import mybir

F32 = mybir.dt.float32
BF16 = mybir.dt.bfloat16
I32 = mybir.dt.int32
U32 = mybir.dt.uint32
ALU = mybir.AluOpType
ACT = mybir.ActivationFunctionType
AX = mybir.AxisListType

P = 128
D = 32
HID = 64
U = 14
EPS = 1e-5
BIG = 1e30
IDLE = (14, 6, 63, 35)
PARTS = 5
APPNP_STEPS = 10
RW = D + 2
NB = 32
NQ = P // D
C7 = 7
MULT = 8
DVE_GROUPS = 6
K1 = 64
K2 = 24
SLOT_BITS = 15


def sizes(n_nodes, n_edges):
    t = -(-n_edges // (P * 2 * U)) * 2 * U
    chunk = P * NB
    return t, P * t, -(-n_nodes // chunk) * chunk


def _cg(j1, j2, j3, m1, m2, m3):
    if m1 + m2 != m3:
        return 0.0
    f = factorial
    pre = sqrt((2 * j3 + 1) * f(j3 + j1 - j2) * f(j3 - j1 + j2) * f(j1 + j2 - j3) / f(j1 + j2 + j3 + 1))
    pre *= sqrt(f(j3 + m3) * f(j3 - m3) * f(j1 - m1) * f(j1 + m1) * f(j2 - m2) * f(j2 + m2))
    s = 0.0
    for k in range(max(0, j2 - j3 - m1, j1 - j3 + m2), min(j1 + j2 - j3, j1 - m1, j2 + m2) + 1):
        s += (-1) ** k / (f(k) * f(j1 + j2 - j3 - k) * f(j1 - m1 - k) * f(j2 + m2 - k)
                          * f(j3 - j2 + m1 + k) * f(j3 - j1 - m2 + k))
    return pre * s


def _real_basis(l):
    a = np.zeros((2 * l + 1, 2 * l + 1), dtype=complex)
    a[l, l] = 1.0
    for m in range(1, l + 1):
        a[l + m, l + m] = (-1) ** m / sqrt(2)
        a[l + m, l - m] = 1.0 / sqrt(2)
        a[l - m, l - m] = 1j / sqrt(2)
        a[l - m, l + m] = -1j * (-1) ** m / sqrt(2)
    return a


def wigner_3j(l1, l2, l3):
    w = np.zeros((2 * l1 + 1, 2 * l2 + 1, 2 * l3 + 1), dtype=complex)
    for m1 in range(-l1, l1 + 1):
        for m2 in range(-l2, l2 + 1):
            if abs(m1 + m2) <= l3:
                w[m1 + l1, m2 + l2, l3 - m1 - m2] = ((-1) ** (l1 - l2 + m1 + m2) / sqrt(2 * l3 + 1)
                                                    * _cg(l1, l2, l3, m1, m2, m1 + m2))
    r = np.einsum("abc,ma,nb,oc->mno", w, _real_basis(l1).conj(), _real_basis(l2).conj(), _real_basis(l3).conj())
    top = r.flat[int(np.argmax(np.abs(r)))]
    return np.real(r / (top / abs(top)))


def gnn_kernel(nc, x, src, dst, dst_next, dst_first, rel, wt_cols, attn_w, w1, b1, w2, b2,
               gcn_w1, gcn_b1, gcn_w2, gcn_b2, ident, upper, out, n_edges):
    E = src.shape[0]
    T = E // P
    NR = out.shape[0] - E
    ROUNDS = NR // (P * NB)
    assert ROUNDS % 2 == 1 and ROUNDS >= 7
    GROUPS = T // U
    NK = NR // P // 8
    R_DIM = w2.shape[1]
    E2 = P * K2
    assert E < 1 << SLOT_BITS and T < 1 << (24 - SLOT_BITS)

    norm = [sqrt(4 * pi) * sqrt(2 * lo + 1) / sqrt(sum(MULT * (2 * min(lo, li) + 1) for li in (0, 1)))
            for lo in (0, 1)]
    y0 = 0.5 / sqrt(pi)
    c1 = sqrt(3.0 / (4.0 * pi))
    c2a, c2b, c2c = 0.5 * sqrt(15.0 / pi), 0.25 * sqrt(5.0 / pi), 0.25 * sqrt(15.0 / pi)

    rec = nc.dram_tensor("node_records", (NR + E, RW), F32).ap()
    rec_pairs = rec.rearrange("n (a b) -> (n a) b", b=2)
    feeders = nc.dram_tensor("feeders", (E, 1), F32).ap()
    edge_records = nc.dram_tensor("edge_records", (E, 4), F32).ap()
    short_slots = nc.dram_tensor("short_slots", (NR + E2, 1), F32).ap()
    short_table = nc.dram_tensor("short_table", (E2, D), F32).ap()
    messages = nc.dram_tensor("messages", (E + E2, D), F32).ap()
    landing = nc.dram_tensor("landing", (E + P * K1, D), F32).ap()
    tables = [nc.dram_tensor(f"edge_table_{i}", (E, D), F32).ap() for i in range(5)]

    with ExitStack() as ctx:
        def sb(name, shape, dt=F32):
            return ctx.enter_context(nc.sbuf_tensor(name, shape, dt))

        def sem(name):
            return ctx.enter_context(nc.semaphore(name))

        ps = ctx.enter_context(nc.psum_tensor("ps", [P, 8, 512], F32))
        carry = ps[:, 7, :]

        xd = sb("xd", [P, T, D])
        xs = sb("xs", [P, T, D])
        bufA = sb("bufA", [P, T * D])
        bufB = sb("bufB", [P, T * D])
        bufN = sb("bufN", [P, T * D])
        bufG = sb("bufG", [P, T * RW])
        contf = sb("contf", [P, D, T], BF16)
        A_jd = bufA[:].rearrange("p (j d) -> p j d", d=D)
        A_dj = bufA[:].rearrange("p (d j) -> p d j", d=D)
        B_dj = bufB[:].rearrange("p (d j) -> p d j", d=D)
        N_jd = bufN[:].rearrange("p (j d) -> p j d", d=D)
        N_dj = bufN[:].rearrange("p (d j) -> p d j", d=D)
        G_jd = bufG[:, 0:T * D].rearrange("p (j d) -> p j d", d=D)
        G_dj = bufG[:, 0:T * D].rearrange("p (d j) -> p d j", d=D)
        G_rec = bufG[:].rearrange("p (j r) -> p j r", r=RW)

        ring_idx = sb("ring_idx", [P, 2, U], I32)
        ring_rows = sb("ring_rows", [P, 2, U * RW])

        src_i = sb("src_i", [P, T], I32)
        dst_i = sb("dst_i", [P, T], I32)
        next_i = sb("next_i", [P, T], I32)
        slot_i = sb("slot_i", [P, T], I32)
        node_i = sb("node_i", [P, T], I32)
        pair_i = sb("pair_i", [P, T], I32)
        src_slot_i = sb("src_slot_i", [P, T], I32)
        dstf = sb("dstf", [P, T])
        cont = sb("cont", [P, T])
        contn = sb("contn", [P, T])
        last = sb("last", [P, T])
        infirst = sb("infirst", [P, T])
        deg = sb("deg", [P, T])
        slotdeg = sb("slotdeg", [P, T, 2])
        act = sb("act", [P, T])
        scale_s = sb("scale_s", [P, T])
        norm_d = sb("norm_d", [P, T])
        dinv_s = sb("dinv_s", [P, T])
        dinv_d = sb("dinv_d", [P, T])
        relv = sb("relv", [P, T, 3])
        ta = sb("ta", [P, T])
        tb = sb("tb", [P, T])
        per_edge4 = sb("per_edge4", [P, 4 * T])
        erec = per_edge4[:].rearrange("p (j r) -> p j r", r=4)
        both = per_edge4[:, 0:2 * T].rearrange("p (r j) -> p r j", r=2)
        tc = per_edge4[:, 2 * T:3 * T]
        td = per_edge4[:, 3 * T:4 * T]
        lnv = sb("lnv", [P, T])
        lnw = sb("lnw", [P, T])
        leaf = sb("leaf", [P, T])
        first2 = sb("first2", [P, 2])
        init2 = sb("init2", [P, 2])
        colmax = sb("colmax", [P, 1])
        diag = sb("diag", [P, P])
        epsc = sb("epsc", [P, 1])
        zeroc = sb("zeroc", [P, 1])

        cand_key = sb("cand_key", [P, K1])
        cand_i = sb("cand_i", [P, K1], I32)
        cand_slot_i = sb("cand_slot_i", [P, K1], I32)
        cand_own_i = sb("cand_own_i", [P, K1], I32)
        cand_col = sb("cand_col", [P, K1])
        cand_feeders = sb("cand_feeders", [P, K1])
        fits = sb("fits", [P, 2])
        path_i = sb("path_i", [1, 1], I32)
        (e_key, e_valid, e_own, e_dst, e_cont, e_infirst, e_last, e_slot, e_q, e_fact, e_t) = (
            sb(n, [P, K2]) for n in ("e_key", "e_valid", "e_own", "e_dst", "e_cont", "e_infirst", "e_last",
                                     "e_slot", "e_q", "e_fact", "e_t"))
        (e_own_i, e_src_i, e_srcslot_i, e_put_i, e_q_i, e_msg_i, e_slot_i) = (
            sb(n, [P, K2], I32) for n in ("e_own_i", "e_src_i", "e_srcslot_i", "e_put_i", "e_q_i", "e_msg_i",
                                          "e_slot_i"))
        e_rec = sb("e_rec", [P, K2, 4])
        e_mdst = sb("e_mdst", [P, 2])
        link_e = sb("link_e", [P, P])
        SW = K2 * D
        g2, r2, base2, msg2, scan2, sum2, cont2, tmp2 = (bufB[:, k * SW:(k + 1) * SW] for k in range(8))
        short_jd = lambda t: t.rearrange("p (j d) -> p j d", d=D)
        short_dj = lambda t: t.rearrange("p (d j) -> p d j", d=D)

        id_sb = sb("id_sb", [P, P])
        up_sb = sb("up_sb", [P, P])
        ones = sb("ones", [P, T])
        dfirst = sb("dfirst", [P, P], I32)
        link_f = sb("link_f", [P, P])
        link_b = sb("link_b", [P, P])
        nolink = sb("nolink", [P, P])
        attn_sb = sb("attn_sb", [P, 2, D])
        w1_sb = sb("w1_sb", [HID, 1])
        w2_sb = sb("w2_sb", [HID + 1, R_DIM])
        b1_sb = sb("b1_sb", [HID, 1])
        gw1_sb = sb("gw1_sb", [P, NQ * HID])
        gw2_sb = sb("gw2_sb", [P, 2, P])
        gb1_sb = sb("gb1_sb", [P, 1])
        gw2c_sb = sb("gw2c_sb", [P, 2, P])
        gb2c_row = sb("gb2c_row", [P, NQ, D])
        gb2c_col = sb("gb2c_col", [P, 1])
        stats = sb("stats", [P, 3, NB])
        eps3c = sb("eps3c", [P, 1])
        gb2_row = sb("gb2_row", [P, D])
        wrow = [bufN[0:HID, i * C7 * P:(i + 1) * C7 * P] for i in range(2)]
        hid = [bufN[0:HID + 1, (2 + i) * C7 * P:(3 + i) * C7 * P] for i in range(2)]

        w000, w011, w110, w101 = (wigner_3j(*l).flat[0] for l in ((0, 0, 0), (0, 1, 1), (1, 1, 0), (1, 0, 1)))
        n_mk = 2 * 9
        sph = bufB[:, 0:8 * T].rearrange("p (j s) -> p j s", s=8)
        mats = bufB[:, 8 * T:(8 + n_mk) * T].rearrange("p (j k o i) -> p j k o i", k=2, o=3, i=3)
        ring_flat = ring_rows[:].rearrange("p h c -> p (h c)")
        gk_p = [t.rearrange("p (c o v k) -> p c o v k", o=3, v=MULT, k=3)
                for t in (ring_flat[:, 0:C7 * 9 * MULT], sb("gk_p1", [P, C7 * 9 * MULT])[:])]
        vec_p = [t.rearrange("p (j b v) -> p j b v", b=3, v=MULT)
                 for t in (sb("vec_p0", [P, U * 3 * MULT])[:], per_edge4[:, 3 * MULT * MULT:3 * MULT * MULT + U * 3 * MULT])]
        factors = sb("factors", [P, 4])
        from_g_p = ring_flat[:, C7 * 9 * MULT:C7 * 9 * MULT + U * D].rearrange("p (j d) -> p j d", d=D)
        gt_p = bufG[:, 0:6 * C7 * MULT * 3].rearrange("p (n i) -> p n i", i=3)
        gs_p = bufG[:, 18 * C7 * MULT:24 * C7 * MULT]
        prod_p = bufG[:, 24 * C7 * MULT:24 * C7 * MULT + U * MULT * 3].rearrange("p (j v i) -> p j v i", v=MULT, i=3)
        assert 24 * C7 * MULT + U * MULT * 3 <= 4 * U * D and 4 <= DVE_GROUPS

        DW = NB * D
        blocks = [b[:, k * DW:(k + 1) * DW] for b in (bufB, bufN) for k in range(T * D // DW)]
        dx, dy, do = blocks[0:2], blocks[2:4], blocks[4:6]
        dsq, dyt_0, dh0, dh1, dsq4, dst_t = blocks[6:12]
        dyt = [dyt_0, bufA[:, T * D - DW:T * D]]
        by_node = lambda t: t.rearrange("p (n d) -> p n d", d=D)

        rec_sb = [b[:, 0:NK * RW].rearrange("p (n r) -> p n r", r=RW)
                  for b in (bufA[:], bufG[:])]
        rec_x = [bufG[:, NK * RW:NK * (RW + D)], xs[:].rearrange("p j d -> p (j d)")[:, 0:NK * D]]

        loaded = sem("loaded")
        rec_copied = sem("rec_copied")
        dst_loaded = sem("dst_loaded")
        xd_landed = sem("xd_landed")
        attr_loaded = sem("attr_loaded")
        consts_ready = sem("consts_ready")
        rec_in = [sem(f"rec_in{i}") for i in range(2)]
        rec_out = [sem(f"rec_out{i}") for i in range(2)]
        staged = [sem(f"staged{i}") for i in range(2)]
        landed = [sem(f"landed{i}") for i in range(2)]
        copied = [sem(f"copied{i}") for i in range(2)]
        out_staged = [sem(f"out_staged{i}") for i in range(2)]
        scattered = [sem(f"scattered{i}") for i in range(2)]
        pool_tick = sem("pool_tick")
        iota_done = sem("iota_done")
        slots_ready = sem("slots_ready")
        table_ready = sem("table_ready")
        table_stored = sem("table_stored")
        state_ready = sem("state_ready")
        vdone = sem("vdone")
        zeroed = sem("zeroed")
        zeros_ready = sem("zeros_ready")
        feeders_ready = sem("feeders_ready")
        feeders_stored = sem("feeders_stored")
        cand_ready = sem("cand_ready")
        cand_own_ready = sem("cand_own_ready")
        rows_landed = [sem(f"rows_landed{k}") for k in range(2)]
        rows_put = sem("rows_put")
        rows_loaded = [sem(f"rows_loaded{c}") for c in range(PARTS)]
        cand_landed = sem("cand_landed")
        erec_ready = sem("erec_ready")
        erec_stored = sem("erec_stored")
        path_known = sem("path_known")
        s_own_ready, s_src_ready, s_put_ready, s_q_ready, s_msg_ready = (
            sem(n) for n in ("s_own_ready", "s_src_ready", "s_put_ready", "s_q_ready", "s_msg_ready"))
        s_msg_loaded = [sem(f"s_msg_loaded{c}") for c in range(PARTS)]
        s_rec_landed, s_r_landed, s_put, s_q_landed, s_landed, s_msg_put = (
            sem(n) for n in ("s_rec_landed", "s_r_landed", "s_put", "s_q_landed", "s_landed", "s_msg_put"))
        s_table_ready, s_stored, s_tail, s_carry, s_vdone = (
            sem(n) for n in ("s_table_ready", "s_stored", "s_tail", "s_carry", "s_vdone"))
        g_staged = [sem(f"g_staged{i}") for i in range(2)]
        g_landed = [sem(f"g_landed{i}") for i in range(2)]
        g_copied = [sem(f"g_copied{i}") for i in range(2)]
        g_table_ready, g_stored, g_tail, g_carry, g_vdone = (
            sem(n) for n in ("g_table_ready", "g_stored", "g_tail", "g_carry", "g_vdone"))
        carries_added = sem("carries_added")
        tail_ready = sem("tail_ready")
        carry_ready = sem("carry_ready")
        centered = sem("centered")
        scaled = sem("scaled")
        parts_ready = sem("parts_ready")
        squared = sem("squared")
        var_ready = sem("var_ready")
        rstd_ready = sem("rstd_ready")
        act_in = sem("act_in")
        act_out = sem("act_out")
        adone = sem("adone")
        sp_tick = sem("sp_tick")
        dve_tick = sem("dve_tick")
        d_in = [sem(f"d_in{u}") for u in range(2)]
        d_out = [sem(f"d_out{u}") for u in range(2)]
        (d_cent, d_sq, d_var, d_rstd, d_y, d_turned, d_yt, d_hid, d_relu_a, d_relu_v, d_sum, d_sq4, d_var4, d_rstd4,
         d_done, d_vdone, d_ln, d_ln4, d_st, d_back) = (sem(n) for n in (
             "d_cent", "d_sq", "d_var", "d_rstd", "d_y", "d_turned", "d_yt", "d_hid", "d_relu_a", "d_relu_v", "d_sum",
             "d_sq4", "d_var4", "d_rstd4", "d_done", "d_vdone", "d_ln", "d_ln4", "d_st", "d_back"))
        m_t = sem("m_t")
        m_in = sem("m_in")
        m_x = sem("m_x")
        m_h = sem("m_h")
        m_a = sem("m_a")
        m_yt = sem("m_yt")
        m_cols = sem("m_cols")
        m_b = sem("m_b")
        m_o = sem("m_o")
        conv_open = sem("conv_open")
        wrow_in = [sem(f"wrow_in{i}") for i in range(2)]
        hid_ready = sem("hid_ready")
        hid_free = sem("hid_free")
        r_ready = sem("r_ready")
        r_used = sem("r_used")
        conv_groups = sem("conv_groups")
        p_ready = sem("p_ready")
        p_used = sem("p_used")
        pdone = sem("pdone")

        LOADS = 14

        def part(c, width=1):
            n = -(-GROUPS // PARTS) * U
            return slice(c * n * width, min((c + 1) * n, T) * width)

        def dense_rounds(engine, step):
            for i in range(3):
                step(i, i % 2, i == 0, 2)
            with engine.Fori(0, (ROUNDS - 5) // 2) as g:
                for u in (1, 0):
                    step(2 * g + 4 - u, u, False, 2)
            step(ROUNDS - 2, 1, False, 1)
            step(ROUNDS - 1, 0, False, 0)

        def dense_stored(engine):
            for u in range(2):
                engine.wait_ge(d_out[u], 16 * ((ROUNDS + 1 - u) // 2))

        block = ctx.enter_context(nc.Block())

        @block.sync
        def _(sp):
            e_view = lambda a: a.rearrange("(p j) -> p j", p=P)
            pairs = [(src_i[:], e_view(src)), (next_i[:], e_view(dst_next)),
                     (dfirst[:], dst_first.partition_broadcast(P)),
                     (up_sb[:], upper), (id_sb[:], ident),
                     (relv[:], rel.rearrange("(p j) c -> p j c", p=P)),
                     (attn_sb[:].rearrange("p a d -> p (a d)"), attn_w.partition_broadcast(P)),
                     (w1_sb[:], w1.rearrange("a h -> h a")),
                     (w2_sb[0:HID, :], w2), (w2_sb[HID:HID + 1, :], b2.unsqueeze(0)),
                     (b1_sb[:], b1.unsqueeze(1)),
                     (gb2_row[:], gcn_b2.partition_broadcast(P))]
            for i in range(2):
                pairs.append((gb1_sb[HID * i:HID * (i + 1), :], gcn_b1.unsqueeze(1)))
            sp.dma_start(dst_i[:], e_view(dst)).then_inc(dst_loaded, 16)
            for a, b in pairs:
                sp.dma_start(a, b).then_inc(loaded, 16)
            sp.wait_ge(consts_ready, 1)
            for q in range(NQ):
                sp.dma_start(gw1_sb[D * q:D * (q + 1), HID * q:HID * (q + 1)], gcn_w1).then_inc(attr_loaded, 16)
                a, r = q // 2, q % 2
                sp.dma_start(gw2_sb[HID * r:HID * (r + 1), a, D * q:D * (q + 1)], gcn_w2).then_inc(attr_loaded, 16)

            def gather(first, idx, dest, width, staged=staged, landed=landed, copied=copied):
                def stage(c, h):
                    sp.dma_start(ring_idx[:, h, :], idx[:, bass.ds(c, U)]).then_inc(staged[h], 16)

                def take(g, h):
                    sp.wait_ge(landed[h], 16 * U * (first + g + 1))
                    sp.dma_start(dest[:, bass.ds((2 * g + h) * U * width, U * width)],
                                 ring_rows[:, h, 0:U * width]).then_inc(copied[h], 16)
                    sp.wait_ge(copied[h], 16 * (first + g + 1))
                    sp.sem_inc(sp_tick, 1)

                for h in range(2):
                    stage(h * U, h)
                with sp.Fori(0, GROUPS // 2 - 1) as g:
                    for h in range(2):
                        take(g, h)
                        stage((2 * g + 2 + h) * U, h)
                for h in range(2):
                    take(GROUPS // 2 - 1, h)

            def scatter(first, idx, rows, width):
                def stage(c, h):
                    sp.dma_start(ring_idx[:, h, :], idx[:, bass.ds(c, U)]).then_inc(out_staged[h], 16)
                    sp.dma_start(ring_rows[:, h, 0:U * width],
                                 rows[:, bass.ds(c * width, U * width)]).then_inc(out_staged[h], 16)

                for h in range(2):
                    stage(h * U, h)
                with sp.Fori(0, GROUPS // 2 - 1) as g:
                    for h in range(2):
                        sp.wait_ge(scattered[h], 16 * U * (first + g + 1))
                        sp.sem_inc(sp_tick, 1)
                        stage((2 * g + 2 + h) * U, h)
                for h in range(2):
                    sp.wait_ge(scattered[h], 16 * U * (first + GROUPS // 2))

            x_rec = x[0:NR, :].rearrange("(k p n) d -> k p (n d)", k=8, p=P)
            rec_rows = rec[0:NR, :].rearrange("(k p n) r -> k p (n r)", k=8, p=P)
            for s in range(2):
                sp.dma_start(rec_x[s], x_rec[s]).then_inc(rec_in[s], 16)
            for k in range(8):
                s = k % 2
                sp.wait_ge(rec_copied, k + 1)
                sp.dma_start(rec_rows[k], rec_sb[s][:].rearrange("p n r -> p (n r)")).then_inc(rec_out[s], 16)
                if k + 2 < 8:
                    sp.dma_start(rec_x[s], x_rec[k + 2]).then_inc(rec_in[s], 16)
            H = GROUPS // 2
            sp.wait_ge(loaded, 16 * LOADS)
            sp.wait_ge(slots_ready, 1)
            for i in range(2):
                sp.wait_ge(rec_out[i], 16 * 4)
            scatter(0, pair_i, slotdeg[:].rearrange("p j c -> p (j c)"), 2)
            gather(0, src_i, bufG, RW)
            sp.wait_ge(feeders_ready, 1)
            sp.dma_start(feeders.rearrange("(p j) a -> p (j a)", p=P), lnv[:]).then_inc(feeders_stored, 16)
            sp.wait_ge(erec_ready, 1)
            sp.dma_start(edge_records.rearrange("(p j) r -> p (j r)", p=P), per_edge4[:]).then_inc(erec_stored, 16)
            table_0 = tables[0].rearrange("(p j) d -> p (j d)", p=P)
            sp.wait_ge(table_ready, 1)
            sp.dma_start(table_0, bufA[:]).then_inc(table_stored, 16)
            sp.wait_ge(path_known, 1)
            path = sp.value_load(path_i[0:1, 0:1], min_val=0, max_val=T + 1)
            with sp.If(path < K2 + 1):
                with sp.Fori(0, APPNP_STEPS - 2) as it:
                    sp.wait_ge(s_table_ready, it + 1)
                    sp.dma_start(short_table.rearrange("(p j) d -> p (j d)", p=P), sum2).then_inc(s_stored, 16)
                sp.wait_ge(s_msg_put, 16 * K2)
                by_edge = messages[0:E, :].rearrange("(p j) d -> p (j d)", p=P)
                for c in range(PARTS):
                    sp.dma_start(bufG[:, part(c, D)], by_edge[:, part(c, D)]).then_inc(s_msg_loaded[c], 16)
            with sp.Else():
                sp.wait_ge(table_stored, 16)
                with sp.Fori(0, APPNP_STEPS - 1) as it:
                    sp.wait_ge(g_table_ready, it + 1)
                    sp.dma_start(table_0, bufA[:]).then_inc(g_stored, 16)
                    sp.wait_ge(g_stored, 16 * (it + 1))
                    gather(it * H, src_slot_i, bufG, D, g_staged, g_landed, g_copied)
            def layer_rows(l):
                with sp.If(path < K2 + 1):
                    sp.wait_ge(rows_put, 16 * K1 * (l + 1))
                    by_edge = landing[0:E, :].rearrange("(p j) d -> p (j d)", p=P)
                    for c in range(PARTS):
                        sp.dma_start(bufG[:, part(c, D)], by_edge[:, part(c, D)]).then_inc(rows_loaded[c], 16)
                with sp.Else():
                    gather((APPNP_STEPS - 1 + l) * H, src_slot_i, bufG, D, g_staged, g_landed, g_copied)

            xd_flat = xd[:].rearrange("p j d -> p (j d)")
            for k in range(3):
                table = tables[1 + k].rearrange("(p j) d -> p (j d)", p=P)
                for c in range(PARTS):
                    sp.wait_ge(parts_ready, PARTS * k + c + 1)
                    sp.dma_start(table[:, part(c, D)], xd_flat[:, part(c, D)]).then_inc(table_stored, 16)
                sp.wait_ge(table_stored, 16 * (1 + PARTS * (k + 1)))
                if k == 1:
                    gather(H, src_slot_i, bufG, D)
                else:
                    layer_rows(k // 2)
            for c in range(PARTS):
                sp.wait_ge(m_x, 1 + -(-part(c).stop // 28))
                sp.dma_start(tables[4].rearrange("(p j) d -> p (j d)", p=P)[:, part(c, D)], bufN[:, part(c, D)]).then_inc(
                    table_stored, 16)
            sp.wait_ge(table_stored, 16 * (1 + PARTS * 4))
            layer_rows(2)
            dense_stored(sp)
            for g in range(GROUPS):
                h = g % 2
                if g >= 2:
                    sp.wait_ge(scattered[h], 16 * U * (H + g // 2))
                sp.wait_ge(state_ready, (g * U) // part(0).stop + 1)
                sp.dma_start(ring_idx[:, h, :], node_i[:, g * U:(g + 1) * U]).then_inc(out_staged[h], 16)
                sp.dma_start(ring_rows[:, h, 0:U * D], xd_flat[:, g * U * D:(g + 1) * U * D]).then_inc(out_staged[h], 16)
            for h in range(2):
                sp.wait_ge(scattered[h], 16 * U * (H + GROUPS // 2))

        @block.gpsimd
        def _(pool):
            nc.gpsimd.iota(slot_i[:], pattern=[[1, T]], base=0, channel_multiplier=T).then_inc(iota_done, 1)
            nc.gpsimd.iota(e_slot_i[:], pattern=[[1, K2]], base=0, channel_multiplier=K2).then_inc(iota_done, 1)
            nc.gpsimd.iota(cand_own_i[:], pattern=[[1, K1]], base=E, channel_multiplier=K1).then_inc(iota_done, 1)
            H = GROUPS // 2
            for k, value in enumerate((norm[0] * w000 * y0, norm[1] * w110, norm[0] * w011, norm[1] * w101 * y0)):
                nc.gpsimd.memset(factors[:, k:k + 1], value).then_inc(iota_done, 1)
            pool.wait_ge(iota_done, 7)

            def gather(first, table, width, staged=staged, landed=landed):
                with pool.Fori(0, H) as g:
                    for h in range(2):
                        pool.wait_ge(staged[h], 16 * (first + g + 1))
                        pool.sem_inc(pool_tick, 1)
                        for c in range(U):
                            pool.indirect_dma_start(
                                ring_rows[:, h, c * width:(c + 1) * width], None, table,
                                bass.IndirectOffsetOnAxis(ap=ring_idx[:, h, c:c + 1], axis=0),
                            ).then_inc(landed[h], 16)

            def scatter(first, table, width):
                with pool.Fori(0, H) as g:
                    for h in range(2):
                        pool.wait_ge(out_staged[h], 32 * (first + g + 1))
                        pool.sem_inc(pool_tick, 1)
                        for c in range(U):
                            pool.indirect_dma_start(
                                table, bass.IndirectOffsetOnAxis(ap=ring_idx[:, h, c:c + 1], axis=0),
                                ring_rows[:, h, c * width:(c + 1) * width], None,
                            ).then_inc(scattered[h], 16)

            def conv_vectors():
                N = nc.gpsimd
                for h in range(2):
                    pool.wait_ge(copied[h], 16 * 2 * H)
                pool.wait_ge(conv_groups, 4)
                per = 8 + 2 * 10

                def factor(k, shape):
                    return factors[:, k:k + 1].unsqueeze(2).to_broadcast(shape)

                with pool.Fori(0, (GROUPS - DVE_GROUPS) // 2) as i:
                    for h in range(2):
                        group = 2 * i + h
                        col = group * U + DVE_GROUPS * U
                        cnt = [0]

                        def note(ins):
                            cnt[0] += 1
                            ins.then_inc(pdone, 1)

                        def settle():
                            pool.wait_ge(pdone, group * per + cnt[0])
                            pool.sem_inc(pool_tick, 1)

                        cols = bass.ds(col, U)
                        xg = xs[:, cols, :]
                        vec = vec_p[h]
                        pool.wait_ge(p_used, 2 * group + 1)
                        pool.sem_inc(pool_tick, 1)
                        note(N.tensor_tensor(from_g_p, G_jd[:, cols, :], act[:, cols].unsqueeze(2).to_broadcast([P, U, D]),
                                             ALU.mult))
                        settle()
                        note(N.tensor_tensor(xg, xg, from_g_p, ALU.add))
                        settle()
                        for b, k in ((0, 0), (2, 1)):
                            note(N.tensor_tensor(vec[:, :, b, :], xg[:, :, 0:MULT], factor(k, [P, U, MULT]), ALU.mult))
                        note(N.tensor_tensor(prod_p, xg[:, :, MULT:D].rearrange("p j (v i) -> p j v i", i=3),
                                             sph[:, cols, 0:3].unsqueeze(2).to_broadcast([P, U, MULT, 3]), ALU.mult))
                        settle()
                        note(N.tensor_tensor(vec[:, :, 1, :], prod_p[:, :, :, 0], prod_p[:, :, :, 1], ALU.add))
                        settle()
                        note(N.tensor_tensor(vec[:, :, 1, :], vec[:, :, 1, :], prod_p[:, :, :, 2], ALU.add))
                        settle()
                        note(N.tensor_tensor(vec[:, :, 1, :], vec[:, :, 1, :], factor(2, [P, U, MULT]), ALU.mult))
                        settle()
                        for s in range(2):
                            half = bass.ds(col + s * C7, C7)
                            x1 = xs[:, half, MULT:D].rearrange("p j (v i) -> p j v i", i=3)
                            mk = mats[:, half]
                            gk = gk_p[s]
                            if s == 1:
                                pool.wait_ge(p_used, 2 * group + 2)
                                pool.sem_inc(pool_tick, 1)
                            n = C7 * MULT
                            note(N.tensor_tensor(gk[:, :, :, :, 0].rearrange("p c o v -> p c v o"), x1,
                                                 factors[:, 3:4].unsqueeze(2).unsqueeze(3).to_broadcast([P, C7, MULT, 3]),
                                                 ALU.mult))
                            for k in range(2):
                                for o in range(3):
                                    at = (3 * k + o) * n
                                    note(N.tensor_tensor(gt_p[:, at:at + n, :].rearrange("p (c v) i -> p c v i", v=MULT), x1,
                                                         mk[:, :, k, o, :].unsqueeze(2).to_broadcast([P, C7, MULT, 3]), ALU.mult))
                            settle()
                            note(N.tensor_tensor(gs_p, gt_p[:, :, 0], gt_p[:, :, 1], ALU.add))
                            settle()
                            for k in range(2):
                                at = slice(3 * k * n, 3 * (k + 1) * n)
                                note(N.tensor_tensor(gk[:, :, :, :, 1 + k].rearrange("p c o v -> p o c v"),
                                                     gs_p[:, at].rearrange("p (o c v) -> p o c v", o=3, v=MULT),
                                                     gt_p[:, at, 2].rearrange("p (o c v) -> p o c v", o=3, v=MULT), ALU.add))
                            settle()
                            pool.sem_inc(p_ready, 1)
                        assert cnt[0] == per, cnt[0]

            column = [0]

            def own_rows(count):
                for c in range(column[0], min(column[0] + count, T)):
                    pool.indirect_dma_start(xd[:, c, :], None, x[0:NR, :],
                                            bass.IndirectOffsetOnAxis(ap=dst_i[:, c:c + 1], axis=0)).then_inc(xd_landed, 16)
                column[0] = min(column[0] + count, T)

            pool.wait_ge(dst_loaded, 16)
            own_rows(T - sum(IDLE))
            scatter(0, rec_pairs, 2)
            gather(0, rec[0:NR, :], RW)
            own_rows(IDLE[0])

            def fetch(dest, table, idx, cols, landed, start=0):
                for c in range(start, cols):
                    pool.indirect_dma_start(dest(c), None, table,
                                            bass.IndirectOffsetOnAxis(ap=idx[:, c:c + 1], axis=0)).then_inc(landed, 16)

            def put(table, rows, idx, done, cols=K2, start=0):
                for c in range(start, cols):
                    pool.indirect_dma_start(table, bass.IndirectOffsetOnAxis(ap=idx[:, c:c + 1], axis=0),
                                            rows(c), None).then_inc(done, 16)

            pool.wait_ge(cand_ready, 1)
            pool.wait_ge(feeders_stored, 16)
            fetch(lambda c: cand_feeders[:, c:c + 1], feeders, cand_slot_i, K1, cand_landed)
            own_rows(IDLE[1])
            rest = column[0]
            pool.wait_ge(path_known, 1)
            path = pool.value_load(path_i[0:1, 0:1], min_val=0, max_val=T + 1)
            with pool.If(path < K2 + 1):
                pool.wait_ge(s_own_ready, 1)
                pool.wait_ge(erec_stored, 16)
                fetch(lambda c: e_rec[:, c, :], edge_records, e_own_i, K2, s_rec_landed)
                pool.wait_ge(s_src_ready, 1)
                pool.wait_ge(table_stored, 16)
                fetch(lambda c: r2[:, c * D:(c + 1) * D], tables[0], e_srcslot_i, K2, s_r_landed)
                pool.wait_ge(s_put_ready, 1)
                put(short_slots, lambda c: e_q[:, c:c + 1], e_put_i, s_put)
                pool.wait_ge(s_put, 16 * K2)
                fetch(lambda c: e_t[:, c:c + 1], short_slots[0:NR, :], e_src_i, K2, s_q_landed)
                pool.wait_ge(s_q_ready, 1)
                for it in range(APPNP_STEPS - 2):
                    pool.wait_ge(s_stored, 16 * (it + 1))
                    fetch(lambda c: g2[:, c * D:(c + 1) * D], short_table, e_q_i, K2, s_landed)
                    if it < APPNP_STEPS - 3:
                        own_rows(IDLE[2] // (APPNP_STEPS - 3))
                pool.wait_ge(s_msg_ready, 1)
                put(messages, lambda c: msg2[:, c * D:(c + 1) * D], e_msg_i, s_msg_put)
                own_rows(T)
            with pool.Else():
                column[0] = rest
                own_rows(T)
                with pool.Fori(0, APPNP_STEPS - 1) as it:
                    gather(it * H, tables[0], D, g_staged, g_landed)
            def layer_rows(l, table, stored):
                with pool.If(path < K2 + 1):
                    pool.wait_ge(table_stored, 16 * stored)
                    pool.wait_ge(cand_own_ready, 1)
                    for k in range(2):
                        fetch(lambda c: bufG[:, c * D:(c + 1) * D], table, cand_slot_i, (k + 1) * K1 // 2,
                              rows_landed[k], k * K1 // 2)
                    for k in range(2):
                        pool.wait_ge(rows_landed[k], 16 * K1 // 2 * (l + 1))
                        put(landing, lambda c: bufG[:, c * D:(c + 1) * D], cand_own_i, rows_put, (k + 1) * K1 // 2,
                            k * K1 // 2)
                with pool.Else():
                    gather((APPNP_STEPS - 1 + l) * H, table, D, g_staged, g_landed)

            layer_rows(0, tables[1], 1 + PARTS)
            gather(H, tables[2], D)
            conv_vectors()
            layer_rows(1, tables[3], 1 + 3 * PARTS)
            layer_rows(2, tables[4], 1 + 4 * PARTS)
            scatter(H, out, D)
            for h in range(2):
                pool.wait_ge(scattered[h], 16 * U * 2 * H)

        @block.tensor
        def _(pe):
            mm = nc.tensor.matmul
            pe.wait_ge(loaded, 16 * LOADS)
            pe.wait_ge(tail_ready, 1)
            nc.tensor.transpose(carry[:, 0:P], link_f[:], id_sb[:]).then_inc(carry_ready, 1)
            pe.wait_ge(tail_ready, 2)
            mm(carry[:, 0:1], link_f[:], deg[:, T - 1:T], start=True, stop=True).then_inc(carry_ready, 1)
            n = [2]

            pe.wait_ge(attr_loaded, 16 * 2 * NQ)

            def dense_turn(j, u):
                pe.wait_ge(d_y, j + 1)
                for b in range(DW // P):
                    ins = nc.tensor.transpose(ps[:, b // 4, (b % 4) * P:(b % 4 + 1) * P],
                                              dy[u][:, b * P:(b + 1) * P], id_sb[:])
                ins.then_inc(d_turned, 1)

            def dense_graph(i, u, first, ahead):
                pe.wait_ge(d_yt, i + 1)
                for a in range(2):
                    for half in range(2):
                        ins = mm(ps[:, 2 + 2 * a + half, :], gw1_sb[:, a * P:(a + 1) * P],
                                 dyt[u][:, half * 512:(half + 1) * 512], start=True, stop=True)
                ins.then_inc(d_hid, 1)
                if ahead:
                    dense_turn(i + 1, 1 - u)
                pe.wait_ge(d_relu_a, i + 1)
                pe.wait_ge(d_relu_v, i + 1)
                if not first:
                    pe.wait_ge(d_done, i)
                for half in range(2):
                    cols = slice(half * 512, (half + 1) * 512)
                    mm(ps[:, 6 + half, :], id_sb[:], dyt[u][:, cols], start=True, stop=False)
                    mm(ps[:, 6 + half, :], gw2c_sb[:, 0, :], dh0[:, cols], start=False, stop=False)
                    ins = mm(ps[:, 6 + half, :], gw2c_sb[:, 1, :], dh1[:, cols], start=False, stop=True)
                ins.then_inc(d_sum, 1)
                pe.wait_ge(d_st, i + 1)
                for b in range(DW // P):
                    ins = nc.tensor.transpose(ps[:, 6 + b // 4, (b % 4) * P:(b % 4 + 1) * P],
                                              dst_t[:, b * P:(b + 1) * P], id_sb[:])
                ins.then_inc(d_back, 1)

            dense_turn(0, 0)
            dense_rounds(pe, dense_graph)

            def hand_on(width, lhs=link_f, tail=None):
                pe.wait_ge(tail_ready, n[0] + 1)
                mm(carry[:, 0:width], lhs[:], tail, start=True, stop=True).then_inc(carry_ready, 1)
                n[0] += 1

            tails = B_dj[:, :, T - 1]
            hand_on(1, tail=ta[:, T - 1:T])
            hand_on(D, tail=tails)
            pe.wait_ge(tail_ready, n[0] + 1)
            mm(carry[0:1, 0:P], fits[:, 0:1], id_sb[:], start=True, stop=True).then_inc(carry_ready, 1)
            n[0] += 1
            pe.wait_ge(path_known, 1)
            path = pe.value_load(path_i[0:1, 0:1], min_val=0, max_val=T + 1)
            with pe.If(path < K2 + 1):
                pe.wait_ge(s_tail, 1)
                mm(carry[:, 0:P], ones[:, 0:P], diag[:], start=True, stop=True).then_inc(s_carry, 1)
                with pe.Fori(0, APPNP_STEPS - 2) as it:
                    pe.wait_ge(s_tail, it + 2)
                    mm(carry[:, 0:D], link_e[:], short_dj(scan2)[:, :, K2 - 1], start=True, stop=True).then_inc(s_carry, 1)
                pe.wait_ge(s_tail, APPNP_STEPS)
                mm(carry[:, 0:D], link_f[:], tails, start=True, stop=True).then_inc(s_carry, 1)
            with pe.Else():
                with pe.Fori(0, APPNP_STEPS - 1) as it:
                    pe.wait_ge(g_tail, it + 1)
                    mm(carry[:, 0:D], link_f[:], tails, start=True, stop=True).then_inc(g_carry, 1)
            pe.wait_ge(tail_ready, n[0] + 1)
            mm(carry[:, 0:P], ones[:, 0:P], diag[:], start=True, stop=True).then_inc(carry_ready, 1)
            n[0] += 1
            hand_on(2, link_b, first2[:])
            hand_on(1, tail=ta[:, T - 1:T])
            hand_on(D, tail=tails)

            with pe.Fori(0, T // C7 // 2) as i:
                for s in range(2):
                    k = 2 * i + s
                    pe.wait_ge(hid_ready, k + 1)
                    for c in range(C7):
                        before = c - 5 + C7 if c >= 5 else c + 5 if c < 2 else c
                        pe.wait_ge(r_used, k * C7 + before + 1)
                        mm(ps[:, c % 5, 0:R_DIM], hid[s][:, c * P:(c + 1) * P], w2_sb[:],
                           start=True, stop=True).then_inc(r_ready, 1)
                    pe.wait_ge(r_ready, (k + 1) * C7)
                    pe.sem_inc(hid_free, 1)
            hand_on(D, tail=tails)
            hand_on(D, tail=tails)

            def turn(k):
                pe.wait_ge(m_in, k + 1)
                for c in range(7):
                    ins = nc.tensor.transpose(ps[:, c // 4, (c % 4) * P:(c % 4 + 1) * P],
                                              bufB[:, (21 + c) * P:(22 + c) * P], id_sb[:])
                ins.then_inc(m_t, 1)

            def hidden(k):
                pe.wait_ge(m_yt, k + 1)
                for s in range(2):
                    for half in range(2):
                        ins = mm(ps[:, 2 + 2 * s + half, 0:448], gw1_sb[:, s * P:(s + 1) * P],
                                 bufB[:, half * 448:(half + 1) * 448], start=True, stop=True)
                ins.then_inc(m_h, 1)

            def product(k):
                pe.wait_ge(m_a, k + 1)
                pe.wait_ge(m_b, k + 1)
                pe.wait_ge(m_x, k + 1)
                for c in range(7):
                    for s in range(2):
                        hs = bufB[:, (1 + s) * 7 * P + c * P:(1 + s) * 7 * P + (c + 1) * P]
                        ins = mm(ps[:, 6 + c // 4, (c % 4) * P + s * HID:(c % 4) * P + (s + 1) * HID], hs,
                                 gw2_sb[:, s, s * HID:(s + 1) * HID], start=True, stop=True)
                ins.then_inc(m_o, 1)

            M = T // 28
            for m in range(2):
                turn(m * M)
                with pe.Fori(0, M - 1) as i:
                    k = i + m * M
                    hidden(k)
                    turn(k + 1)
                    product(k)
                hidden((m + 1) * M - 1)
                product((m + 1) * M - 1)
            hand_on(D, tail=tails)

        @block.scalar
        def _(act_e):
            A = nc.scalar.activation
            nc.scalar.preload_act_table_set("natural_log_exp_and_others")
            x_c = x.rearrange("(k p n) d -> k p (n d)", p=P, n=NB)
            o_c = out[0:NR, :].rearrange("(k p n) d -> k p (n d)", p=P, n=NB)
            for u in range(2):
                act_e.dma_start(dx[u], x_c[u]).then_inc(d_in[u], 16)
            act_e.wait_ge(consts_ready, 1)
            for k in range(8):
                s = k % 2
                act_e.wait_ge(rec_in[s], 16 * (k // 2 + 1))
                if k >= 2:
                    act_e.wait_ge(rec_out[s], 16 * (k // 2))
                A(rec_sb[s][:, :, 0:D], rec_x[s].rearrange("p (n d) -> p n d", d=D), ACT.Copy).then_inc(rec_copied, 1)
            act_e.wait_ge(loaded, 16 * LOADS)
            flat2 = lambda t: t.rearrange("p a b -> p (a b)")
            chunk = lambda v, k: v[bass.ds(k, 1)].rearrange("a p c -> (a p) c")

            def dense_square(j, u):
                act_e.wait_ge(d_cent, j + 1)
                A(dsq, dy[u], ACT.Square).then_inc(d_sq, 1)
                act_e.dma_start(dx[u], chunk(x_c, j + 2)).then_inc(d_in[u], 16)

            def dense_rstd(n, k, var, ln, rstd, scale, eps):
                act_e.wait_ge(var, n + 1)
                A(stats[:, k, :], stats[:, k, :], ACT.Ln, bias=eps[:, 0:1], scale=scale).then_inc(ln, 1)
                act_e.wait_ge(ln, n + 1)
                A(stats[:, k, :], stats[:, k, :], ACT.Exp, bias=zeroc[:, 0:1], scale=-0.5).then_inc(rstd, 1)

            three = (1 + EPS + EPS * EPS) / D

            def dense_copy(j, u):
                act_e.wait_ge(d_turned, j + 1)
                A(dyt[u], flat2(ps[:, 0:2, :]), ACT.Copy).then_inc(d_yt, 1)

            def dense_act(i, u, first, ahead):
                act_e.wait_ge(d_hid, i + 1)
                A(dh0, flat2(ps[:, 2:4, :]), ACT.Relu, bias=gb1_sb[:, 0:1]).then_inc(d_relu_a, 1)
                if ahead:
                    dense_copy(i + 1, 1 - u)
                if not first:
                    act_e.wait_ge(d_done, i)
                    act_e.dma_start(chunk(o_c, i - 1), do[1 - u]).then_inc(d_out[1 - u], 16)
                if ahead == 2:
                    dense_square(i + 2, u)
                    dense_rstd(i + 2, 1, d_var, d_ln, d_rstd, three, eps3c)
                act_e.wait_ge(d_sum, i + 1)
                A(dst_t, flat2(ps[:, 6:8, :]), ACT.Identity, bias=gb2c_col[:, 0:1]).then_inc(d_st, 1)
                act_e.wait_ge(d_back, i + 1)
                A(dsq4, flat2(ps[:, 6:8, :]), ACT.Square).then_inc(d_sq4, 1)
                dense_rstd(i, 2, d_var4, d_ln4, d_rstd4, 1.0 / D, epsc)

            for j in range(2):
                dense_square(j, j)
                dense_rstd(j, 1, d_var, d_ln, d_rstd, three, eps3c)
            dense_copy(0, 0)
            dense_rounds(act_e, dense_act)
            act_e.wait_ge(d_done, ROUNDS)
            act_e.dma_start(o_c[ROUNDS - 1], do[0]).then_inc(d_out[0], 16)
            for u in range(2):
                act_e.wait_ge(d_in[u], 16 * ((ROUNDS + 1 - u) // 2 + 1))

            act_e.wait_ge(zeros_ready, 1)
            zeros = xs[:].rearrange("p j d -> p (j d)")
            act_e.dma_start(messages[0:E, :].rearrange("(p j) d -> p (j d)", p=P), zeros).then_inc(zeroed, 16)
            act_e.dma_start(landing[0:E, :].rearrange("(p j) d -> p (j d)", p=P), zeros).then_inc(zeroed, 16)
            act_e.dma_start(short_slots[0:NR, :].rearrange("(p n) a -> p (n a)", p=P), zeros[:, 0:NR // P]).then_inc(zeroed, 16)

            k_in = [0]

            def ln_exp(t):
                A(t, t, ACT.Ln, bias=zeroc[:, 0:1]).then_inc(adone, 1)
                k_in[0] += 1
                act_e.wait_ge(adone, k_in[0])
                return A(t, t, ACT.Exp, bias=zeroc[:, 0:1], scale=-0.5)

            norms = [0]

            def layer_norm(y, tmp, in_turn=False):
                n = PARTS * norms[0]
                norms[0] += 1

                def square(c):
                    act_e.wait_ge(centered, n + c + 1)
                    A(tmp[:, part(c, D)], y[:, part(c, D)], ACT.Square).then_inc(squared, 1)

                def rstd(c):
                    v = lnw[:, part(c)]
                    act_e.wait_ge(var_ready, n + c + 1)
                    A(v, v, ACT.Ln, bias=epsc[:, 0:1], scale=1.0 / D).then_inc(adone, 1)
                    k_in[0] += 1
                    act_e.wait_ge(adone, k_in[0])
                    A(v, v, ACT.Exp, bias=zeroc[:, 0:1], scale=-0.5).then_inc(rstd_ready, 1)

                if in_turn:
                    for c in range(PARTS):
                        square(c)
                        rstd(c)
                    return
                square(0)
                for c in range(1, PARTS):
                    square(c)
                    rstd(c - 1)
                rstd(PARTS - 1)

            act_e.wait_ge(act_in, 1)
            for t in (norm_d, dinv_d, scale_s, dinv_s):
                ins = ln_exp(t[:])
            ins.then_inc(act_out, 1)
            flat = lambda t: t.rearrange("p j d -> p (j d)")
            layer_norm(flat(xd[:]), bufA[:])
            layer_norm(flat(xs[:]), bufA[:])
            layer_norm(bufN[:], bufA[:])
            act_e.wait_ge(act_in, 2)
            A(tb[:], tb[:], ACT.Exp, bias=zeroc[:, 0:1]).then_inc(act_out, 1)
            layer_norm(flat(xd[:]), bufA[:])
            wt_rows = wt_cols.rearrange("(k c) p -> k (c p)", c=C7)
            act_e.wait_ge(act_in, 3)
            ln_exp(ta[:]).then_inc(act_out, 1)
            act_e.wait_ge(conv_open, 1)
            for s in range(2):
                act_e.dma_start(wrow[s], wt_rows[s].partition_broadcast(HID)).then_inc(wrow_in[s], 16)
            with act_e.Fori(0, T // C7 // 2) as i:
                for s in range(2):
                    act_e.wait_ge(wrow_in[s], 16 * (i + 1))
                    act_e.wait_ge(hid_free, 2 * i + s + 1)
                    A(hid[s][0:HID, :], wrow[s], ACT.Relu, bias=b1_sb[:, 0:1], scale=w1_sb[:, 0:1]).then_inc(hid_ready, 1)
                    act_e.wait_ge(hid_ready, 2 * i + s + 1)
                    act_e.dma_start(wrow[s], wt_rows[bass.ds(2 * i + s + 2, 1)].rearrange("a c -> (a c)")
                                    .partition_broadcast(HID)).then_inc(wrow_in[s], 16)
            for s in range(2):
                act_e.wait_ge(wrow_in[s], 16 * (T // C7 // 2 + 1))
            layer_norm(flat(xd[:]), bufA[:])
            layer_norm(flat(xs[:]), bufA[:])
            M = T // 28
            def bring(inp, col):
                A(bufB[:, 21 * P:28 * P], inp[:, col], ACT.Copy).then_inc(m_in, 1)

            def turned_out(k):
                act_e.wait_ge(m_t, k + 1)
                A(bufB[:, 0:7 * P], flat2(ps[:, 0:2, :])[:, 0:7 * P], ACT.Copy).then_inc(m_yt, 1)

            def relu(k):
                act_e.wait_ge(m_h, k + 1)
                A(bufB[:, 7 * P:14 * P].rearrange("p (a b) -> p a b", a=2), ps[:, 2:4, 0:448], ACT.Relu,
                  bias=gb1_sb[:, 0:1]).then_inc(m_a, 1)

            act_e.wait_ge(m_x, 1)
            for m, inp in enumerate((bufA[:], flat(xs[:]))):
                act_e.wait_ge(m_cols, 1)
                bring(inp, slice(0, 7 * P))
                with act_e.Fori(0, M - 1) as i:
                    turned_out(i + m * M)
                    act_e.wait_ge(m_cols, i + 2)
                    bring(inp, bass.ds(i * 7 * P + 7 * P, 7 * P))
                    relu(i + m * M)
                turned_out((m + 1) * M - 1)
                relu((m + 1) * M - 1)
            layer_norm(flat(xd[:]), bufA[:], in_turn=True)

        @block.vector
        def _(dve):
            V = nc.vector
            done = [0]

            def link(ins):
                done[0] += 1
                ins.then_inc(vdone, 1)
                dve.wait_ge(vdone, done[0])

            def bj(col):
                return col.unsqueeze(2).to_broadcast([P, T, D])

            def bd(col):
                return col.unsqueeze(1).to_broadcast([P, D, T])

            turned = lambda t: t.rearrange("p j d -> p d j")
            flat = lambda t: t.rearrange("p j d -> p (j d)")

            V.memset(gw1_sb[:], 0.0).then_inc(vdone, 1)
            V.memset(gw2_sb[:], 0.0).then_inc(vdone, 1)
            V.memset(ones[:], 1.0).then_inc(vdone, 1)
            V.memset(epsc[:], EPS).then_inc(vdone, 1)
            V.memset(eps3c[:], EPS ** 3 / 1.21).then_inc(vdone, 1)
            V.memset(zeroc[:], 0.0).then_inc(vdone, 1)
            V.memset(cont[:, 0:1], 0.0).then_inc(vdone, 1)
            V.memset(rec_sb[0][:, :, D:RW], 0.0).then_inc(vdone, 1)
            V.memset(rec_sb[1][:, :, D:RW], 0.0).then_inc(vdone, 1)
            done[0] = 9
            dve.wait_ge(vdone, 9)
            dve.sem_inc(consts_ready, 1)


            dve.wait_ge(loaded, 16 * LOADS)
            dve.wait_ge(dst_loaded, 16)
            link(V.tensor_copy(dstf[:], dst_i[:]))
            link(V.tensor_copy(ta[:], next_i[:]))
            link(V.tensor_tensor(cont[:, 1:T], dstf[:, 1:T], dstf[:, 0:T - 1], ALU.is_equal))
            link(V.tensor_tensor(contn[:], dstf[:], ta[:], ALU.is_equal))
            link(V.tensor_scalar(last[:], contn[:], -1.0, 1.0, ALU.mult, ALU.add))
            link(V.tensor_scalar(infirst[:], dstf[:], dstf[:, 0:1], None, ALU.is_equal))
            link(V.tensor_copy(diag[:], dfirst[:]))
            V.scalar_tensor_tensor(out=link_f[:], in0=diag[:], scalar=dstf[:, T - 1:T], in1=up_sb[:],
                                   op0=ALU.is_equal, op1=ALU.mult).then_inc(tail_ready, 1)
            dve.wait_ge(carry_ready, 1)
            link(V.tensor_copy(link_b[:], carry[:, 0:P]))
            link(V.tensor_scalar(nolink[:], link_b[:], -1.0, BIG, ALU.add, ALU.mult))
            V.tensor_tensor_scan(deg[:], cont[:], ones[:], 0.0, ALU.mult, ALU.add).then_inc(tail_ready, 1)
            dve.wait_ge(carry_ready, 2)
            link(V.scalar_tensor_tensor(out=deg[:], in0=infirst[:], scalar=carry[:, 0:1], in1=deg[:],
                                        op0=ALU.mult, op1=ALU.add))
            dve.wait_ge(iota_done, 7)
            link(V.tensor_copy(slotdeg[:, :, 0], slot_i[:]))
            link(V.tensor_copy(slotdeg[:, :, 1], deg[:]))
            link(V.tensor_scalar(ta[:], slotdeg[:, :, 0], float(NR), None, ALU.add))
            link(V.tensor_tensor(tb[:], dstf[:], ta[:], ALU.subtract))
            link(V.tensor_tensor(tb[:], tb[:], last[:], ALU.mult))
            link(V.tensor_tensor(tb[:], tb[:], ta[:], ALU.add))
            link(V.tensor_copy(node_i[:], tb[:]))
            link(V.tensor_scalar(tb[:], tb[:], float(RW // 2), float(D // 2), ALU.mult, ALU.add))
            V.tensor_copy(pair_i[:], tb[:]).then_inc(slots_ready, 1)
            link(V.tensor_copy(contf[:], bd(cont[:])))

            dve.wait_ge(attr_loaded, 16 * 2 * NQ)
            for a in range(2):
                w = gw2_sb[:, a, :].rearrange("p (g d) -> p g d", d=D)
                st = stats[:, 0, 0:NQ]
                link(V.tensor_reduce(st, w, AX.X, ALU.add))
                link(V.tensor_scalar(st, st, 1.0 / D, None, ALU.mult))
                link(V.tensor_tensor(gw2c_sb[:, a, :].rearrange("p (g d) -> p g d", d=D), w,
                                     st.unsqueeze(2).to_broadcast([P, NQ, D]), ALU.subtract))
            link(V.tensor_reduce(colmax[:], gb2_row[:], AX.X, ALU.add))
            link(V.tensor_scalar(colmax[:], colmax[:], 1.0 / D, None, ALU.mult))
            for q in range(NQ):
                link(V.tensor_scalar(gb2c_row[:, q, :], gb2_row[:], colmax[:, 0:1], None, ALU.subtract))
            link(V.tensor_tensor(gb2c_row[:], gb2c_row[:], id_sb[:].rearrange("p (q d) -> p q d", d=D), ALU.mult))
            link(V.tensor_reduce(gb2c_col[:], gb2c_row[:].rearrange("p q d -> p (q d)"), AX.X, ALU.add))

            over = lambda k: stats[:, k, :].unsqueeze(2).to_broadcast([P, NB, D])

            def dense_center(j, u):
                dve.wait_ge(d_in[u], 16 * (j // 2 + 1) if isinstance(j, int) else 8 * (j - u) + 16)
                V.tensor_reduce(stats[:, 0, :], by_node(dx[u]), AX.X, ALU.add).then_inc(d_vdone, 1)
                dve.wait_ge(d_vdone, 2 * j + 1)
                V.tensor_scalar(stats[:, 0, :], stats[:, 0, :], 1.0 / D, None, ALU.mult).then_inc(d_vdone, 1)
                dve.wait_ge(d_vdone, 2 * j + 2)
                V.tensor_tensor(by_node(dy[u]), by_node(dx[u]), over(0), ALU.subtract).then_inc(d_cent, 1)

            def dense_variance(j):
                dve.wait_ge(d_sq, j + 1)
                V.tensor_reduce(stats[:, 1, :], by_node(dsq), AX.X, ALU.add).then_inc(d_var, 1)

            def dense_scale(j, u):
                dve.wait_ge(d_rstd, j + 1)
                V.tensor_tensor(by_node(dy[u]), by_node(dy[u]), over(1), ALU.mult).then_inc(d_y, 1)

            def dense_dve(i, u, first, ahead):
                dve.wait_ge(d_hid, i + 1)
                V.tensor_scalar(dh1, ps[:, 4:6, :].rearrange("p a b -> p (a b)"), gb1_sb[:, 0:1], 0.0,
                                ALU.add, ALU.max).then_inc(d_relu_v, 1)
                if ahead == 2:
                    dense_center(i + 2, u)
                    dense_variance(i + 2)
                    dense_scale(i + 2, u)
                dve.wait_ge(d_sq4, i + 1)
                V.tensor_reduce(stats[:, 2, :], by_node(dsq4), AX.X, ALU.add).then_inc(d_var4, 1)
                dve.wait_ge(d_rstd4, i + 1)
                if isinstance(i, int):
                    if i >= 2:
                        dve.wait_ge(d_out[u], 16 * (i // 2))
                else:
                    dve.wait_ge(d_out[u], 8 * (i - u))
                V.tensor_tensor(by_node(do[u]), ps[:, 6:8, :].rearrange("p a (n d) -> p (a n) d", d=D), over(2),
                                ALU.mult).then_inc(d_done, 1)

            for j in range(2):
                dense_center(j, j)
                dense_variance(j)
                dense_scale(j, j)
            dense_rounds(dve, dense_dve)
            dve.wait_ge(rec_copied, 8)
            V.memset(xs[:], 0.0).then_inc(zeros_ready, 1)

            n_carry = [2]

            def add_carries(last_step):
                for d in range(D):
                    step = V.scalar_tensor_tensor(out=A_jd[:, :, d], in0=infirst[:], scalar=carry[:, d:d + 1],
                                                  in1=B_dj[:, d, :], op0=ALU.mult, op1=ALU.add)
                    if d < D - 1:
                        step.then_inc(carries_added, 1)
                last_step(step)
                added[0] += D - 1
                dve.wait_ge(carries_added, added[0])

            added = [0]

            def carry_piece(cols):
                w = cols.stop - cols.start
                room = bufG[:, 28 * P:28 * P + D * w].rearrange("p (d j) -> p d j", d=D)
                link(V.tensor_tensor(room, infirst[:, cols].unsqueeze(1).to_broadcast([P, D, w]),
                                     carry[:, 0:D].unsqueeze(2).to_broadcast([P, D, w]), ALU.mult))
                link(V.tensor_tensor(turned(A_jd[:, cols]), B_dj[:, :, cols], room, ALU.add))

            def segment_sums(whole=True):
                V.tensor_tensor_scan(bufB[:], contf[:].rearrange("p d j -> p (d j)"), bufA[:], 0.0,
                                     ALU.mult, ALU.add).then_inc(tail_ready, 1)
                n_carry[0] += 1
                dve.wait_ge(carry_ready, n_carry[0])
                if whole:
                    add_carries(link)

            norms = [0]

            def layer_norm(y, tmp, signal=None, before=None, in_turn=False):
                n = PARTS * norms[0]
                norms[0] += 1

                def center(c):
                    cols = part(c)
                    if before is not None:
                        before(c)
                    yc = y[:, cols]
                    w = cols.stop - cols.start
                    link(V.tensor_reduce(lnv[:, cols], yc, AX.X, ALU.add))
                    link(V.tensor_scalar(lnv[:, cols], lnv[:, cols], 1.0 / D, None, ALU.mult))
                    V.tensor_tensor(yc, yc, lnv[:, cols].unsqueeze(2).to_broadcast([P, w, D]), ALU.subtract).then_inc(centered, 1)

                def variance(c):
                    cols = part(c)
                    dve.wait_ge(squared, n + c + 1)
                    V.tensor_reduce(lnw[:, cols], tmp[:, cols], AX.X, ALU.add).then_inc(var_ready, 1)

                def scale(c):
                    cols = part(c)
                    yc = y[:, cols]
                    dve.wait_ge(rstd_ready, n + c + 1)
                    ins = V.tensor_tensor(yc, yc, lnw[:, cols].unsqueeze(2).to_broadcast(
                        [P, cols.stop - cols.start, D]), ALU.mult)
                    ins.then_inc(scaled, 1)
                    if signal is not None:
                        dve.wait_ge(scaled, n + c + 1)
                        dve.sem_inc(signal, 1)

                if in_turn:
                    for c in range(PARTS):
                        center(c)
                        variance(c)
                        scale(c)
                    dve.wait_ge(scaled, n + PARTS)
                    return
                center(0)
                for c in range(1, PARTS):
                    center(c)
                    variance(c - 1)
                    if c > 1:
                        scale(c - 2)
                variance(PARTS - 1)
                scale(PARTS - 2)
                scale(PARTS - 1)
                dve.wait_ge(scaled, n + PARTS)

            def gathered(n):
                for h in range(2):
                    dve.wait_ge(copied[h], 16 * (GROUPS // 2) * (n + 1))

            def leaves_only():
                link(V.tensor_scalar(leaf[:], act[:], -1.0, 1.0, ALU.mult, ALU.add))
                link(V.tensor_tensor(xs[:], xs[:], bj(leaf[:]), ALU.mult))

            short_done = [0]
            general_done = [4 * (APPNP_STEPS - 1)]

            def from_table(l, steps, then):
                with dve.If(path < K2 + 1):
                    def short_step(ins):
                        short_done[0] += 1
                        ins.then_inc(s_vdone, 1)
                        dve.wait_ge(s_vdone, short_done[0])

                    for c in range(PARTS):
                        cols = part(c)
                        dve.wait_ge(rows_loaded[c], 16 * (l + 1))
                        short_step(V.tensor_tensor(xs[:, cols, :], xs[:, cols, :], G_jd[:, cols, :], ALU.add))
                        then(cols, cols.stop - cols.start, short_step)
                with dve.Else():
                    base = general_done[0]
                    rows = bufB[:, 0:U * D].rearrange("p (j d) -> p j d", d=D)
                    with dve.Fori(0, GROUPS // 2) as i:
                        for h in range(2):
                            group = 2 * i + h
                            cols = bass.ds(group * U, U)
                            count = [0]

                            def step(ins):
                                count[0] += 1
                                ins.then_inc(g_vdone, 1)
                                dve.wait_ge(g_vdone, base + group * (steps + 2) + count[0])

                            dve.wait_ge(g_copied[h], 16 * ((APPNP_STEPS - 1 + l) * (GROUPS // 2) + 1) + 16 * i)
                            dve.sem_inc(dve_tick, 1)
                            step(V.tensor_tensor(rows, G_jd[:, cols, :],
                                                 act[:, cols].unsqueeze(2).to_broadcast([P, U, D]), ALU.mult))
                            step(V.tensor_tensor(xs[:, cols, :], xs[:, cols, :], rows, ALU.add))
                            then(cols, U, step)
                            assert count[0] == steps + 2
                    general_done[0] += (steps + 2) * GROUPS

            gathered(0)
            link(V.tensor_scalar(act[:], G_rec[:, :, D + 1], 0.0, None, ALU.is_gt))
            link(V.tensor_tensor(ta[:], G_rec[:, :, D], slotdeg[:, :, 0], ALU.subtract))
            link(V.tensor_tensor(ta[:], ta[:], act[:], ALU.mult))
            link(V.tensor_tensor(ta[:], ta[:], slotdeg[:, :, 0], ALU.add))
            link(V.tensor_copy(src_slot_i[:], ta[:]))
            link(V.tensor_copy(norm_d[:], deg[:]))
            link(V.tensor_scalar(dinv_d[:], deg[:], 1.0, None, ALU.add))
            link(V.tensor_scalar(scale_s[:], G_rec[:, :, D + 1], 1.0, None, ALU.max))
            link(V.tensor_scalar(dinv_s[:], G_rec[:, :, D + 1], 1.0, None, ALU.add))
            dve.sem_inc(act_in, 1)

            row0 = slotdeg[:, 0:1, 0]
            link(V.tensor_scalar(tb[:], slotdeg[:, :, 0], row0, -1.0, ALU.subtract, ALU.mult))
            link(V.tensor_scalar(tb[:], tb[:], float(T), float(1 << SLOT_BITS), ALU.add, ALU.mult))
            link(V.tensor_tensor(tb[:], tb[:], ta[:], ALU.add))
            link(V.tensor_tensor(tb[:], tb[:], act[:], ALU.mult))
            V.tensor_tensor_scan(ta[:], cont[:], act[:], 0.0, ALU.mult, ALU.add).then_inc(tail_ready, 1)
            dve.wait_ge(carry_ready, 3)
            link(V.scalar_tensor_tensor(out=lnv[:], in0=infirst[:], scalar=carry[:, 0:1], in1=ta[:],
                                        op0=ALU.mult, op1=ALU.add))
            dve.sem_inc(feeders_ready, 1)

            def greatest(dest, keys, count):
                for k in range(0, count, 8):
                    link(V.max(dest[:, k:k + 8], keys))
                    if k + 8 < count:
                        link(V.match_replace(keys, dest[:, k:k + 8], keys, 0.0))

            greatest(cand_key, tb[:], K1)
            link(V.tensor_copy(cand_i[:], cand_key[:]))
            V.tensor_scalar(cand_slot_i[:], cand_i[:], (1 << SLOT_BITS) - 1, None, ALU.bitwise_and).then_inc(cand_ready, 1)
            link(V.tensor_scalar(cand_i[:], cand_i[:], SLOT_BITS, None, ALU.logical_shift_right))
            link(V.tensor_copy(cand_col[:], cand_i[:]))
            link(V.tensor_reduce(fits[:, 0:1], act[:], AX.X, ALU.add))
            link(V.tensor_scalar(fits[:, 0:1], fits[:, 0:1], float(K1 - K2), None, ALU.subtract))
            own, nobody, valid = (lnw[:, k * K1:(k + 1) * K1] for k in range(3))
            link(V.tensor_copy(nobody, cand_own_i[:]))
            link(V.tensor_scalar(valid, cand_col[:], 0.0, None, ALU.is_gt))
            link(V.tensor_scalar(own, cand_col[:], -1.0, float(T), ALU.mult, ALU.add))
            link(V.tensor_scalar(own, own, row0, None, ALU.add))
            link(V.tensor_tensor(own, own, nobody, ALU.subtract))
            link(V.tensor_tensor(own, own, valid, ALU.mult))
            link(V.tensor_tensor(own, own, nobody, ALU.add))
            V.tensor_copy(cand_own_i[:], own).then_inc(cand_own_ready, 1)
            dve.wait_ge(zeroed, 48)
            link(V.tensor_copy(xs[:], G_rec[:, :, 0:D]))
            dve.wait_ge(act_out, 1)
            link(V.tensor_tensor(tb[:], scale_s[:], act[:], ALU.mult))
            link(V.tensor_tensor(scale_s[:], tb[:], tb[:], ALU.mult))
            link(V.tensor_scalar(scale_s[:], scale_s[:], 0.9, None, ALU.mult))
            link(V.tensor_copy(erec[:, :, 0], scale_s[:]))
            link(V.tensor_copy(erec[:, :, 1], dstf[:]))
            link(V.tensor_copy(erec[:, :, 2], src_i[:]))
            link(V.tensor_copy(erec[:, :, 3], src_slot_i[:]))
            dve.sem_inc(erec_ready, 1)

            dense_stored(dve)
            link(V.tensor_tensor(N_dj, turned(xs[:]), bd(tb[:]), ALU.mult))
            link(V.tensor_copy(bufA[:], bufN[:]))
            n_carry[0] = 3
            segment_sums()
            dve.sem_inc(table_ready, 1)

            dve.wait_ge(cand_landed, 16 * K1)
            link(V.scalar_tensor_tensor(out=cand_col[:], in0=cand_feeders[:], scalar=0.0, in1=cand_col[:],
                                        op0=ALU.is_gt, op1=ALU.mult))
            link(V.tensor_scalar(cand_key[:], cand_col[:], 0.0, None, ALU.is_gt))
            link(V.tensor_reduce(fits[:, 1:2], cand_key[:], AX.X, ALU.add))
            V.tensor_tensor(fits[:, 0:1], fits[:, 0:1], fits[:, 1:2], ALU.max).then_inc(tail_ready, 1)
            dve.wait_ge(carry_ready, 5)
            n_carry[0] = 5
            link(V.tensor_reduce(colmax[0:1, :], carry[0:1, 0:P], AX.X, ALU.max))
            V.tensor_copy(path_i[:], colmax[0:1, :]).then_inc(path_known, 1)
            dve.wait_ge(path_known, 1)
            path = dve.value_load(path_i[0:1, 0:1], min_val=0, max_val=T + 1)

            with dve.If(path < K2 + 1):
                s_done = [0]

                def note(ins):
                    s_done[0] += 1
                    ins.then_inc(s_vdone, 1)
                    dve.wait_ge(s_vdone, s_done[0])

                def sd(col):
                    return col.unsqueeze(1).to_broadcast([P, D, K2])

                def sj(col):
                    return col.unsqueeze(2).to_broadcast([P, K2, D])

                for k in range(0, K2, 8):
                    note(V.max(e_key[:, k:k + 8], cand_col[:]))
                    if k + 8 < K2:
                        note(V.match_replace(cand_col[:], e_key[:, k:k + 8], cand_col[:], 0.0))
                note(V.tensor_scalar(e_valid[:], e_key[:], 0.0, None, ALU.is_gt))
                note(V.tensor_scalar(e_own[:], e_key[:], -1.0, float(T), ALU.mult, ALU.add))
                note(V.tensor_tensor(e_own[:], e_own[:], e_valid[:], ALU.mult))
                note(V.tensor_scalar(e_own[:], e_own[:], row0, None, ALU.add))
                V.tensor_copy(e_own_i[:], e_own[:]).then_inc(s_own_ready, 1)
                note(V.tensor_copy(e_slot[:], e_slot_i[:]))
                note(V.tensor_scalar(e_t[:], e_slot[:], float(E), None, ALU.add))
                note(V.tensor_tensor(e_own[:], e_own[:], e_t[:], ALU.subtract))
                note(V.tensor_tensor(e_own[:], e_own[:], e_valid[:], ALU.mult))
                note(V.tensor_tensor(e_own[:], e_own[:], e_t[:], ALU.add))
                note(V.tensor_copy(e_msg_i[:], e_own[:]))
                note(V.memset(e_cont[:, 0:1], 0.0))
                dve.wait_ge(s_rec_landed, 16 * K2)
                note(V.tensor_copy(e_src_i[:], e_rec[:, :, 2]))
                V.tensor_copy(e_srcslot_i[:], e_rec[:, :, 3]).then_inc(s_src_ready, 1)
                note(V.tensor_tensor(e_fact[:], e_rec[:, :, 0], e_valid[:], ALU.mult))
                note(V.scalar_tensor_tensor(out=e_dst[:], in0=e_rec[:, :, 1], scalar=1.0, in1=e_valid[:],
                                            op0=ALU.add, op1=ALU.mult))
                note(V.tensor_reduce(e_mdst[:, 0:1], e_dst[:], AX.X, ALU.max))
                note(V.tensor_scalar(e_mdst[:, 1:2], e_mdst[:, 0:1], 0.0, None, ALU.is_gt))
                note(V.tensor_scalar(e_t[:, 0:1], e_mdst[:, 1:2], 1.0, row0, ALU.subtract, ALU.mult))
                note(V.tensor_tensor(e_mdst[:, 0:1], e_mdst[:, 0:1], e_t[:, 0:1], ALU.add))
                note(V.tensor_scalar(e_t[:], e_valid[:], -1.0, 1.0, ALU.mult, ALU.add))
                note(V.scalar_tensor_tensor(out=e_dst[:], in0=e_t[:], scalar=e_mdst[:, 0:1], in1=e_dst[:],
                                            op0=ALU.mult, op1=ALU.add))
                note(V.tensor_scalar(e_dst[:], e_dst[:], 1.0, None, ALU.subtract))
                V.tensor_scalar(diag[:], id_sb[:], e_dst[:, 0:1], None, ALU.mult).then_inc(s_tail, 1)
                note(V.tensor_tensor(e_cont[:, 1:K2], e_dst[:, 1:K2], e_dst[:, 0:K2 - 1], ALU.is_equal))
                note(V.tensor_scalar(e_infirst[:], e_dst[:], e_dst[:, 0:1], None, ALU.is_equal))
                note(V.tensor_copy(short_dj(cont2), sd(e_cont[:])))
                dve.wait_ge(s_carry, 1)
                note(V.scalar_tensor_tensor(out=link_e[:], in0=carry[:, 0:P], scalar=e_dst[:, K2 - 1:K2], in1=up_sb[:],
                                            op0=ALU.is_equal, op1=ALU.mult))
                note(V.tensor_scalar(e_last[:, 0:K2 - 1], e_cont[:, 1:K2], -1.0, 1.0, ALU.mult, ALU.add))
                note(V.tensor_reduce(e_last[:, K2 - 1:K2], link_e[:], AX.X, ALU.max))
                note(V.tensor_scalar(e_last[:, K2 - 1:K2], e_last[:, K2 - 1:K2], -1.0, 1.0, ALU.mult, ALU.add))
                note(V.tensor_scalar(e_last[:], e_last[:], e_mdst[:, 1:2], None, ALU.mult))
                note(V.tensor_scalar(e_q[:], e_slot[:], 1.0, None, ALU.add))
                note(V.tensor_scalar(e_t[:], e_slot[:], float(NR), None, ALU.add))
                note(V.tensor_tensor(e_dst[:], e_dst[:], e_t[:], ALU.subtract))
                note(V.tensor_tensor(e_dst[:], e_dst[:], e_last[:], ALU.mult))
                note(V.tensor_tensor(e_dst[:], e_dst[:], e_t[:], ALU.add))
                note(V.tensor_copy(e_put_i[:], e_dst[:]))
                dve.sem_inc(s_put_ready, 1)

                def s_sums(mark, carry_count):
                    V.tensor_tensor_scan(scan2, cont2, msg2, 0.0, ALU.mult, ALU.add).then_inc(s_tail, 1)
                    dve.wait_ge(s_carry, carry_count)
                    mark(V.tensor_tensor(short_dj(tmp2), sd(e_infirst[:]),
                                         carry[:, 0:D].unsqueeze(2).to_broadcast([P, D, K2]), ALU.mult))
                    mark(V.tensor_tensor(short_jd(sum2).rearrange("p j d -> p d j"), short_dj(scan2),
                                         short_dj(tmp2), ALU.add))
                    dve.sem_inc(s_table_ready, 1)

                dve.wait_ge(s_r_landed, 16 * K2)
                note(V.tensor_tensor(short_dj(msg2), turned(short_jd(r2)), sd(e_fact[:]), ALU.mult))
                note(V.tensor_scalar(short_dj(base2), short_dj(msg2), 0.1, None, ALU.mult))
                s_sums(note, 2)
                dve.wait_ge(s_q_landed, 16 * K2)
                note(V.scalar_tensor_tensor(out=e_fact[:], in0=e_t[:], scalar=0.0, in1=e_fact[:],
                                            op0=ALU.is_gt, op1=ALU.mult))
                note(V.tensor_scalar(e_t[:], e_t[:], 1.0, 0.0, ALU.subtract, ALU.max))
                note(V.tensor_copy(e_q_i[:], e_t[:]))
                dve.sem_inc(s_q_ready, 1)
                s_base, s_per = s_done[0], 4
                with dve.Fori(0, APPNP_STEPS - 3) as it:
                    marks = [0]

                    def mark(ins):
                        marks[0] += 1
                        ins.then_inc(s_vdone, 1)
                        dve.wait_ge(s_vdone, s_base + it * s_per + marks[0])

                    dve.wait_ge(s_landed, it * 16 * K2 + 16 * K2)
                    mark(V.tensor_tensor(short_dj(msg2), turned(short_jd(g2)), sd(e_fact[:]), ALU.mult))
                    mark(V.tensor_tensor(msg2, msg2, base2, ALU.add))
                    s_sums(mark, it + 3)
                    assert marks[0] == s_per
                s_done[0] += s_per * (APPNP_STEPS - 3)
                dve.wait_ge(s_landed, 16 * K2 * (APPNP_STEPS - 2))
                note(V.tensor_tensor(short_jd(msg2), short_jd(g2), sj(e_fact[:]), ALU.mult))
                note(V.tensor_tensor(short_jd(msg2), short_jd(msg2), short_dj(base2).rearrange("p d j -> p j d"), ALU.add))
                dve.sem_inc(s_msg_ready, 1)
                for c in range(PARTS):
                    cols = part(c)
                    dve.wait_ge(s_msg_loaded[c], 16)
                    note(V.scalar_tensor_tensor(out=A_dj[:, :, cols], in0=N_dj[:, :, cols], scalar=0.1,
                                                in1=turned(G_jd[:, cols, :]), op0=ALU.mult, op1=ALU.add))
                V.tensor_tensor_scan(bufB[:], contf[:].rearrange("p d j -> p (d j)"), bufA[:], 0.0,
                                     ALU.mult, ALU.add).then_inc(s_tail, 1)
                dve.wait_ge(s_carry, APPNP_STEPS)
                note(V.tensor_tensor(G_dj, bd(infirst[:]), carry[:, 0:D].unsqueeze(2).to_broadcast([P, D, T]), ALU.mult))
                note(V.tensor_tensor(A_jd.rearrange("p j d -> p d j"), B_dj, G_dj, ALU.add))
                short_done[0] = s_done[0]
            with dve.Else():
                g_per, H = 4, GROUPS // 2
                dve.sem_inc(g_table_ready, 1)
                with dve.Fori(0, APPNP_STEPS - 1) as it:
                    def mark(k):
                        dve.wait_ge(g_vdone, it * g_per + k)

                    for h in range(2):
                        dve.wait_ge(g_copied[h], it * 16 * H + 16 * H)
                    V.tensor_tensor(A_dj, turned(G_jd), bd(scale_s[:]), ALU.mult).then_inc(g_vdone, 1)
                    mark(1)
                    V.scalar_tensor_tensor(out=bufA[:], in0=bufN[:], scalar=0.1, in1=bufA[:],
                                           op0=ALU.mult, op1=ALU.add).then_inc(g_vdone, 1)
                    mark(2)
                    V.tensor_tensor_scan(bufB[:], contf[:].rearrange("p d j -> p (d j)"), bufA[:], 0.0,
                                         ALU.mult, ALU.add).then_inc(g_tail, 1)
                    dve.wait_ge(g_carry, it + 1)
                    V.tensor_tensor(G_dj, bd(infirst[:]), carry[:, 0:D].unsqueeze(2).to_broadcast([P, D, T]),
                                    ALU.mult).then_inc(g_vdone, 1)
                    mark(3)
                    V.tensor_tensor(A_jd.rearrange("p j d -> p d j"), B_dj, G_dj, ALU.add).then_inc(g_vdone, 1)
                    mark(4)
                    dve.sem_inc(g_table_ready, 1)
            link(V.tensor_scalar(ta[:], norm_d[:], 0.9, None, ALU.mult))
            dve.wait_ge(xd_landed, 16 * T)
            link(V.tensor_tensor(A_jd, A_jd, bj(ta[:]), ALU.mult))
            link(V.scalar_tensor_tensor(out=flat(xd[:]), in0=flat(xd[:]), scalar=1.1, in1=bufA[:],
                                        op0=ALU.mult, op1=ALU.add))
            layer_norm(xd[:], A_jd, parts_ready)

            def carried():
                n_carry[0] += 1
                dve.wait_ge(carry_ready, n_carry[0])

            link(V.tensor_scalar(flat(xs[:]), flat(xs[:]), 1.1, None, ALU.mult))
            layer_norm(xs[:], A_jd)
            leaves_only()
            link(V.tensor_copy(bufN[:], flat(xs[:])))
            layer_norm(N_jd, A_jd)
            link(V.tensor_tensor(A_jd, xd[:], attn_sb[:, 1, :].unsqueeze(1).to_broadcast([P, T, D]), ALU.mult))
            link(V.tensor_reduce(td[:], A_jd, AX.X, ALU.add))

            def source_scores(cols, n, step):
                rows = bufB[:, U * D:(U + n) * D].rearrange("p (j d) -> p j d", d=D)
                step(V.tensor_tensor(rows, xs[:, cols, :], attn_sb[:, 0, :].unsqueeze(1).to_broadcast([P, n, D]), ALU.mult))
                step(V.tensor_reduce(tb[:, cols], rows, AX.X, ALU.add))

            from_table(0, 2, source_scores)
            link(V.tensor_scalar(ta[:], cont[:], -1.0, BIG, ALU.add, ALU.mult))
            link(V.tensor_tensor_scan(tc[:], ta[:], tb[:], -BIG, ALU.add, ALU.max))
            V.tensor_scalar(diag[:], id_sb[:], tc[:, T - 1:T], None, ALU.mult).then_inc(tail_ready, 1)
            carried()
            link(V.tensor_tensor(diag[:], link_b[:], carry[:, 0:P], ALU.mult))
            link(V.tensor_tensor(diag[:], diag[:], nolink[:], ALU.add))
            link(V.tensor_reduce(colmax[:], diag[:], AX.X, ALU.max))
            link(V.tensor_scalar(ta[:], infirst[:], -1.0, BIG, ALU.add, ALU.mult))
            link(V.scalar_tensor_tensor(out=tc[:], in0=ta[:], scalar=colmax[:, 0:1], in1=tc[:],
                                        op0=ALU.add, op1=ALU.max))
            for r, t in enumerate((tc, td)):
                link(V.tensor_tensor(both[:, r, :], t[:], last[:], ALU.mult))
            for r in range(2):
                link(V.tensor_tensor(ta[:], both[:, r, :], infirst[:], ALU.mult))
                link(V.tensor_reduce(first2[:, r:r + 1], ta[:], AX.X, ALU.add))
            dve.sem_inc(tail_ready, 1)
            carried()
            link(V.tensor_copy(init2[:], carry[:, 0:2]))
            for r, t in enumerate((tc, td)):
                link(V.tensor_tensor_scan(t[:, ::-1], contn[:, ::-1], both[:, r, ::-1], init2[:, r:r + 1],
                                          ALU.mult, ALU.add))
            for t in (tb, tc):
                link(V.tensor_tensor(t[:], t[:], td[:], ALU.add))
                link(V.scalar_tensor_tensor(out=t[:], in0=t[:], scalar=0.01, in1=t[:], op0=ALU.mult, op1=ALU.max))
            V.tensor_tensor(tb[:], tb[:], tc[:], ALU.subtract).then_inc(act_in, 1)
            dve.wait_ge(act_out, 2)
            V.tensor_tensor_scan(ta[:], cont[:], tb[:], 0.0, ALU.mult, ALU.add).then_inc(tail_ready, 1)
            carried()
            link(V.scalar_tensor_tensor(out=ta[:], in0=infirst[:], scalar=carry[:, 0:1], in1=ta[:],
                                        op0=ALU.mult, op1=ALU.add))
            link(V.tensor_scalar(ta[:], ta[:], 1.0 / BIG, None, ALU.max))
            link(V.reciprocal(ta[:], ta[:]))
            link(V.tensor_tensor(A_dj, turned(xs[:]), bd(tb[:]), ALU.mult))
            segment_sums()
            link(V.tensor_tensor(A_jd, A_jd, bj(ta[:]), ALU.mult))
            link(V.tensor_tensor(xd[:], xd[:], A_jd, ALU.add))
            layer_norm(xd[:], A_jd, parts_ready)

            rx, ry, rz = (relv[:, :, i] for i in range(3))
            link(V.tensor_tensor(ta[:], rx, rx, ALU.mult))
            link(V.tensor_tensor(tb[:], ry, ry, ALU.mult))
            link(V.tensor_tensor(ta[:], ta[:], tb[:], ALU.add))
            link(V.tensor_tensor(tb[:], rz, rz, ALU.mult))
            V.tensor_tensor(ta[:], ta[:], tb[:], ALU.add).then_inc(act_in, 1)
            dve.wait_ge(act_out, 3)
            link(V.tensor_tensor(relv[:], relv[:], ta[:].unsqueeze(2).to_broadcast([P, T, 3]), ALU.mult))
            for s, r in enumerate((ry, rz, rx)):
                link(V.tensor_scalar(sph[:, :, s], r, c1, None, ALU.mult))
            for s, a, b in ((3, rx, ry), (4, ry, rz), (6, rx, rz)):
                link(V.scalar_tensor_tensor(out=sph[:, :, s], in0=a, scalar=c2a, in1=b, op0=ALU.mult, op1=ALU.mult))
            link(V.tensor_tensor(tb[:], rz, rz, ALU.mult))
            link(V.tensor_scalar(sph[:, :, 5], tb[:], 3 * c2b, -c2b, ALU.mult, ALU.add))
            link(V.scalar_tensor_tensor(out=tb[:], in0=rx, scalar=c2c, in1=rx, op0=ALU.mult, op1=ALU.mult))
            link(V.scalar_tensor_tensor(out=tc[:], in0=ry, scalar=c2c, in1=ry, op0=ALU.mult, op1=ALU.mult))
            link(V.tensor_tensor(sph[:, :, 7], tb[:], tc[:], ALU.subtract))
            for k in (1, 2):
                w = wigner_3j(1, k, 1)
                for o in range(3):
                    for i in range(3):
                        terms = [(norm[1] * w[o, f, i], sph[:, :, (0 if k == 1 else 3) + f])
                                 for f in range(2 * k + 1) if abs(w[o, f, i]) > 1e-9]
                        m = mats[:, :, k - 1, o, i]
                        if not terms:
                            link(V.memset(m, 0.0))
                        for n, (c, y) in enumerate(terms):
                            link(V.tensor_scalar(m, y, c, None, ALU.mult) if n == 0 else
                                 V.scalar_tensor_tensor(out=m, in0=y, scalar=c, in1=m, op0=ALU.mult, op1=ALU.add))
            link(V.tensor_copy(flat(xs[:]), bufN[:]))
            for t in hid:
                link(V.memset(t[HID:HID + 1, :], 1.0))
            dve.sem_inc(hid_free, 2)
            dve.sem_inc(conv_open, 1)
            def rooms(buf, at, *shapes):
                for shape in shapes:
                    size = int(np.prod(shape))
                    assert at + size <= buf.shape[1]
                    yield buf[:, at:at + size]
                    at += size

            q1, q0, q2, gk, gt, vec, prod = rooms(
                bufN, 4 * C7 * P, (C7, MULT, 3), (C7, 3, MULT), (C7, MULT, 3), (C7, 3, MULT, 3), (6, C7, MULT, 3),
                (U, 3, MULT), (U, MULT, 3))
            prod1 = list(rooms(bufB, (8 + n_mk) * T, *[(MULT, 3, 3 * MULT)] * 2)) + list(
                rooms(relv[:].rearrange("p j c -> p (j c)"), 0, (MULT, 3, 3 * MULT)))
            prod0 = list(rooms(bufG, T * D, *[(3, MULT, MULT)] * 2)) + list(rooms(per_edge4, 0, (3, MULT, MULT)))
            gk = gk.rearrange("p (c o v k) -> p c o v k", o=3, v=MULT, k=3)
            gk_flat = gk.rearrange("p c o v k -> p c o (v k)")
            gt_flat = gt
            gt = gt.rearrange("p (s c v i) -> p s c v i", c=C7, v=MULT, i=3)
            prod1 = [t.rearrange("p (u o w) -> p u o w", u=MULT, o=3) for t in prod1]
            prod0 = [t.rearrange("p (b u v) -> p b u v", b=3, u=MULT) for t in prod0]
            q1, q2 = (t.rearrange("p (c u o) -> p c u o", u=MULT, o=3) for t in (q1, q2))
            q0 = q0.rearrange("p (c b u) -> p c b u", b=3, u=MULT)
            vec = vec.rearrange("p (j b v) -> p j b v", b=3, v=MULT)
            prod = prod.rearrange("p (j v i) -> p j v i", v=MULT, i=3)
            def products(col, gk_r, vec_of, note, settle, inputs_read=None):
                multiplied, summed = {}, {}

                def multiply(c):
                    if c >= 3:
                        settle(summed[c - 3])
                    dve.wait_ge(r_ready, col + c + 1)
                    rr = ps[:, c % 5, :]
                    note(V.tensor_tensor(
                        prod1[c % 3],
                        rr[:, 3 * MULT * MULT:R_DIM].rearrange("p (u w) -> p u w", u=MULT).unsqueeze(2).to_broadcast(
                            [P, MULT, 3, 3 * MULT]),
                        gk_r[:, c].unsqueeze(1).to_broadcast([P, MULT, 3, 3 * MULT]), ALU.mult))
                    multiplied[c] = note(V.tensor_tensor(
                        prod0[c % 3], rr[:, 0:3 * MULT * MULT].rearrange("p (b u v) -> p b u v", b=3, u=MULT),
                        vec_of(c).unsqueeze(2).to_broadcast([P, 3, MULT, MULT]), ALU.mult))

                multiply(0)
                for c in range(C7):
                    if c + 1 < C7:
                        multiply(c + 1)
                    settle(multiplied[c])
                    dve.sem_inc(r_used, 1)
                    if c == C7 - 1 and inputs_read is not None:
                        dve.sem_inc(inputs_read, 1)
                    note(V.tensor_reduce(q1[:, c], prod1[c % 3], AX.X, ALU.add))
                    summed[c] = note(V.tensor_reduce(q0[:, c], prod0[c % 3], AX.X, ALU.add))
                settle()
                out_c = A_dj[:, :, bass.ds(col, C7)]
                note(V.tensor_tensor(out_c[:, 0:MULT, :].rearrange("p u c -> p c u"), q0[:, :, 0, :], q0[:, :, 1, :], ALU.add))
                note(V.tensor_tensor(q2, q0[:, :, 2, :].unsqueeze(3).to_broadcast([P, C7, MULT, 3]),
                                     sph[:, bass.ds(col, C7), 0:3].unsqueeze(2).to_broadcast([P, C7, MULT, 3]), ALU.mult))
                settle()
                note(V.tensor_tensor(out_c[:, MULT:D, :].rearrange("p w c -> p c w"),
                                     q1.rearrange("p c u o -> p c (u o)"), q2.rearrange("p c u o -> p c (u o)"), ALU.add))
                settle()

            dve.sem_inc(r_used, C7)
            dve.sem_inc(p_used, 2)
            PER_GROUP = 7
            from_g = gt_flat[:, 0:U * D].rearrange("p (j d) -> p j d", d=D)
            PER = 7 + 6 + 4 * C7 + 3
            assert U == 2 * C7
            base = done[0]
            with dve.Fori(0, DVE_GROUPS // 2) as i:
                for h in range(2):
                    group = 2 * i + h
                    first_col = group * U
                    before = base + group * (PER_GROUP + 2 * PER)
                    cnt = [0]

                    def note(ins):
                        cnt[0] += 1
                        ins.then_inc(vdone, 1)
                        return cnt[0]

                    def settle(n=None):
                        dve.wait_ge(vdone, before + (cnt[0] if n is None else n))

                    dve.wait_ge(copied[h], 16 * (GROUPS // 2 + 1) + 16 * i)
                    dve.sem_inc(dve_tick, 1)
                    xg = xs[:, bass.ds(first_col, U), :]
                    note(V.tensor_tensor(from_g, G_jd[:, bass.ds(first_col, U), :],
                                         act[:, bass.ds(first_col, U)].unsqueeze(2).to_broadcast([P, U, D]), ALU.mult))
                    settle()
                    note(V.tensor_tensor(xg, xg, from_g, ALU.add))
                    settle()
                    note(V.tensor_scalar(vec[:, :, 0, :], xg[:, :, 0:MULT], norm[0] * w000 * y0, None, ALU.mult))
                    note(V.tensor_scalar(vec[:, :, 2, :], xg[:, :, 0:MULT], norm[1] * w110, None, ALU.mult))
                    note(V.tensor_tensor(prod, xg[:, :, MULT:D].rearrange("p j (v i) -> p j v i", i=3),
                                         sph[:, bass.ds(first_col, U), 0:3].unsqueeze(2).to_broadcast([P, U, MULT, 3]), ALU.mult))
                    settle()
                    note(V.tensor_reduce(vec[:, :, 1, :], prod, AX.X, ALU.add))
                    settle()
                    note(V.tensor_scalar(vec[:, :, 1, :], vec[:, :, 1, :], norm[0] * w011, None, ALU.mult))
                    assert cnt[0] == PER_GROUP
                    for s in range(2):
                        col = first_col + s * C7
                        x1 = xs[:, bass.ds(col, C7), MULT:D].rearrange("p j (v i) -> p j v i", i=3)
                        mk = mats[:, bass.ds(col, C7)]
                        settle()
                        note(V.tensor_scalar(gk[:, :, :, :, 0].rearrange("p c o v -> p c v o"), x1,
                                             norm[1] * w101 * y0, None, ALU.mult))
                        for k in range(2):
                            for o in range(3):
                                note(V.tensor_tensor(gt[:, 3 * k + o], x1, mk[:, :, k, o, :].unsqueeze(2).to_broadcast(
                                    [P, C7, MULT, 3]), ALU.mult))
                        settle()
                        for k in range(2):
                            for o in range(3):
                                note(V.tensor_reduce(gk[:, :, o, :, 1 + k], gt[:, 3 * k + o], AX.X, ALU.add))
                        settle()
                        products(col, gk_flat, lambda c: vec[:, s * C7 + c, :, :], note, settle)
                        assert cnt[0] == PER_GROUP + (s + 1) * PER, cnt[0]
                    dve.sem_inc(conv_groups, 1)
            base_p = base + DVE_GROUPS * (PER_GROUP + 2 * PER)
            PER_P = 4 * C7 + 3
            with dve.Fori(0, (GROUPS - DVE_GROUPS) // 2) as i:
                for h in range(2):
                    for s in range(2):
                        r = 4 * i + 2 * h + s
                        cnt = [0]

                        def note(ins):
                            cnt[0] += 1
                            ins.then_inc(vdone, 1)
                            return cnt[0]

                        def settle(n=None):
                            dve.wait_ge(vdone, base_p + r * PER_P + (cnt[0] if n is None else n))

                        dve.wait_ge(p_ready, r + 1)
                        products(r * C7 + DVE_GROUPS * U, gk_p[s].rearrange("p c o v k -> p c o (v k)"),
                                 lambda c: vec_p[h][:, s * C7 + c, :, :], note, settle, p_used)
                        assert cnt[0] == PER_P, cnt[0]
            done[0] += (PER_GROUP + 2 * PER) * DVE_GROUPS + PER_P * 2 * (GROUPS - DVE_GROUPS)
            segment_sums()
            link(V.tensor_tensor(xd[:], xd[:], A_jd, ALU.add))
            layer_norm(xd[:], A_jd, parts_ready)

            layer_norm(xs[:], A_jd)
            leaves_only()
            link(V.tensor_tensor(N_jd, xd[:], bj(dinv_d[:]), ALU.mult))

            def weighted(cols, n, step):
                step(V.tensor_tensor(A_dj[:, :, cols], turned(xs[:, cols, :]),
                                     dinv_s[:, cols].unsqueeze(1).to_broadcast([P, D, n]), ALU.mult))

            from_table(1, 1, weighted)
            segment_sums()
            dve.sem_inc(m_x, 1)
            for c in range(0, T, 28):
                cols = slice(c, c + 28)
                link(V.tensor_tensor(A_jd[:, cols], A_jd[:, cols], N_jd[:, cols], ALU.add))
                V.tensor_tensor(A_jd[:, cols], A_jd[:, cols], dinv_d[:, cols].unsqueeze(2).to_broadcast([P, 28, D]),
                                ALU.mult).then_inc(m_cols, 1)
            dve.wait_ge(m_cols, T // 28)
            for m, dest in enumerate((bufN[:], flat(xs[:]))):
                with dve.Fori(0, T // 28) as i:
                    k = i + m * (T // 28)
                    dve.wait_ge(m_h, k + 1)
                    V.tensor_scalar(bufB[:, 14 * P:21 * P].rearrange("p (a b) -> p a b", a=2), ps[:, 4:6, 0:448],
                                    gb1_sb[:, 0:1], 0.0, ALU.add, ALU.max).then_inc(m_b, 1)
                    dve.wait_ge(m_o, k + 1)
                    dve.sem_inc(dve_tick, 1)
                    V.tensor_copy(dest[:, bass.ds(i * 28 * D, 28 * D)],
                                  ps[:, 6:8, :].rearrange("p a b -> p (a b)")[:, 0:28 * D]).then_inc(m_x, 1)
            dve.wait_ge(m_x, 1 + 2 * (T // 28))
            leaves_only()
            dve.wait_ge(table_stored, 16 * (1 + PARTS * 4))
            link(V.tensor_tensor(N_jd, N_jd, bj(dinv_d[:]), ALU.mult))
            link(V.tensor_tensor(N_jd, N_jd, bj(dinv_d[:]), ALU.mult))
            link(V.tensor_tensor(N_jd, N_jd, gb2_row[:].unsqueeze(1).to_broadcast([P, T, D]), ALU.add))
            link(V.tensor_tensor(xd[:], xd[:], N_jd, ALU.add))
            from_table(2, 1, weighted)
            segment_sums(whole=False)

            def result(c):
                cols = part(c)
                w = cols.stop - cols.start
                a, x_c = A_jd[:, cols], xd[:, cols]
                carry_piece(cols)
                link(V.tensor_tensor(a, a, dinv_d[:, cols].unsqueeze(2).to_broadcast([P, w, D]), ALU.mult))
                link(V.tensor_tensor(x_c, x_c, a, ALU.add))

            layer_norm(xd[:], A_jd, state_ready, before=result, in_turn=True)


def kernel(x, src, dst, edge_attr_3, edge_weight, L1_gnn_attn_w, L2_gnn_w1, L2_gnn_b1, L2_gnn_w2, L2_gnn_b2,
           L3_gnn_W1, L3_gnn_b1, L3_gnn_W2, L3_gnn_b2):
    import concourse.bacc as bacc
    from concourse.bass_utils import run_bass_kernel_spmd

    x, src, dst, rel, weight = (np.asarray(a) for a in (x, src, dst, edge_attr_3, edge_weight))
    n, e = x.shape[0], src.shape[0]
    T, E, NR = sizes(n, e)
    assert n < NR

    def padded(a, rows, value):
        return np.concatenate([a, np.full((rows - a.shape[0],) + a.shape[1:], value, a.dtype)])

    ends = padded(padded(dst, E, n), E + 1, n + 1)
    arrays = {
        "x": padded(x, NR + 2 * P * NB, 0), "src": padded(src, E, 0),
        "dst": ends[:E], "dst_next": ends[1:], "dst_first": ends[:E:T],
        "rel": padded(rel, E, 1), "wt_cols": padded(padded(weight, E, 0).reshape(P, T).T, T + 2 * C7, 0),
        "attn_w": L1_gnn_attn_w, "w1": L2_gnn_w1, "b1": L2_gnn_b1, "w2": L2_gnn_w2, "b2": L2_gnn_b2,
        "gcn_w1": L3_gnn_W1, "gcn_b1": L3_gnn_b1, "gcn_w2": L3_gnn_W2, "gcn_b2": L3_gnn_b2,
        "ident": np.eye(P, dtype=np.float32),
        "upper": np.triu(np.ones((P, P), np.float32), 1),
    }
    arrays = {f"in_{k}": np.ascontiguousarray(v) for k, v in arrays.items()}
    nc = bacc.Bacc("TRN2", target_bir_lowering=False, num_devices=1)
    args = [nc.dram_tensor(k, v.shape, mybir.dt.from_np(v.dtype), kind="ExternalInput").ap()
            for k, v in arrays.items()]
    out = nc.dram_tensor("out", (NR + E, D), F32, kind="ExternalOutput").ap()
    gnn_kernel(nc, *args, out, e)
    return run_bass_kernel_spmd(nc, [arrays], core_ids=[0]).results[0]["out"][:n]
```
